# Optimizing a Trainium2 kernel written in Bass

```python
import numpy as np
import jax
import jax.numpy as jnp

def _softmax(x, axis=-1):
    return jax.nn.softmax(x, axis=axis)

def _gelu(x):
    return jax.nn.gelu(x, approximate=True)

def _silu(x):
    return jax.nn.silu(x)

def _sigmoid(x):
    return jax.nn.sigmoid(x)

def _layernorm(x, axis=-1, eps=1e-05):
    m = jnp.mean(x, axis=axis, keepdims=True)
    v = jnp.var(x, axis=axis, keepdims=True)
    return (x - m) / jnp.sqrt(v + eps)

def _scatter_add(tgt, idx, src, axis=0):
    return tgt.at[idx].add(src)

def _segment_sum(src, seg, n):
    return jax.ops.segment_sum(src, seg, n)
kernel_name = 'mk_xattn_ffn_d1_seqx_r4_39d8c2'

def setup_inputs(seed: int=0):
    np.random.seed(seed)
    _w = jnp.asarray

    def _rec_inputs():
        import jax
        import jax.numpy as jnp
        _rk = jax.random.key(seed)
        x = -0.0005207 + 1.001 * jax.random.normal(jax.random.fold_in(_rk, 1), (8, 512, 256), jnp.float32)
        _lenS = 512 - jax.random.randint(jax.random.fold_in(_rk, 7), (8,), 0, max(1, 512 // 4) + 1, jnp.int32)
        _lenS2 = 64 - jax.random.randint(jax.random.fold_in(_rk, 8), (8,), 0, max(1, 64 // 4) + 1, jnp.int32)
        _ctx_1024P = jax.random.normal(jax.random.fold_in(_rk, 11), (8, 16, 256), jnp.float32)
        _ctx_1024c = jax.random.dirichlet(jax.random.fold_in(_rk, 511), 0.3 * jnp.ones((16,), jnp.float32), (8, 64))
        _ctx_1024t = jnp.einsum('bsk,bkd->bsd', _ctx_1024c, _ctx_1024P)
        _ctx_1024t = _ctx_1024t * jax.lax.rsqrt(jnp.mean(jnp.square(_ctx_1024t)) + 1e-12) * 0.953939
        ctx_1024 = 4.13588e-05 + 0.999923 * (_ctx_1024t + 0.3 * jax.random.normal(jax.random.fold_in(_rk, 611), (8, 64, 256), jnp.float32))
        _validS = jnp.arange(512)[None, :] < _lenS[:, None]
        _validS2 = jnp.arange(64)[None, :] < _lenS2[:, None]
        _causal = jnp.tril(jnp.ones((512, 512), dtype=bool))
        mask_BxS2_bf1 = jnp.ones((8, 64), dtype=bool)
        return (x, ctx_1024, mask_BxS2_bf1)
    x, ctx_1024, mask_BxS2_bf1 = _rec_inputs()

    def _L0_xattn_setup():
        import jax, jax.numpy as jnp
        import numpy as np
        B, T, S, DM, H, D, TOPK = (4, 128, 512, 256, 16, 64, 32)
        INNER = H * D
        key = jax.random.key(seed)
        ks = jax.random.split(key, 7)
        x = jax.random.normal(ks[0], (B, T, DM), dtype=jnp.float32)
        mem_keys = jax.random.normal(ks[1], (B, S, DM), dtype=jnp.float32)
        mem_values = jax.random.normal(ks[2], (B, S, DM), dtype=jnp.float32)
        mem_mask = jnp.ones((B, S), dtype=bool)
        sc = 0.02
        Wq = sc * jax.random.normal(ks[3], (DM, INNER), dtype=jnp.float32)
        Wk = sc * jax.random.normal(ks[4], (DM, INNER), dtype=jnp.float32)
        Wv = sc * jax.random.normal(ks[5], (DM, INNER), dtype=jnp.float32)
        Wo = sc * jax.random.normal(ks[6], (INNER, DM), dtype=jnp.float32)
        inv_temp = jnp.ones((H,), dtype=jnp.float32)
        return {'x': x, 'mem_keys': mem_keys, 'mem_values': mem_values, 'mem_mask': mem_mask, 'Wq': Wq, 'Wk': Wk, 'Wv': Wv, 'Wo': Wo, 'inv_temp': inv_temp}
    _L0_xattn_all = _L0_xattn_setup()
    _L0_xattn_in = {k: v for k, v in _L0_xattn_all.items() if k in ('Wq', 'Wk', 'Wv', 'Wo', 'inv_temp')}
    del _L0_xattn_all

    def _L0_ffn_setup():
        import jax, jax.numpy as jnp
        import numpy as np
        B, S, H, NH, E, F = (4, 256, 256, 16, 8, 1024)
        D = H // NH
        EPS = 1e-05

        def _layernorm(x, g, b):
            mu = jnp.mean(x, axis=-1, keepdims=True)
            var = jnp.var(x, axis=-1, keepdims=True)
            return (x - mu) * jax.lax.rsqrt(var + EPS) * g + b
        key = jax.random.key(seed)
        ks = jax.random.split(key, 16)
        s = 0.02
        return {'x': jax.random.normal(ks[0], (B, S, H), jnp.float32), 'ln1_g': jnp.ones((H,), jnp.float32), 'ln1_b': jnp.zeros((H,), jnp.float32), 'ln2_g': jnp.ones((H,), jnp.float32), 'ln2_b': jnp.zeros((H,), jnp.float32), 'wq': jax.random.normal(ks[1], (H, H), jnp.float32) * s, 'bq': jnp.zeros((H,), jnp.float32), 'wk': jax.random.normal(ks[2], (H, H), jnp.float32) * s, 'bk': jnp.zeros((H,), jnp.float32), 'wv': jax.random.normal(ks[3], (H, H), jnp.float32) * s, 'bv': jnp.zeros((H,), jnp.float32), 'wo': jax.random.normal(ks[4], (H, H), jnp.float32) * s, 'bo': jnp.zeros((H,), jnp.float32), 'gate_w': jax.random.normal(ks[5], (H, E), jnp.float32) * s, 'gate_b': jnp.zeros((E,), jnp.float32), 'w1': jax.random.normal(ks[6], (E, H, F), jnp.float32) * s, 'b1': jnp.zeros((E, F), jnp.float32), 'w2': jax.random.normal(ks[7], (E, F, H), jnp.float32) * s, 'b2': jnp.zeros((E, H), jnp.float32)}
    _L0_ffn_all = _L0_ffn_setup()
    _L0_ffn_in = {k: v for k, v in _L0_ffn_all.items() if k in ('ln1_g', 'ln1_b', 'ln2_g', 'ln2_b', 'wq', 'bq', 'wk', 'bk', 'wv', 'bv', 'wo', 'bo', 'gate_w', 'gate_b', 'w1', 'b1', 'w2', 'b2')}
    del _L0_ffn_all
    return {'x': x, 'ctx_1024': ctx_1024, 'mask_BxS2_bf1': mask_BxS2_bf1, 'L0_xattn_Wq': _L0_xattn_in['Wq'], 'L0_xattn_Wk': _L0_xattn_in['Wk'], 'L0_xattn_Wv': _L0_xattn_in['Wv'], 'L0_xattn_Wo': _L0_xattn_in['Wo'], 'L0_xattn_inv_temp': _L0_xattn_in['inv_temp'], 'L0_ffn_ln1_g': _L0_ffn_in['ln1_g'], 'L0_ffn_ln1_b': _L0_ffn_in['ln1_b'], 'L0_ffn_ln2_g': _L0_ffn_in['ln2_g'], 'L0_ffn_ln2_b': _L0_ffn_in['ln2_b'], 'L0_ffn_wq': _L0_ffn_in['wq'], 'L0_ffn_bq': _L0_ffn_in['bq'], 'L0_ffn_wk': _L0_ffn_in['wk'], 'L0_ffn_bk': _L0_ffn_in['bk'], 'L0_ffn_wv': _L0_ffn_in['wv'], 'L0_ffn_bv': _L0_ffn_in['bv'], 'L0_ffn_wo': _L0_ffn_in['wo'], 'L0_ffn_bo': _L0_ffn_in['bo'], 'L0_ffn_gate_w': _L0_ffn_in['gate_w'], 'L0_ffn_gate_b': _L0_ffn_in['gate_b'], 'L0_ffn_w1': _L0_ffn_in['w1'], 'L0_ffn_b1': _L0_ffn_in['b1'], 'L0_ffn_w2': _L0_ffn_in['w2'], 'L0_ffn_b2': _L0_ffn_in['b2']}

def reference(x, ctx_1024, mask_BxS2_bf1, L0_xattn_Wq, L0_xattn_Wk, L0_xattn_Wv, L0_xattn_Wo, L0_xattn_inv_temp, L0_ffn_ln1_g, L0_ffn_ln1_b, L0_ffn_ln2_g, L0_ffn_ln2_b, L0_ffn_wq, L0_ffn_bq, L0_ffn_wk, L0_ffn_bk, L0_ffn_wv, L0_ffn_bv, L0_ffn_wo, L0_ffn_bo, L0_ffn_gate_w, L0_ffn_gate_b, L0_ffn_w1, L0_ffn_b1, L0_ffn_w2, L0_ffn_b2):
    import jax
    import jax.numpy as jnp

    def _L0_xattn_ref(x, mem_keys, mem_values, mem_mask, Wq, Wk, Wv, Wo, inv_temp):
        import jax, jax.numpy as jnp
        import numpy as np
        B, T, S, DM, H, D, TOPK = (4, 128, 512, 256, 16, 64, 32)
        INNER = H * D
        b, t, _ = x.shape
        s = mem_keys.shape[1]
        q = (x @ Wq).reshape(b, t, H, D).transpose(0, 2, 1, 3)
        k = (mem_keys @ Wk).reshape(b, s, H, D).transpose(0, 2, 1, 3)
        v = (mem_values @ Wv).reshape(b, s, H, D).transpose(0, 2, 1, 3)
        q = q * inv_temp.reshape(1, H, 1, 1)
        scores = jnp.einsum('bhtd,bhsd->bhts', q, k) / jnp.asarray(np.sqrt(D), x.dtype)
        scores = jnp.where(mem_mask[:, None, None, :], scores, -jnp.inf)
        full_attn = jax.nn.softmax(scores, axis=-1)
        topk_vals = jax.lax.top_k(scores, TOPK)[0]
        threshold = topk_vals[..., -1:]
        topk_mask = (scores >= threshold).astype(scores.dtype)
        sparse_attn = full_attn * topk_mask
        sparse_attn = sparse_attn / (jnp.sum(sparse_attn, axis=-1, keepdims=True) + 1e-08)
        attn = full_attn + jax.lax.stop_gradient(sparse_attn - full_attn)
        out = jnp.einsum('bhts,bhsd->bhtd', attn, v)
        out = out.transpose(0, 2, 1, 3).reshape(b, t, INNER)
        return out @ Wo

    def _L0_ffn_ref(x, ln1_g, ln1_b, ln2_g, ln2_b, wq, bq, wk, bk, wv, bv, wo, bo, gate_w, gate_b, w1, b1, w2, b2):
        import jax, jax.numpy as jnp
        import numpy as np
        B, S, H, NH, E, F = (4, 256, 256, 16, 8, 1024)
        D = H // NH
        EPS = 1e-05

        def _layernorm(x, g, b):
            mu = jnp.mean(x, axis=-1, keepdims=True)
            var = jnp.var(x, axis=-1, keepdims=True)
            return (x - mu) * jax.lax.rsqrt(var + EPS) * g + b
        b, s, h = x.shape
        hn = _layernorm(x, ln1_g, ln1_b)
        q = (hn @ wq + bq).reshape(b, s, NH, D).transpose(0, 2, 1, 3)
        k = (hn @ wk + bk).reshape(b, s, NH, D).transpose(0, 2, 1, 3)
        v = (hn @ wv + bv).reshape(b, s, NH, D).transpose(0, 2, 1, 3)
        scores = jnp.einsum('bhqd,bhkd->bhqk', q, k) / jnp.sqrt(jnp.float32(D))
        attn = jax.nn.softmax(scores, axis=-1)
        o = jnp.einsum('bhqk,bhkd->bhqd', attn, v)
        o = o.transpose(0, 2, 1, 3).reshape(b, s, h)
        x = x + (o @ wo + bo)
        hn2 = _layernorm(x, ln2_g, ln2_b).reshape(-1, h)
        logits = hn2 @ gate_w + gate_b
        idx = jnp.argmax(logits, axis=-1)
        mid = jax.nn.relu(jnp.einsum('th,ehf->etf', hn2, w1) + b1[:, None, :])
        y = jnp.einsum('etf,efh->eth', mid, w2) + b2[:, None, :]
        moe = y[idx, jnp.arange(hn2.shape[0])]
        return x + moe.reshape(b, s, h)
    x = x + _L0_xattn_ref(_layernorm(x, axis=-1), ctx_1024, ctx_1024, mask_BxS2_bf1, L0_xattn_Wq, L0_xattn_Wk, L0_xattn_Wv, L0_xattn_Wo, L0_xattn_inv_temp)
    x = x + _L0_ffn_ref(_layernorm(x, axis=-1), L0_ffn_ln1_g, L0_ffn_ln1_b, L0_ffn_ln2_g, L0_ffn_ln2_b, L0_ffn_wq, L0_ffn_bq, L0_ffn_wk, L0_ffn_bk, L0_ffn_wv, L0_ffn_bv, L0_ffn_wo, L0_ffn_bo, L0_ffn_gate_w, L0_ffn_gate_b, L0_ffn_w1, L0_ffn_b1, L0_ffn_w2, L0_ffn_b2)
    return x

_drawn_inputs = setup_inputs


def setup_inputs(seed=0):
    import zlib

    import numpy as np

    out = dict(_drawn_inputs(seed))
    spreads = {'L0_xattn_inv_temp': (1.0, 0.6),
     'L0_ffn_ln1_g': (1.0, 0.6),
     'L0_ffn_ln1_b': (0.0, 0.689),
     'L0_ffn_ln2_g': (1.0, 0.2),
     'L0_ffn_ln2_b': (0.0, 0.1),
     'L0_ffn_bq': (0.0, 0.8),
     'L0_ffn_bk': (0.0, 0.8),
     'L0_ffn_bv': (0.0, 0.393),
     'L0_ffn_bo': (0.0, 0.1),
     'L0_ffn_gate_b': (0.0, 0.1),
     'L0_ffn_b1': (0.0, 0.367),
     'L0_ffn_b2': (0.0, 0.1)}
    factors = {'L0_ffn_wq': 8.0, 'L0_ffn_wk': 8.0, 'L0_ffn_wv': 4.297}
    for name, (base, spread) in spreads.items():
        noise = np.random.default_rng([zlib.crc32(name.encode()), seed]).standard_normal(out[name].shape)
        drawn = base * np.exp(spread * noise) if base else spread * noise
        out[name] = jnp.asarray(drawn.astype(out[name].dtype))
    for name, factor in factors.items():
        out[name] = (out[name] * factor).astype(out[name].dtype)
    return out
```

```python
from contextlib import ExitStack

import concourse.bass as bass
from concourse import mybir

F32 = mybir.dt.float32
F32R = mybir.dt.float32r
I32 = mybir.dt.int32
U32 = mybir.dt.uint32
U8 = mybir.dt.uint8
ALU = mybir.AluOpType
ACT = mybir.ActivationFunctionType
AX = mybir.AxisListType

P = 128
B, S, DM = 8, 512, 256
KT = DM // P
H, CK = 16, 64
HP = H // 2
PAIRS = CK // 2
NH, D = 16, 16
NT = S // P
TILES = B * NT
TOK = B * S
E, FF = 8, 1024
FT = FF // P
ETILES = (TOK - E) // P + E
SLOTS = ETILES * P
G = NH // 4
VC = 32
EPS = 1e-5
BIG = 3.0e38
MASKED = 1.0e30

COLS = {}
for _name, _n in (("temp", HP), ("ln1_g", KT), ("ln1_b", KT), ("bq", KT), ("bk", KT), ("bv", KT),
                  ("ln2_g", KT), ("ln2_b", KT)):
    COLS[_name] = sum(n for _, n in COLS.values()), _n
NCOLS = sum(n for _, n in COLS.values())

XS = [("M", c) for c in range(4)] + [("VW", c) for c in range(4)]
XS += [("sc", t, h) for t in (0, 1, 2) for h in range(2)]
XS += [("pT", 0, h) for h in range(2)] + [("sc", 3, h) for h in range(2)]
XS += [("pT", t, h) for t in (1, 2, 3) for h in range(2)]
XT = [("xn", 0), ("xn", 1), ("xn", 2), ("av", 0), ("yn", 0), ("xn", 3), ("av", 1), ("yn", 1),
      ("av", 2), ("yn", 2), ("av", 3), ("yn", 3)]
FR = [("q", 0), ("q", 1), ("k", 0), ("k", 1)] + [("v", t) for t in range(NT)]
FR += [("s", 0, h, t) for h in range(4) for t in range(NT)] + [("ct", 0)]
for _g in range(G):
    for _t in range(NT):
        for _h in range(4):
            if _g + 1 < G:
                FR += [("s", _g + 1, _h, _t)]
            FR += [("st", _g, _h, _t)]
    if _g + 1 < G:
        FR += [("ct", _g + 1)]
    FR += [("ot", _g)]
for _t in range(NT + 1):
    if _t < NT:
        FR += [("oT", _t), ("wo", _t)]
    if _t > 0:
        FR += [("zT", _t - 1), ("gate", _t - 1)]
XS_N = {u: n for n, u in enumerate(XS)}
XT_N = {u: n for n, u in enumerate(XT)}
FR_N = {u: n for n, u in enumerate(FR)}
NFR = 4
assert len(XS) % 2 == 0 and len(FR) % NFR == 0

NCONST = 12
STEPS_P = 35
STEPS_V = 45
W1COLS = KT * FF + FT

DCON = {}
for _name, _n in (("before", P), ("ones", P), ("order", E), ("steps", TILES), ("tile", ETILES), ("part", 1),
                  ("token", TILES)):
    DCON[_name] = sum(n for _, n in DCON.values()), _n
NDCON = sum(n for _, n in DCON.values())

def reads(j, per, count):
    return j * per + count


def at(i, per, count):
    return i * per + (count + 1)


def program(nc, x, ctxT, maskb, wqT, wk, wv, wo, cols, fwq, fwk, fwv, fwo, bo, gate_w, gate_b,
            w1b, w2t, b2, ident_in, dcon_in, out):
    ctx = ExitStack()
    with ctx:
        started = []

        def sb(name, shape, dt=F32):
            return ctx.enter_context(nc.sbuf_tensor(name, shape, dt))

        def bank(name):
            return ctx.enter_context(nc.psum_tensor(name, [P, 512], F32))

        def sem(name):
            return ctx.enter_context(nc.semaphore(name))

        def lsem(name):
            started.append(sem(name))
            return started[-1]

        def dram(name, shape, dt=F32):
            return nc.dram_tensor(name, shape, dt, kind="Internal").ap()

        kT_d = dram("kT_d", (HP, P, B * CK))
        vT_d = dram("vT_d", (HP, P, B * CK))
        parts_d = dram("parts_d", (4, NH * D, S))
        rows_d = dram("rows_d", (TOK + 1, 2 * DM))
        token_d = dram("token_d", (SLOTS, 1), U32)
        widx_d = dram("widx_d", (ETILES, P, 2), U32)

        ident = sb("ident", [P, P])
        col = sb("col", [P, NCOLS])
        bias_m = sb("bias_m", [P, B * CK])
        mask_u = sb("mask_u", [P, B * CK], U8)
        bo_b = sb("bo_b", [P, DM])
        gb_b = sb("gb_b", [P, E])
        wqT_s = sb("wqT_s", [P, HP, DM])
        wo_s = sb("wo_s", [P, HP, DM])
        fw = {n: sb("f" + n, [P, KT, DM]) for n in ("q", "k", "v", "o")}
        gw = sb("gw", [P, KT, E])
        logits = sb("logits", [P, TILES * E])
        zrow = sb("zrow", [NT * 4, P])

        def cv(name, n):
            return col[:, COLS[name][0] + n:COLS[name][0] + n + 1]

        attn_space = ExitStack()

        def sa(name, shape, dt=F32):
            return attn_space.enter_context(nc.sbuf_tensor(name, shape, dt))

        kbd = sa("kbd", [P, HP, P])
        vbd = sa("vbd", [P, HP, P])
        M = sa("M", [P, KT, H * CK])
        VW = sa("VW", [P, HP, DM])
        xb = sa("xb", [P, NT, DM])
        xstat = sa("xstat", [P, NT, 6])
        xmv = sa("xmv", [P, NT, 2])
        xr = sa("xr", [P, NT, 2])
        xn = sa("xn", [P, NT, DM])
        xnT = sa("xnT", [P, KT, P])
        sraw = sa("sraw", [P, H * CK])
        s = sa("s", [P, 2, H, CK])
        e = sa("e", [P, 2, H, CK])
        m = sa("m", [P, 2, H, CK])
        hi = sa("hi", [P, H, PAIRS])
        lo = sa("lo", [P, 2, H, PAIRS])
        nhi = sa("nhi", [P, H, PAIRS])
        mx = sa("mx", [P, 2, H])
        lo17 = sa("lo17", [P, H, 17])
        nh17 = sa("nh17", [P, H, 17])
        merged = sa("merged", [P, H, 17])
        thr = sa("thr", [P, H])
        sums = sa("sums", [P, 2, H])
        den = sa("den", [P, H])
        rden = sa("rden", [P, 2, H])
        pT = sa("pT", [P, HP * P])
        x1 = sa("x1", [P, NT, DM])
        ystat = sa("ystat", [P, 6])
        ymv = sa("ymv", [P, 2])
        yv = sa("yv", [P, 4])
        mhalf = sa("mhalf", [P, NT])
        yr = sa("yr", [P, 2, 4])
        y = sa("y", [P, 2, DM])
        yn = sa("yn", [P, DM])
        yb = sa("yb", [P, NT, DM])
        hnT = sa("hnT", [P, KT, S])

        parts = sa("parts", [P, 2, 2, S], F32R)
        qs = sa("qs", [P, 8, S], F32R)
        ks = sa("ks", [P, 8, S], F32R)
        v32 = sa("v32", [P, NT, NH, VC])
        nmax = sa("nmax", [P, 2, 4 * NT])
        cT = sa("cT", [NT * 4, P], F32R)
        pt = sa("pt", [P, 2, 4, S])
        osb = sa("osb", [P, S])
        rz = sa("rz", [P, NT, 4])
        on = sa("on", [P, NT, DM])
        oT = sa("oT", [P, KT, P])
        z = sa("z", [P, 2, DM])
        zstat = sa("zstat", [P, 6])
        zmv = sa("zmv", [P, 2])
        zr = sa("zr", [P, 2, 2])
        row = sa("row", [P, 2, 2 * DM])
        znT = sa("znT", [P, KT, P])
        neverslot = sa("neverslot", [P, ETILES], U32)

        pre_ctx = sraw[:, :].rearrange("p (k n) -> p k n", k=KT)
        pre_w = [b[:, :, :, :].rearrange("p a h c -> p (a h c)").rearrange("p (k n) -> p k n", k=KT) for b in (s, e)]
        pre_out = [[m[:, r, 8 * n:8 * n + 8, :].rearrange("p h c -> p (h c)") for n in range(2)] for r in range(2)]

        xs = [bank(f"xs{n}") for n in range(2)]
        xt = bank("xt")
        fr = [bank(f"fr{n}") for n in range(NFR)]
        ob = bank("ob")
        ET, EH, EO = fr[0:2], [xs[0], xs[1], fr[2], fr[3]], [xt, ob]

        const_loaded, proj_loaded = sem("const_loaded"), sem("proj_loaded")
        zeroed, consts_ready = sem("zeroed"), sem("consts_ready")
        kv_full, p_set = sem("kv_full"), sem("p_set")
        kv_copied = [sem("k_copied"), sem("v_copied")]
        kv_stored = [[sem(f"k_stored{n}") for n in range(2)], [sem(f"v_stored{n}") for n in range(2)]]
        kbd_loaded, x_loaded = lsem("kbd_loaded"), lsem("x_loaded")
        v_step, v_gate, p_step, p_gate = lsem("v_step"), sem("v_gate"), lsem("p_step"), sem("p_gate")
        xs_full, xt_full, fr_full, o_full = lsem("xs_full"), lsem("xt_full"), lsem("fr_full"), lsem("o_full")
        xs_emptied = [lsem(f"xs_emptied{n}") for n in range(2)]
        xt_emptied, o_emptied = lsem("xt_emptied"), lsem("o_emptied")
        fr_emptied = [lsem(f"fr_emptied{n}") for n in range(NFR)]
        xr_ready, xn_ready = lsem("xr_ready"), lsem("xn_ready")
        s_ready, split_done, neg_done, mask_done = (lsem("s_ready"), lsem("split_done"), lsem("neg_done"),
                                                    lsem("mask_done"))
        d_ready, e_ready, em_ready, rden_ready, p_ready = (lsem("d_ready"), lsem("e_ready"), lsem("em_ready"),
                                                           lsem("rden_ready"), lsem("p_ready"))
        mx_ready, xmv_ready, ymv_ready, zmv_ready = lsem("mx_ready"), lsem("xmv_ready"), lsem("ymv_ready"), lsem("zmv_ready")
        yr_ready, y_ready, yn_ready, yb_ready = lsem("yr_ready"), lsem("y_ready"), lsem("yn_ready"), lsem("yb_ready")
        part_hi, parts_stored = lsem("part_hi"), [lsem(f"parts_stored{n}") for n in range(2)]
        stack_loaded = [lsem("stack_loaded0"), lsem("stack_loaded1")]
        c_loaded = lsem("c_loaded")
        zr_ready, zn_ready, res_ready = lsem("zr_ready"), lsem("zn_ready"), lsem("res_ready")
        rows_stored, scratch_set = [lsem(f"rows_stored{n}") for n in range(2)], sem("scratch_set")

        dcon_loaded, d_step, oh_ready, count_full = (sem("dcon_loaded"), sem("d_step"), sem("oh_ready"),
                                                     sem("count_full"))
        slots_ready, rec_ready, tokens_set, rec_set = (sem("slots_ready"), sem("rec_ready"), sem("tokens_set"),
                                                       sem("rec_set"))

        def pair(name):
            return [sem(f"{name}{n}") for n in range(2)]

        gid_loaded, sid_loaded, wid_loaded = pair("gid_loaded"), pair("sid_loaded"), pair("wid_loaded")
        rows_in, w1_in, w2_in, b2_in = pair("rows_in"), pair("w1_in"), pair("w2_in"), pair("b2_in")
        turned, turned_out = pair("turned"), pair("turned_out")
        l1_full, l2_full = pair("l1_full"), pair("l2_full")
        mid_act, mid_dve = pair("mid_act"), pair("mid_dve")
        resb_ready, ot_ready, scattered = pair("resb_ready"), pair("ot_ready"), pair("scattered")

        def xs_written(eng, i, u):
            eng.wait_ge(xs_full, at(i, len(XS), XS_N[u] + 1))

        def xs_read(eng, i, u):
            n = XS_N[u]
            eng.wait_ge(xs_emptied[n % 2], at(i, len(XS) // 2, n // 2 + 1))

        def xt_written(eng, i, u):
            eng.wait_ge(xt_full, at(i, len(XT), XT_N[u] + 1))

        def xt_read(eng, i, u):
            eng.wait_ge(xt_emptied, at(i, len(XT), XT_N[u] + 1))

        def fr_written(eng, i, u):
            eng.wait_ge(fr_full, at(i, len(FR), FR_N[u] + 1))

        def fr_read(eng, i, u):
            n = FR_N[u]
            eng.wait_ge(fr_emptied[n % NFR], at(i, len(FR) // NFR, n // NFR + 1))

        def fr_bank(u):
            return fr[FR_N[u] % NFR]

        def fr_sem(u):
            return fr_emptied[FR_N[u] % NFR]

        with nc.Block() as start:
            def raise_to_one(eng, share):
                for q in started[share::5]:
                    eng.sem_inc(q, 1)

            @start.sync
            def _(sp):
                raise_to_one(sp, 0)

            @start.tensor
            def _(pe):
                raise_to_one(pe, 1)

            @start.scalar
            def _(act):
                raise_to_one(act, 2)

            @start.vector
            def _(dve):
                raise_to_one(dve, 3)

            @start.gpsimd
            def _(pool):
                raise_to_one(pool, 4)

        block_ctx = ExitStack()
        block = block_ctx.enter_context(nc.Block())

        @block.sync
        def _(sp):
            def cload(dst, src):
                sp.dma_start(dst, src).then_inc(const_loaded, 16)

            sp.dma_start(pre_ctx, ctxT.rearrange("(k p) n -> p k n", p=P)).then_inc(proj_loaded, 16)
            sp.dma_start(pre_w[0], wk.rearrange("(k p) n -> p k n", p=P)).then_inc(proj_loaded, 16)
            sp.dma_start(pre_w[1], wv.rearrange("(k p) n -> p k n", p=P)).then_inc(proj_loaded, 16)
            cload(col[:, :], cols)
            cload(ident[:, :], ident_in)
            cload(mask_u[:, :], maskb.to_broadcast((P, B * CK)))
            cload(wqT_s[:, :, :], wqT.rearrange("(h p) n -> p h n", p=P))
            cload(wo_s[:, :, :], wo.rearrange("(h p) n -> p h n", p=P))
            for name, w in (("q", fwq), ("k", fwk), ("v", fwv), ("o", fwo)):
                cload(fw[name][:, :, :], w.rearrange("(k p) n -> p k n", p=P))
            cload(gw[:, :, :], gate_w.rearrange("(k p) n -> p k n", p=P))
            cload(bo_b[:, :], bo.to_broadcast((P, DM)))
            cload(gb_b[:, :], gate_b.to_broadcast((P, E)))
            for n in range(2 * HP):
                sp.wait_ge(kv_copied[n % 2], n // 2 + 1)
                sp.dma_start((kT_d, vT_d)[n % 2][n // 2], pre_out[(n // 2) % 2][n % 2])\
                  .then_inc(kv_stored[n % 2][(n // 2) % 2], 16)
            for q in kv_stored[0] + kv_stored[1]:
                sp.wait_ge(q, 16 * HP // 2)
            sp.wait_ge(zeroed, 2)
            sp.dma_start(token_d.rearrange("(p t) o -> p (t o)", p=P), neverslot[:, :]).then_inc(scratch_set, 16)
            sp.dma_start(rows_d[TOK:TOK + 1, :].rearrange("o (a c) -> (o a) c", c=P), zrow[0:4, :])\
              .then_inc(scratch_set, 16)

            with sp.Fori(0, B) as i:
                sp.wait_ge(xt_emptied, at(i, len(XT), 0))
                sp.dma_start(xb[:, :, :], x[bass.ds(i, 1)].rearrange("a (t p) d -> p (a t) d", p=P))\
                  .then_inc(x_loaded, 16)
                sp.wait_ge(xs_full, at(i, len(XS), 0))
                for dst, src in ((kbd, kT_d), (vbd, vT_d)):
                    for hh in range(2):
                        r = slice(CK * hh, CK * hh + CK)
                        sp.dma_start(dst[r, :, r],
                                     src[:, r, bass.ds(i * CK, CK)].rearrange("h p s -> p h s"))\
                          .then_inc(kbd_loaded, 16)
                for n, u in enumerate((("q", 0), ("q", 1), ("k", 0), ("k", 1))):
                    base, mt = 2 * (n // 2), n % 2
                    fr_read(sp, i, u)
                    for j in range(2):
                        sp.dma_start(parts_d[base + j, mt * P:(mt + 1) * P, :],
                                     parts[:, n % 2, j, :].bitcast(F32)).then_inc(parts_stored[n % 2], 16)
                for q in parts_stored:
                    sp.wait_ge(q, at(i, 64, 64))

                def load_stack(g):
                    sl = slice(4 * (g % 2), 4 * (g % 2) + 4)
                    if g >= 2:
                        fr_written(sp, i, ("st", g - 2, 3, NT - 1))
                    for dst, order in ((qs, (0, 0, 1, 1)), (ks, (2, 3, 2, 3))):
                        for r, part in enumerate(order):
                            src = parts_d[part, 64 * g:64 * g + 64, :].rearrange("(h d) s -> d h s", d=D)
                            sp.dma_start(dst[D * r:D * r + D, sl, :].bitcast(F32), src)\
                              .then_inc(stack_loaded[g % 2], 16)
                    sp.dma_start(qs[4 * D:4 * D + 1, sl, :].bitcast(F32).rearrange("o h (t c) -> o (h t) c", c=P),
                                 zrow[:, :]).then_inc(stack_loaded[g % 2], 16)

                def load_max(g):
                    sl = slice(4 * (g % 2), 4 * (g % 2) + 4)
                    fr_read(sp, i, ("ct", g))
                    sp.dma_start(qs[4 * D:4 * D + 1, sl, :].bitcast(F32).rearrange("o h (t c) -> o (h t) c", c=P),
                                 cT[:, :].bitcast(F32)).then_inc(c_loaded, 16)

                load_stack(0)
                load_stack(1)
                load_max(0)
                load_stack(2)
                load_max(1)
                load_stack(3)
                load_max(2)
                load_max(3)
                for t in range(NT):
                    sp.wait_ge(res_ready, at(i, NT, t + 1))
                    sp.wait_ge(zn_ready, at(i, NT, t + 1))
                    sp.dma_start(rows_d[bass.ds(i * S + t * P, P), :], row[:, t % 2, :]).then_inc(rows_stored[t % 2], 16)
            for q in rows_stored:
                sp.wait_ge(q, 16 * TILES // 2 + 1)
            sp.wait_ge(scratch_set, 32)

        @block.tensor
        def _(pe):
            def mm(o, l, r, first=True, last=True):
                return pe.matmul(o, l, r, start=first, stop=last)

            def tr(o, src):
                return pe.transpose(o, src, ident[:, :])

            pe.wait_ge(proj_loaded, 48)
            for n in range(2 * HP):
                if n >= NFR:
                    pe.wait_ge(kv_copied[n % 2], (n - NFR) // 2 + 1)
                hp = n // 2
                for k in range(KT):
                    ins = mm(fr[n % NFR][:, :], pre_w[n % 2][:, k, hp * P:(hp + 1) * P], pre_ctx[:, k, :],
                             k == 0, k == KT - 1)
                ins.then_inc(kv_full, 1)
            pe.wait_ge(const_loaded, 16 * NCONST)
            for q in kv_copied:
                pe.wait_ge(q, HP)
            pe.wait_ge(zeroed, 2)

            def xs_slot(i, u):
                n = XS_N[u]
                pe.wait_ge(xs_emptied[n % 2], at(i, len(XS) // 2, n // 2))
                return xs[n % 2]

            def xt_slot(i, u):
                pe.wait_ge(xt_emptied, at(i, len(XT), XT_N[u]))
                return xt

            def fr_slot(i, u):
                n = FR_N[u]
                pe.wait_ge(fr_emptied[n % NFR], at(i, len(FR) // NFR, n // NFR))
                return fr[n % NFR]

            def fold(i):
                pe.wait_ge(kbd_loaded, at(i, 64, 64))
                for c in range(4):
                    o = xs_slot(i, ("M", c))
                    mt, half = c // 2, c % 2
                    for j in range(4):
                        hp = 4 * half + j
                        ins = mm(o[:, j * P:(j + 1) * P], wqT_s[:, hp, mt * P:(mt + 1) * P], kbd[:, hp, :])
                    ins.then_inc(xs_full, 1)
                for c in range(4):
                    o = xs_slot(i, ("VW", c))
                    for j in range(2):
                        hp = 2 * c + j
                        ins = mm(o[:, j * DM:(j + 1) * DM], vbd[:, hp, :], wo_s[:, hp, :])
                    ins.then_inc(xs_full, 1)

            def x_turn(i, t):
                pe.wait_ge(xn_ready, at(i, NT, t + 1))
                o = xt_slot(i, ("xn", t))
                for k in range(KT):
                    ins = tr(o[:, k * P:(k + 1) * P], xn[:, t, k * P:(k + 1) * P])
                ins.then_inc(xt_full, 1)

            def x_scores(i, t):
                xt_read(pe, i, ("xn", t))
                for half in range(2):
                    o = xs_slot(i, ("sc", t, half))
                    if t == 0 and half == 0:
                        xs_read(pe, i, ("M", 3))
                    for k in range(KT):
                        ins = mm(o[:, :], xnT[:, k, :], M[:, k, half * 512:(half + 1) * 512], k == 0, k == KT - 1)
                    ins.then_inc(xs_full, 1)

            def x_pT(i, t):
                pe.wait_ge(p_ready, at(i, NT, t + 1))
                for half in range(2):
                    o = xs_slot(i, ("pT", t, half))
                    for j in range(4):
                        h0 = 8 * half + 2 * j
                        ins = tr(o[:, j * P:(j + 1) * P],
                                 m[:, t % 2, h0:h0 + 2, :].rearrange("p h c -> p (h c)"))
                    ins.then_inc(xs_full, 1)

            def x_av(i, t):
                o = xt_slot(i, ("av", t))
                xs_read(pe, i, ("pT", t, 1))
                for hp in range(HP):
                    ins = mm(o[:, 0:DM], pT[:, hp * P:(hp + 1) * P], VW[:, hp, :], hp == 0, hp == HP - 1)
                ins.then_inc(xt_full, 1)

            def y_turn(i, t):
                pe.wait_ge(yn_ready, at(i, NT, t + 1))
                o = xt_slot(i, ("yn", t))
                for k in range(KT):
                    ins = tr(o[:, k * P:(k + 1) * P], yn[:, k * P:(k + 1) * P])
                ins.then_inc(xt_full, 1)

            def X(i):
                fold(i)
                for t in range(2):
                    x_turn(i, t)
                    x_scores(i, t)
                for t in range(NT):
                    if t > 0:
                        y_turn(i, t - 1)
                    if t < 2:
                        x_turn(i, t + 2)
                        if t == 0:
                            x_scores(i, 2)
                            x_pT(i, 0)
                        else:
                            x_scores(i, 3)
                            x_pT(i, 1)
                    else:
                        x_pT(i, t)
                    x_av(i, t)
                y_turn(i, NT - 1)

            def projections(i):
                xt_read(pe, i, ("yn", NT - 1))
                for name in ("q", "k"):
                    for mt in range(2):
                        o = fr_slot(i, (name, mt))
                        for k in range(KT):
                            ins = mm(o[:, :], fw[name][:, k, mt * P:(mt + 1) * P], hnT[:, k, :], k == 0, k == KT - 1)
                        ins.then_inc(fr_full, 1)
                for t in range(NT):
                    o = fr_slot(i, ("v", t))
                    for k in range(KT):
                        ins = mm(o[:, 0:DM], hnT[:, k, t * P:(t + 1) * P], fw["v"][:, k, :], k == 0, k == KT - 1)
                    ins.then_inc(fr_full, 1)

            def s_unit(i, g, h, t):
                sl = 4 * (g % 2) + h
                o = fr_slot(i, ("s", g, h, t))
                mm(o[:, :], qs[:, sl, t * P:(t + 1) * P], ks[:, sl, :]).then_inc(fr_full, 1)

            def st_unit(i, g, h, t):
                sl = 4 * (g % 2) + h
                o = fr_slot(i, ("st", g, h, t))
                mm(o[:, :], ks[:, sl, t * P:(t + 1) * P], qs[:, sl, :]).then_inc(fr_full, 1)

            def turn_max(i, g):
                fr_read(pe, i, ("s", g, 3, NT - 1))
                o = fr_slot(i, ("ct", g))
                tr(o[0:4 * NT, 0:P], nmax[:, g % 2, :]).then_inc(fr_full, 1)

            def pv(i, g, t):
                fr_read(pe, i, ("st", g, 3, t))
                if t == 0:
                    pe.wait_ge(o_emptied, at(i, G, g))
                for h in range(4):
                    ins = pe.matmul(ob[VC * h:VC * h + VC, :], v32[:, t, 4 * g + h, :], pt[:, t % 2, h, :],
                                    start=(t == 0), stop=(t == NT - 1))
                ins.then_inc(o_full, 1)

            def turn_o(i, g):
                pe.wait_ge(o_emptied, at(i, G, g + 1))
                o = fr_slot(i, ("ot", g))
                for t in range(NT):
                    ins = tr(o[:, t * P:(t + 1) * P], osb[:, t * P:(t + 1) * P])
                ins.then_inc(fr_full, 1)

            def attention(i):
                pe.wait_ge(stack_loaded[0], at(i, 16 * 9 * 2, 16 * 9))
                for h in range(4):
                    for t in range(NT):
                        s_unit(i, 0, h, t)
                turn_max(i, 0)
                for g in range(G):
                    if g + 1 < G:
                        pe.wait_ge(stack_loaded[(g + 1) % 2], at(i, 16 * 9 * 2, 16 * 9 * ((g + 1) // 2 + 1)))
                    for t in range(NT):
                        for h in range(4):
                            if g + 1 < G:
                                s_unit(i, g + 1, h, t)
                            if h == 0 and t == 0:
                                pe.wait_ge(c_loaded, at(i, 16 * G, 16 * (g + 1)))
                            st_unit(i, g, h, t)
                        if t > 0:
                            pv(i, g, t - 1)
                    if g + 1 < G:
                        turn_max(i, g + 1)
                    pv(i, g, NT - 1)
                    turn_o(i, g)

            def out_proj(i, t):
                if t == 0:
                    fr_read(pe, i, ("ot", G - 1))
                o = fr_slot(i, ("oT", t))
                for k in range(KT):
                    ins = tr(o[:, k * P:(k + 1) * P], on[:, t, k * P:(k + 1) * P])
                ins.then_inc(fr_full, 1)
                o = fr_slot(i, ("wo", t))
                fr_read(pe, i, ("oT", t))
                for k in range(KT):
                    ins = mm(o[:, 0:DM], oT[:, k, :], fw["o"][:, k, :], k == 0, k == KT - 1)
                ins.then_inc(fr_full, 1)

            def gate(i, t):
                pe.wait_ge(zn_ready, at(i, NT, t + 1))
                o = fr_slot(i, ("zT", t))
                for k in range(KT):
                    ins = tr(o[:, k * P:(k + 1) * P], row[:, t % 2, k * P:(k + 1) * P])
                ins.then_inc(fr_full, 1)
                o = fr_slot(i, ("gate", t))
                fr_read(pe, i, ("zT", t))
                for k in range(KT):
                    ins = mm(o[:, 0:E], znT[:, k, :], gw[:, k, :], k == 0, k == KT - 1)
                ins.then_inc(fr_full, 1)

            with pe.Fori(0, B) as i:
                X(i)
                projections(i)
                attention(i)
                for t in range(NT + 1):
                    if t < NT:
                        out_proj(i, t)
                    if t > 0:
                        gate(i, t - 1)

        @block.scalar
        def _(act):
            def copy(o, src, scale=1.0, bias=None):
                if bias is None:
                    return act.activation(o, src, ACT.Copy, scale=scale)
                return act.activation(o, src, ACT.Identity, scale=scale, bias=bias)

            act.wait_ge(consts_ready, 1)
            for n in range(HP):
                act.wait_ge(kv_full, 2 * n + 1)
                if n >= 2:
                    act.wait_ge(kv_stored[0][n % 2], 16 * (n // 2))
                act.activation(pre_out[n % 2][0], fr[(2 * n) % NFR][:, :], ACT.Copy, scale=cv("temp", n))\
                   .then_inc(kv_copied[0], 1)
            act.wait_ge(consts_ready, 2)

            def fold_out(i):
                for c in range(4):
                    u = ("M", c)
                    xs_written(act, i, u)
                    copy(M[:, c // 2, (c % 2) * 512:(c % 2 + 1) * 512], xs[XS_N[u] % 2][:, :])\
                        .then_inc(xs_emptied[XS_N[u] % 2], 1)
                for c in range(4):
                    u = ("VW", c)
                    xs_written(act, i, u)
                    copy(VW[:, 2 * c:2 * c + 2, :].rearrange("p h d -> p (h d)"), xs[XS_N[u] % 2][:, :])\
                        .then_inc(xs_emptied[XS_N[u] % 2], 1)

            def x_norm(i, t):
                act.wait_ge(xr_ready, at(i, NT, t + 1))
                copy(xn[:, t, :], xb[:, t, :], xr[:, t, 0:1], xr[:, t, 1:2]).then_inc(xn_ready, 1)

            def scores_out(i, t):
                xt_written(act, i, ("xn", t))
                copy(xnT[:, :, :].rearrange("p k c -> p (k c)"), xt[:, 0:DM]).then_inc(xt_emptied, 1)
                for half in range(2):
                    u = ("sc", t, half)
                    xs_written(act, i, u)
                    if t > 0 and half == 0:
                        act.wait_ge(s_ready, at(i, NT, t))
                    copy(sraw[:, half * 512:(half + 1) * 512], xs[XS_N[u] % 2][:, :])\
                        .then_inc(xs_emptied[XS_N[u] % 2], 1)

            def negate(i, t):
                act.wait_ge(split_done, at(i, NT, t + 1))
                if t > 0:
                    act.wait_ge(mask_done, at(i, NT, t))
                act.activation(nhi[:, :, :].rearrange("p h c -> p (h c)"),
                               hi[:, :, :].rearrange("p h c -> p (h c)"), ACT.Copy, scale=-1.0)\
                   .then_inc(neg_done, 1)

            def exponent(i, t):
                act.wait_ge(d_ready, at(i, NT, t + 1))
                ev = e[:, t % 2, :, :].rearrange("p h c -> p (h c)")
                act.activation(ev, ev, ACT.Exp).then_inc(e_ready, 1)

            def pT_out(i, t):
                for half in range(2):
                    u = ("pT", t, half)
                    xs_written(act, i, u)
                    copy(pT[:, half * 512:(half + 1) * 512], xs[XS_N[u] % 2][:, :])\
                        .then_inc(xs_emptied[XS_N[u] % 2], 1)

            def y_norm(i, t):
                act.wait_ge(yr_ready, at(i, NT, t + 1))
                r = yr[:, t % 2, :]
                if t > 1:
                    act.wait_ge(yb_ready, at(i, NT, t - 1))
                copy(y[:, t % 2, :], x1[:, t, :], r[:, 0:1], r[:, 2:3]).then_inc(y_ready, 1)
                if t > 0:
                    xt_written(act, i, ("yn", t - 1))
                copy(yn[:, :], x1[:, t, :], r[:, 1:2], r[:, 3:4]).then_inc(yn_ready, 1)
                xt_written(act, i, ("yn", t))
                for k in range(KT):
                    ins = copy(hnT[:, k, t * P:(t + 1) * P], xt[:, k * P:(k + 1) * P], cv("ln1_g", k), cv("ln1_b", k))
                ins.then_inc(xt_emptied, 1)

            def X(i):
                fold_out(i)
                for t in range(NT):
                    x_norm(i, t)
                scores_out(i, 0)
                scores_out(i, 1)
                negate(i, 0)
                exponent(i, 0)
                for t in range(NT):
                    if t + 1 < NT:
                        negate(i, t + 1)
                        exponent(i, t + 1)
                    if t > 0:
                        y_norm(i, t - 1)
                    if t + 2 < NT:
                        scores_out(i, t + 2)
                    pT_out(i, t)
                y_norm(i, NT - 1)

            def heads_out(i):
                for n, u in enumerate((("q", 0), ("q", 1), ("k", 0), ("k", 1))):
                    fr_written(act, i, u)
                    if n >= 2:
                        act.wait_ge(parts_stored[n % 2], at(i, 64, 32))
                    copy(parts[:, n % 2, 0, :], fr_bank(u)[:, :], 1.0, cv("b" + u[0], n % 2))\
                        .then_inc(part_hi, 1)
                for t in range(NT):
                    u = ("v", t)
                    fr_written(act, i, u)
                    copy(v32[:, t, :, 0:D], fr_bank(u)[:, 0:DM].rearrange("p (h d) -> p h d", d=D))\
                        .then_inc(fr_sem(u), 1)

            def exps(i, g):
                for t in range(NT):
                    n = g * NT + t
                    act.wait_ge(o_full, at(i, G * NT, max(n - 1, 0)))
                    for h in range(4):
                        u = ("st", g, h, t)
                        fr_written(act, i, u)
                        act.activation(pt[:, t % 2, h, :], fr_bank(u)[:, :], ACT.Exp, scale=D ** -0.5)\
                           .then_inc(fr_sem(u), 1)

            def max_out(i, g):
                u = ("ct", g)
                fr_written(act, i, u)
                if g > 0:
                    act.wait_ge(c_loaded, at(i, 16 * G, 16 * g))
                copy(cT[:, :], fr_bank(u)[0:4 * NT, 0:P]).then_inc(fr_sem(u), 1)

            def o_out(i, g):
                act.wait_ge(o_full, at(i, G * NT, NT * (g + 1)))
                if g > 0:
                    fr_written(act, i, ("ot", g - 1))
                copy(osb[:, :], ob[:, :]).then_inc(o_emptied, 1)

            def tail_out(i, t):
                u = ("oT", t)
                fr_written(act, i, u)
                for k in range(KT):
                    ins = copy(oT[:, k, :], fr_bank(u)[:, k * P:(k + 1) * P], 1.0, cv("bv", k))
                ins.then_inc(fr_sem(u), 1)

            def z_norm(i, t):
                act.wait_ge(zr_ready, at(i, NT, t + 1))
                act.wait_ge(rows_stored[t % 2], at(i, 8 * NT, 16 * (t // 2)))
                copy(row[:, t % 2, 0:DM], z[:, t % 2, :], zr[:, t % 2, 0:1], zr[:, t % 2, 1:2]).then_inc(zn_ready, 1)
                u = ("zT", t)
                fr_written(act, i, u)
                for k in range(KT):
                    ins = copy(znT[:, k, :], fr_bank(u)[:, k * P:(k + 1) * P], cv("ln2_g", k), cv("ln2_b", k))
                ins.then_inc(fr_sem(u), 1)

            with act.Fori(0, B) as i:
                X(i)
                heads_out(i)
                max_out(i, 0)
                for g in range(G):
                    exps(i, g)
                    if g + 1 < G:
                        max_out(i, g + 1)
                    o_out(i, g)
                for t in range(NT + 1):
                    if t < NT:
                        tail_out(i, t)
                    if t > 0:
                        z_norm(i, t - 1)

        @block.vector
        def _(dve):
            steps = [0, 0]

            def step(ins):
                steps[1] += 1
                ins.then_inc(v_step, 1)

            def settle(i):
                dve.wait_ge(v_step, at(i, STEPS_V, steps[0] + steps[1]))

            nc.vector.memset(zrow[:, :], 0.0)
            nc.vector.memset(kbd[:, :, :], 0.0)
            nc.vector.memset(vbd[:, :, :], 0.0)
            nc.vector.memset(lo17[:, :, 0:1], BIG)
            nc.vector.memset(nh17[:, :, 16:17], -BIG)
            nc.vector.memset(neverslot[:, :], TOK).then_inc(zeroed, 1)
            dve.wait_ge(const_loaded, 16 * NCONST)
            t0 = COLS["temp"]
            nc.vector.tensor_scalar(col[:, t0[0]:t0[0] + t0[1]], col[:, t0[0]:t0[0] + t0[1]], CK ** -0.5, None,
                                    ALU.mult).then_inc(consts_ready, 1)
            nc.vector.tensor_scalar(bias_m[:, :], mask_u[:, :], 1.0, MASKED, ALU.subtract, ALU.mult)\
              .then_inc(consts_ready, 1)
            for n in range(HP):
                dve.wait_ge(kv_full, 2 * n + 2)
                if n >= 2:
                    dve.wait_ge(kv_stored[1][n % 2], 16 * (n // 2))
                nc.vector.tensor_copy(pre_out[n % 2][1], fr[(2 * n + 1) % NFR][:, :]).then_inc(kv_copied[1], 1)

            def x_stats(i):
                dve.wait_ge(x_loaded, at(i, 16, 16))
                for t in range(NT):
                    ins = nc.vector.bn_stats(xstat[:, t, :], xb[:, t, :])
                step(ins)
                settle(i)
                dve.wait_ge(xr_ready, at(i, NT, 0))
                dve.sem_inc(v_gate, 1)
                for t in range(NT):
                    ins = nc.vector.bn_aggr(xmv[:, t, :], xstat[:, t, :])
                ins.then_inc(xmv_ready, 1)

            def split(i, t):
                dve.wait_ge(s_ready, at(i, NT, t + 1))
                a, b = s[:, t % 2, :, 0:PAIRS], s[:, t % 2, :, PAIRS:CK]
                if t > 0:
                    dve.wait_ge(neg_done, at(i, NT, t))
                step(nc.vector.tensor_tensor(hi[:, :, :], a, b, ALU.max))
                settle(i)
                nc.vector.tensor_tensor(lo[:, t % 2, :, :], a, b, ALU.min).then_inc(split_done, 1)
                nc.vector.tensor_reduce(mx[:, t % 2, :], hi[:, :, :], AX.X, ALU.max).then_inc(mx_ready, 1)

            def threshold(i, t):
                lv, nv = lo[:, t % 2, :, :], nhi[:, :, :]
                dve.wait_ge(split_done, at(i, NT, t + 1))
                dve.wait_ge(neg_done, at(i, NT, t + 1))
                dve.sem_inc(v_gate, 1)
                for h in range(H):
                    nc.vector.max(lo17[:, h, 1:9], lv[:, h, :])
                    ins = nc.vector.max(nh17[:, h, 0:8], nv[:, h, :])
                step(ins)
                settle(i)
                dve.sem_inc(v_gate, 1)
                for h in range(H):
                    nc.vector.match_replace(lv[:, h, :], lo17[:, h, 1:9], lv[:, h, :], -BIG)
                    ins = nc.vector.match_replace(nv[:, h, :], nh17[:, h, 0:8], nv[:, h, :], -BIG)
                step(ins)
                settle(i)
                dve.sem_inc(v_gate, 1)
                for h in range(H):
                    nc.vector.max(lo17[:, h, 9:17], lv[:, h, :])
                    ins = nc.vector.max(nh17[:, h, 8:16], nv[:, h, :])
                step(ins)
                settle(i)
                step(nc.vector.scalar_tensor_tensor(merged[:, :, :], nh17[:, :, :], -1.0, lo17[:, :, :],
                                                    ALU.mult, ALU.min))
                settle(i)
                step(nc.vector.tensor_reduce(thr[:, :], merged[:, :, :], AX.X, ALU.max))
                settle(i)
                if t >= 2:
                    xs_written(dve, i, ("pT", t - 2, 1))
                nc.vector.tensor_tensor(m[:, t % 2, :, :], s[:, t % 2, :, :],
                                        thr[:, :].unsqueeze(2).to_broadcast((P, H, CK)), ALU.is_ge)\
                  .then_inc(mask_done, 1)

            def denominators(i, t):
                dve.wait_ge(e_ready, at(i, NT, t + 1))
                nc.vector.tensor_reduce(sums[:, 1, :], e[:, t % 2, :, :], AX.X, ALU.add)
                dve.wait_ge(em_ready, at(i, NT, t + 1))
                step(nc.vector.tensor_reduce(sums[:, 0, :], m[:, t % 2, :, :], AX.X, ALU.add))
                settle(i)
                step(nc.vector.scalar_tensor_tensor(den[:, :], sums[:, 1, :], 1e-8, sums[:, 0, :],
                                                    ALU.mult, ALU.add))
                settle(i)
                nc.vector.reciprocal(rden[:, t % 2, :], den[:, :]).then_inc(rden_ready, 1)

            def stats(i, src, st, mv):
                step(nc.vector.bn_stats(st, src))
                settle(i)
                dve.sem_inc(v_gate, 1)
                return nc.vector.bn_aggr(mv, st)

            def residual(i, t):
                xt_written(dve, i, ("av", t))
                nc.vector.tensor_tensor(x1[:, t, :], xt[:, 0:DM], xb[:, t, :], ALU.add).then_inc(xt_emptied, 1)
                xt_read(dve, i, ("av", t))
                dve.wait_ge(yr_ready, at(i, NT, t))
                stats(i, x1[:, t, :], ystat[:, :], ymv[:, :]).then_inc(ymv_ready, 1)

            def X(i):
                x_stats(i)
                split(i, 0)
                for t in range(NT):
                    threshold(i, t)
                    if t + 1 < NT:
                        split(i, t + 1)
                    denominators(i, t)
                    if t > 0:
                        residual(i, t - 1)
                residual(i, NT - 1)

            def low_parts(i):
                for n, u in enumerate((("q", 0), ("q", 1), ("k", 0), ("k", 1))):
                    dve.wait_ge(part_hi, at(i, 4, n + 1))
                    nc.vector.scalar_tensor_tensor(parts[:, n % 2, 1, :], fr_bank(u)[:, :], cv("b" + u[0], n % 2),
                                                   parts[:, n % 2, 0, :].bitcast(F32), ALU.add, ALU.subtract)\
                      .then_inc(fr_sem(u), 1)

            def maxima(i, g, h, t):
                u = ("s", g, h, t)
                fr_written(dve, i, u)
                nc.vector.tensor_reduce(nmax[:, g % 2, 4 * h + t:4 * h + t + 1], fr_bank(u)[:, :], AX.X, ALU.max,
                                        negate=True).then_inc(fr_sem(u), 1)

            def normalise(i, g):
                u = ("ot", g)
                fr_written(dve, i, u)
                o = fr_bank(u)[:, :].rearrange("p (t h c) -> p t h c", t=NT, c=VC)
                step(nc.vector.reciprocal(rz[:, :, :], o[:, :, :, D]))
                settle(i)
                nc.vector.tensor_tensor(on[:, :, 4 * D * g:4 * D * (g + 1)].rearrange("p t (h d) -> p t h d", d=D),
                                        o[:, :, :, 0:D], rz[:, :, :].unsqueeze(3).to_broadcast((P, NT, 4, D)),
                                        ALU.mult).then_inc(fr_sem(u), 1)

            def z_rows(i, t):
                u = ("wo", t)
                fr_written(dve, i, u)
                if t > 1:
                    dve.wait_ge(res_ready, at(i, NT, t - 1))
                nc.vector.tensor_tensor(z[:, t % 2, :], fr_bank(u)[:, 0:DM], yb[:, t, :], ALU.add)\
                  .then_inc(fr_sem(u), 1)
                fr_read(dve, i, u)
                dve.wait_ge(zr_ready, at(i, NT, t))
                stats(i, z[:, t % 2, :], zstat[:, :], zmv[:, :]).then_inc(zmv_ready, 1)

            def gate(i, t):
                u = ("gate", t)
                fr_written(dve, i, u)
                nc.vector.tensor_tensor(logits[:, bass.ds(i * (NT * E) + t * E, E)], fr_bank(u)[:, 0:E], gb_b[:, :],
                                        ALU.add).then_inc(fr_sem(u), 1)

            def F(i):
                low_parts(i)
                for h in range(4):
                    for t in range(NT):
                        maxima(i, 0, h, t)
                for g in range(G):
                    if g + 1 < G:
                        for t in range(NT):
                            for h in range(4):
                                maxima(i, g + 1, h, t)
                    normalise(i, g)
                for t in range(NT + 1):
                    if t < NT:
                        z_rows(i, t)
                    if t > 0:
                        gate(i, t - 1)

            with dve.Fori(0, B) as i:
                X(i)
                F(i)
            assert steps[1] == STEPS_V, steps

        @block.gpsimd
        def _(pool):
            gp = nc.gpsimd
            gp.memset(qs[:, :, :].bitcast(F32), 0.0)
            gp.memset(ks[:, :, :].bitcast(F32), 0.0).then_inc(p_set, 1)
            gp.memset(mhalf[:, :], -0.5)
            gp.memset(v32[:, :, :, :], 0.0).then_inc(p_set, 1)
            pool.wait_ge(p_set, 2)
            gp.memset(ks[4 * D:4 * D + 1, :, :].bitcast(F32), 1.0).then_inc(p_set, 1)
            pool.wait_ge(p_set, 3)
            gp.memset(v32[:, :, :, D:D + 1], 1.0).then_inc(zeroed, 1)
            pool.wait_ge(consts_ready, 2)
            pool.wait_ge(zeroed, 2)

            steps = [0]

            def hold():
                pool.sem_inc(p_gate, 1)

            def settle(i, ins):
                steps[0] += 1
                ins.then_inc(p_step, 1)
                pool.wait_ge(p_step, at(i, STEPS_P, steps[0]))
                hold()

            def inv_std(i, o, var, tmp):
                settle(i, gp.tensor_scalar(tmp, var, EPS, None, ALU.add))
                return gp.tensor_tensor(o, tmp, mhalf[:, 0:tmp.shape[1]], ALU.pow)

            def x_factors(i):
                pool.wait_ge(xmv_ready, at(i, 1, 1))
                hold()
                settle(i, inv_std(i, xr[:, :, 0], xmv[:, :, 1], yv[:, 0:NT]))
                settle(i, gp.tensor_tensor(yv[:, 0:NT], xmv[:, :, 0], xr[:, :, 0], ALU.mult))
                gp.tensor_scalar(xr[:, :, 1], yv[:, 0:NT], -1.0, None, ALU.mult).then_inc(xr_ready, NT)

            def y_factors(i, t):
                pool.wait_ge(ymv_ready, at(i, NT, t + 1))
                if t > 1:
                    pool.wait_ge(yn_ready, at(i, NT, t - 1))
                hold()
                r = yr[:, t % 2, :]
                settle(i, inv_std(i, r[:, 0:1], ymv[:, 1:2], yv[:, 0:1]))
                settle(i, gp.tensor_scalar(yv[:, 1:2], ymv[:, 1:2], r[:, 0:1], r[:, 0:1], ALU.mult, ALU.mult))
                settle(i, inv_std(i, yv[:, 2:3], yv[:, 1:2], yv[:, 3:4]))
                settle(i, gp.tensor_tensor(r[:, 1:2], r[:, 0:1], yv[:, 2:3], ALU.mult))
                gp.tensor_scalar(r[:, 2:4], r[:, 0:2], ymv[:, 0:1], -1.0, ALU.mult, ALU.mult).then_inc(yr_ready, 1)

            def z_factors(i, t):
                pool.wait_ge(zmv_ready, at(i, NT, t + 1))
                if t > 1:
                    pool.wait_ge(zn_ready, at(i, NT, t - 1))
                hold()
                settle(i, inv_std(i, zr[:, t % 2, 0:1], zmv[:, 1:2], yv[:, 0:1]))
                gp.tensor_scalar(zr[:, t % 2, 1:2], zmv[:, 0:1], zr[:, t % 2, 0:1], -1.0, ALU.mult, ALU.mult)\
                  .then_inc(zr_ready, 1)

            def add_bias(i, t):
                xs_read(pool, i, ("sc", t, 1))
                if t > 1:
                    pool.wait_ge(mask_done, at(i, NT, t - 1))
                hold()
                gp.tensor_tensor(s[:, t % 2, :, :], sraw[:, :].rearrange("p (h c) -> p h c", c=CK),
                                 bias_m[:, bass.ds(i * CK, CK)].unsqueeze(1).to_broadcast((P, H, CK)), ALU.add)\
                  .then_inc(s_ready, 1)

            def shift(i, t):
                pool.wait_ge(mx_ready, at(i, NT, t + 1))
                pool.wait_ge(s_ready, at(i, NT, t + 1))
                if t > 1:
                    pool.wait_ge(rden_ready, at(i, NT, t - 1))
                gp.tensor_tensor(e[:, t % 2, :, :], s[:, t % 2, :, :],
                                 mx[:, t % 2, :].unsqueeze(2).to_broadcast((P, H, CK)), ALU.subtract)\
                  .then_inc(d_ready, 1)

            def keep_top(i, t):
                pool.wait_ge(mask_done, at(i, NT, t + 1))
                pool.wait_ge(e_ready, at(i, NT, t + 1))
                gp.tensor_tensor(m[:, t % 2, :, :], m[:, t % 2, :, :], e[:, t % 2, :, :], ALU.mult)\
                  .then_inc(em_ready, 1)

            def weights(i, t):
                pool.wait_ge(rden_ready, at(i, NT, t + 1))
                gp.tensor_tensor(m[:, t % 2, :, :], m[:, t % 2, :, :],
                                 rden[:, t % 2, :].unsqueeze(2).to_broadcast((P, H, CK)), ALU.mult)\
                  .then_inc(p_ready, 1)

            def y_bias(i, t):
                pool.wait_ge(y_ready, at(i, NT, t + 1))
                gp.tensor_tensor(yb[:, t, :], y[:, t % 2, :], bo_b[:, :], ALU.add).then_inc(yb_ready, 1)

            def X(i):
                x_factors(i)
                add_bias(i, 0)
                shift(i, 0)
                add_bias(i, 1)
                for t in range(NT):
                    keep_top(i, t)
                    if t + 1 < NT:
                        shift(i, t + 1)
                    weights(i, t)
                    if t > 0:
                        y_factors(i, t - 1)
                        y_bias(i, t - 1)
                    if t + 2 < NT:
                        add_bias(i, t + 2)
                y_factors(i, NT - 1)
                y_bias(i, NT - 1)

            def store_rows(i, t):
                fr_read(pool, i, ("wo", t))
                pool.wait_ge(rows_stored[t % 2], at(i, 8 * NT, 16 * (t // 2)))
                gp.tensor_tensor(row[:, t % 2, DM:2 * DM], x1[:, t, :], z[:, t % 2, :], ALU.add)\
                  .then_inc(res_ready, 1)

            with pool.Fori(0, B) as i:
                X(i)
                for t in range(NT):
                    z_factors(i, t)
                    store_rows(i, t)
            assert steps[0] == STEPS_P, steps

        attn_space.close()
        block_ctx.close()

        dcon = sb("dcon", [P, NDCON])
        oh = sb("oh", [P, TILES, E])
        ow = sb("ow", [P, TILES, E])
        best = sb("best", [P, TILES])
        tot = sb("tot", [P, TILES, E])
        pre = sb("pre", [P, 2, TILES, E])
        need = sb("need", [P, E, TILES])
        cnt = sb("cnt", [P, E])
        cum = sb("cum", [P, 3, E])
        base = sb("base", [P, E])
        slot = sb("slot", [P, TILES])
        slot_u = sb("slot_u", [P, TILES], U32)
        tok_u = sb("tok_u", [P, TILES], U32)
        past = sb("past", [P, ETILES, E])
        ex = sb("ex", [P, ETILES])
        keep = sb("keep", [P, ETILES])
        wix = sb("wix", [P, ETILES])
        rec = sb("rec", [P, ETILES, 2], U32)

        gid = sb("gid", [P, 2, 1], U32)
        sid = sb("sid", [P, 2, 1], U32)
        wid = sb("wid", [P, 2, 2], U32)
        rows = sb("rows", [P, 2, 2 * DM])
        znT2 = sb("znT2", [P, 2, KT, P])
        w1s = sb("w1s", [P, 2, W1COLS])
        w2s = sb("w2s", [P, 2, FT, DM])
        b2s = sb("b2s", [P, 2, DM])
        mid = sb("mid", [P, 2, FT, P])
        resb = sb("resb", [P, 2, DM])
        ot = sb("ot", [P, 2, DM])

        def dc(name):
            a, n = DCON[name]
            return dcon[:, a:a + n]

        def freed(eng, signal, j, per):
            if not isinstance(j, int) or j > 0:
                eng.wait_ge(signal, reads(j, per, 0))

        def tiles(eng, step):
            full = (ETILES - 2) // 2
            for q in range(2):
                step(0, q, True)
            with eng.Fori(1, full) as j:
                step(j, 0, True)
                step(j, 1, True)
            for n in range(2 * full, ETILES):
                step(n // 2, n % 2, n + 2 < ETILES)

        block = ctx.enter_context(nc.Block())

        @block.sync
        def _(sp):
            sp.dma_start(dcon[:, :], dcon_in).then_inc(dcon_loaded, 16)
            sp.wait_ge(rec_ready, 2)
            sp.dma_start(widx_d.rearrange("n p c -> p n c"), rec[:, :, :]).then_inc(rec_set, 16)
            sp.wait_ge(rec_set, 16)
            sp.wait_ge(tokens_set, 16 * TILES)

            def ids(j, q, more):
                n = j * 2 + q
                freed(sp, rows_in[q], j, 16)
                sp.dma_start(gid[:, q, :], token_d[bass.ds(n * P, P), :]).then_inc(gid_loaded[q], 16)
                freed(sp, w1_in[q], j, 16)
                freed(sp, w2_in[q], j, 16)
                freed(sp, b2_in[q], j, 16)
                sp.dma_start(wid[:, q, :], widx_d[bass.ds(n, 1)].rearrange("o p c -> (o p) c"))\
                  .then_inc(wid_loaded[q], 16)
                freed(sp, scattered[q], j, 16)
                sp.dma_start(sid[:, q, :], token_d[bass.ds(n * P, P), :]).then_inc(sid_loaded[q], 16)

            tiles(sp, ids)
            for q in range(2):
                sp.wait_ge(scattered[q], 16 * ((ETILES + 1 - q) // 2))

        @block.vector
        def _(dve):
            count = [0]

            def settle(ins):
                count[0] += 1
                ins.then_inc(d_step, 1)
                dve.wait_ge(d_step, count[0])

            lg = logits[:, :].rearrange("p (t e) -> p t e", e=E)
            v = nc.vector
            dve.wait_ge(dcon_loaded, 16)
            settle(v.tensor_reduce(best[:, :], lg, AX.X, ALU.max))
            settle(v.tensor_tensor(oh[:, :, :], lg, best[:, :].unsqueeze(2).to_broadcast((P, TILES, E)), ALU.is_ge))
            settle(v.tensor_tensor(ow[:, :, :], oh[:, :, :], dc("order").unsqueeze(1).to_broadcast((P, TILES, E)),
                                   ALU.mult))
            settle(v.tensor_reduce(best[:, :], ow[:, :, :], AX.X, ALU.max))
            v.tensor_tensor(oh[:, :, :], ow[:, :, :], best[:, :].unsqueeze(2).to_broadcast((P, TILES, E)),
                            ALU.is_equal).then_inc(oh_ready, 1)
            dve.wait_ge(count_full, 1)
            settle(v.tensor_copy(tot[:, :, :].rearrange("p t e -> p (t e)"), ob[:, 0:TILES * E]))
            settle(v.tensor_copy(pre[:, 0, :, :], tot[:, :, :]))
            a, step = 0, 1
            while step < TILES:
                v.tensor_copy(pre[:, 1 - a, 0:step, :], pre[:, a, 0:step, :])
                settle(v.tensor_tensor(pre[:, 1 - a, step:, :], pre[:, a, step:, :], pre[:, a, 0:TILES - step, :],
                                       ALU.add))
                a, step = 1 - a, 2 * step
            settle(v.tensor_copy(cnt[:, :], pre[:, a, TILES - 1, :]))
            settle(v.tensor_tensor(need[:, :, :], cnt[:, :].unsqueeze(2).to_broadcast((P, E, TILES)),
                                   dc("steps").unsqueeze(1).to_broadcast((P, E, TILES)), ALU.is_gt))
            settle(v.tensor_reduce(cum[:, 0, :], need[:, :, :], AX.X, ALU.add))
            settle(v.tensor_copy(cum[:, 1, :], cum[:, 0, :]))
            c, step = 1, 1
            while step < E:
                v.tensor_copy(cum[:, 3 - c, 0:step], cum[:, c, 0:step])
                settle(v.tensor_tensor(cum[:, 3 - c, step:], cum[:, c, step:], cum[:, c, 0:E - step], ALU.add))
                c, step = 3 - c, 2 * step
            settle(v.tensor_tensor(base[:, :], cum[:, c, :], cum[:, 0, :], ALU.subtract))
            settle(v.tensor_scalar(base[:, :], base[:, :], float(P), None, ALU.mult))
            settle(v.tensor_tensor(ow[:, :, :], pre[:, a, :, :], tot[:, :, :], ALU.subtract))
            settle(v.tensor_tensor(tot[:, :, :], ow[:, :, :], base[:, :].unsqueeze(1).to_broadcast((P, TILES, E)),
                                   ALU.add))
            settle(v.tensor_tensor(ow[:, :, :].rearrange("p t e -> p (t e)"), xt[:, 0:TILES * E],
                                   tot[:, :, :].rearrange("p t e -> p (t e)"), ALU.add))
            settle(v.tensor_tensor(tot[:, :, :], ow[:, :, :], oh[:, :, :], ALU.mult))
            settle(v.tensor_reduce(slot[:, :], tot[:, :, :], AX.X, ALU.add))
            v.tensor_copy(tok_u[:, :], dc("token")).then_inc(slots_ready, 1)
            v.tensor_copy(slot_u[:, :], slot[:, :]).then_inc(slots_ready, 1)
            settle(v.tensor_tensor(past[:, :, :], dc("tile").unsqueeze(2).to_broadcast((P, ETILES, E)),
                                   cum[:, c, :].unsqueeze(1).to_broadcast((P, ETILES, E)), ALU.is_ge))
            settle(v.tensor_reduce(wix[:, :], past[:, :, :], AX.X, ALU.add))
            v.memset(keep[:, 0:2], 0.0)
            settle(v.tensor_scalar(ex[:, :], wix[:, :], float(E - 1), None, ALU.min))
            v.tensor_copy(rec[:, :, 1], ex[:, :]).then_inc(rec_ready, 1)
            settle(v.tensor_tensor(keep[:, 2:], ex[:, 2:], ex[:, 0:ETILES - 2], ALU.is_equal))
            settle(v.scalar_tensor_tensor(wix[:, :], keep[:, :], float(E), ex[:, :], ALU.mult, ALU.add))
            settle(v.tensor_scalar(wix[:, :], wix[:, :], float(P), dc("part"), ALU.mult, ALU.add))
            v.tensor_copy(rec[:, :, 0], wix[:, :]).then_inc(rec_ready, 1)

            def tile(j, q, more):
                dve.wait_ge(rows_in[q], reads(j, 16, 16))
                dve.wait_ge(b2_in[q], reads(j, 16, 16))
                freed(dve, ot_ready[q], j, 1)
                v.tensor_tensor(resb[:, q, :], rows[:, q, DM:2 * DM], b2s[:, q, :], ALU.add)\
                 .then_inc(resb_ready[q], 1)
                dve.wait_ge(l1_full[q], reads(j, 2, 2))
                for f in range(FT // 2, FT):
                    o = EH[2 * q + 1]
                    c0 = (f - FT // 2) * P
                    ins = v.tensor_scalar(mid[:, q, f, :], o[:, c0:c0 + P], w1s[:, q, KT * FF + f:KT * FF + f + 1],
                                          0.0, ALU.add, ALU.max)
                ins.then_inc(mid_dve[q], 1)
                dve.wait_ge(l2_full[q], reads(j, 1, 1))
                dve.wait_ge(resb_ready[q], reads(j, 1, 1))
                freed(dve, scattered[q], j, 16)
                v.tensor_tensor(ot[:, q, :], EO[q][:, 0:DM], resb[:, q, :], ALU.add).then_inc(ot_ready[q], 1)

            tiles(dve, tile)

        @block.tensor
        def _(pe):
            pe.wait_ge(oh_ready, 1)
            pe.matmul(xt[:, 0:TILES * E], dc("before"), oh[:, :, :].rearrange("p t e -> p (t e)"))
            pe.matmul(ob[:, 0:TILES * E], dc("ones"), oh[:, :, :].rearrange("p t e -> p (t e)"))\
              .then_inc(count_full, 1)

            def turn(j, q):
                pe.wait_ge(rows_in[q], reads(j, 16, 16))
                for k in range(KT):
                    ins = pe.transpose(ET[q][:, k * P:(k + 1) * P], rows[:, q, k * P:(k + 1) * P], ident[:, :])
                ins.then_inc(turned[q], 1)

            def tile(j, q, more, last=False):
                pe.wait_ge(turned_out[q], reads(j, 1, 1))
                pe.wait_ge(w1_in[q], reads(j, 16, 16))
                for half in range(2):
                    for f in range(FT // 2):
                        ff = half * (FT // 2) + f
                        for k in range(KT):
                            ins = pe.matmul(EH[2 * q + half][:, f * P:(f + 1) * P],
                                            w1s[:, q, k * FF + ff * P:k * FF + (ff + 1) * P], znT2[:, q, k, :],
                                            start=(k == 0), stop=(k == KT - 1))
                    ins.then_inc(l1_full[q], 1)
                if not last:
                    turn(j + q, 1 - q)
                pe.wait_ge(w2_in[q], reads(j, 16, 16))
                pe.wait_ge(mid_act[q], reads(j, 1, 1))
                pe.wait_ge(mid_dve[q], reads(j, 1, 1))
                freed(pe, ot_ready[q], j, 1)
                for f in range(FT):
                    ins = pe.matmul(EO[q][:, 0:DM], mid[:, q, f, :], w2s[:, q, f, :], start=(f == 0), stop=(f == FT - 1))
                ins.then_inc(l2_full[q], 1)

            pe.wait_ge(slots_ready, 2)
            turn(0, 0)
            tiles(pe, lambda j, q, more: tile(j, q, more, isinstance(j, int) and 2 * j + q == ETILES - 1))

        @block.scalar
        def _(act):
            def turned_to(j, q):
                act.wait_ge(turned[q], reads(j, 1, 1))
                for k in range(KT):
                    ins = act.activation(znT2[:, q, k, :], ET[q][:, k * P:(k + 1) * P], ACT.Identity,
                                         scale=cv("ln2_g", k), bias=cv("ln2_b", k))
                ins.then_inc(turned_out[q], 1)

            def tile(j, q, more):
                act.wait_ge(l1_full[q], reads(j, 2, 1))
                for f in range(FT // 2):
                    ins = act.activation(mid[:, q, f, :], EH[2 * q][:, f * P:(f + 1) * P], ACT.Relu,
                                         bias=w1s[:, q, KT * FF + f:KT * FF + f + 1])
                ins.then_inc(mid_act[q], 1)
                if more or not isinstance(j, int) or 2 * j + q + 1 < ETILES:
                    turned_to(j + q, 1 - q)

            turned_to(0, 0)
            tiles(act, tile)

        @block.gpsimd
        def _(pool):
            gp = nc.gpsimd

            def gather(dst, src, index, signal, bound=None):
                pool.sem_inc(p_gate, 1)
                gp.indirect_dma_start(dst, None, src, bass.IndirectOffsetOnAxis(index, 0), bounds_check=bound,
                                      oob_is_err=False).then_inc(signal, 16)

            pool.wait_ge(slots_ready, 2)
            for t in range(TILES):
                gp.indirect_dma_start(token_d, bass.IndirectOffsetOnAxis(slot_u[:, t:t + 1], 0), tok_u[:, t:t + 1],
                                      None, bounds_check=SLOTS - 1, oob_is_err=False).then_inc(tokens_set, 16)
                pool.wait_ge(tokens_set, 16 * (t + 1))

            def fetch_rows(j, q):
                pool.wait_ge(gid_loaded[q], reads(j, 16, 16))
                gather(rows[:, q, :], rows_d, gid[:, q, 0:1], rows_in[q], TOK)
                pool.wait_ge(wid_loaded[q], reads(j, 16, 16))
                gather(b2s[:, q, :], b2, wid[:, q, 1:2], b2_in[q], E - 1)

            def fetch_w1(j, q):
                gather(w1s[:, q, :], w1b, wid[:, q, 0:1], w1_in[q], E * P - 1)

            def fetch_w2(j, q):
                gather(w2s[:, q, :, :].rearrange("p f d -> p (f d)"), w2t, wid[:, q, 0:1], w2_in[q], E * P - 1)

            for q in range(2):
                fetch_rows(0, q)
                fetch_w1(0, q)
                fetch_w2(0, q)

            def tile(j, q, more):
                if more:
                    pool.wait_ge(turned[q], reads(j, 1, 1))
                    pool.wait_ge(resb_ready[q], reads(j, 1, 1))
                    fetch_rows(j + 1, q)
                    pool.wait_ge(l1_full[q], reads(j, 2, 2))
                    pool.wait_ge(mid_act[q], reads(j, 1, 1))
                    pool.wait_ge(mid_dve[q], reads(j, 1, 1))
                    fetch_w1(j + 1, q)
                    pool.wait_ge(l2_full[q], reads(j, 1, 1))
                    fetch_w2(j + 1, q)
                pool.wait_ge(ot_ready[q], reads(j, 1, 1))
                pool.wait_ge(sid_loaded[q], reads(j, 16, 16))
                freed(pool, scattered[1 - q], j + q, 16)
                pool.sem_inc(p_gate, 1)
                gp.indirect_dma_start(out, bass.IndirectOffsetOnAxis(sid[:, q, 0:1], 0), ot[:, q, :], None,
                                      bounds_check=TOK - 1, oob_is_err=False).then_inc(scattered[q], 16)

            tiles(pool, tile)
    return nc


def kernel(x, ctx_1024, mask_BxS2_bf1, L0_xattn_Wq, L0_xattn_Wk, L0_xattn_Wv, L0_xattn_Wo, L0_xattn_inv_temp,
           L0_ffn_ln1_g, L0_ffn_ln1_b, L0_ffn_ln2_g, L0_ffn_ln2_b, L0_ffn_wq, L0_ffn_bq, L0_ffn_wk, L0_ffn_bk,
           L0_ffn_wv, L0_ffn_bv, L0_ffn_wo, L0_ffn_bo, L0_ffn_gate_w, L0_ffn_gate_b, L0_ffn_w1, L0_ffn_b1,
           L0_ffn_w2, L0_ffn_b2):
    import numpy as np
    import concourse.bacc as bacc
    from concourse.bass_utils import run_bass_kernel_spmd

    def col(v):
        return v.reshape(-1, P).T

    temp = np.repeat(np.asarray(L0_xattn_inv_temp), CK)
    w1 = np.asarray(L0_ffn_w1).reshape(E, KT, P, FF).transpose(0, 2, 1, 3).reshape(E * P, KT * FF)
    b1 = np.asarray(L0_ffn_b1).reshape(E, FT, P).transpose(0, 2, 1).reshape(E * P, FT)
    w2 = np.asarray(L0_ffn_w2).reshape(E, FT, P, DM).transpose(0, 2, 1, 3).reshape(E * P, FT * DM)
    dcon = np.zeros((P, NDCON), np.float32)
    for name, value in (("before", np.triu(np.ones((P, P)), 1)), ("ones", 1.0), ("order", E - np.arange(E)),
                        ("steps", P * np.arange(TILES)), ("tile", np.arange(ETILES)),
                        ("part", np.arange(P)[:, None]),
                        ("token", P * np.arange(TILES)[None, :] + np.arange(P)[:, None])):
        a, n = DCON[name]
        dcon[:, a:a + n] = value
    arrays = {
        "x": x,
        "ctxT": np.asarray(ctx_1024).reshape(B * CK, DM).T,
        "maskb": np.asarray(mask_BxS2_bf1).reshape(1, B * CK).view(np.uint8),
        "wqT": np.asarray(L0_xattn_Wq).T, "wk": L0_xattn_Wk, "wv": L0_xattn_Wv, "wo": L0_xattn_Wo,
        "cols": np.concatenate([col(np.asarray(v)) for v in (temp, L0_ffn_ln1_g, L0_ffn_ln1_b, L0_ffn_bq, L0_ffn_bk,
                                                             L0_ffn_bv, L0_ffn_ln2_g, L0_ffn_ln2_b)], axis=1),
        "fwq": L0_ffn_wq, "fwk": L0_ffn_wk, "fwv": L0_ffn_wv, "fwo": L0_ffn_wo,
        "bo": np.asarray(L0_ffn_bo).reshape(1, DM), "gate_w": L0_ffn_gate_w,
        "gate_b": np.asarray(L0_ffn_gate_b).reshape(1, E),
        "w1b": np.concatenate([w1, b1], axis=1), "w2t": w2, "b2": L0_ffn_b2,
        "ident_in": np.eye(P, dtype=np.float32), "dcon_in": dcon,
    }
    arrays = {name: np.ascontiguousarray(a) for name, a in arrays.items()}
    nc = bacc.Bacc("TRN2", target_bir_lowering=False, num_devices=1)
    args = {name: nc.dram_tensor(name, a.shape, mybir.dt.from_np(a.dtype), kind="ExternalInput").ap()
            for name, a in arrays.items()}
    out = nc.dram_tensor("out", (TOK, DM), F32, kind="ExternalOutput").ap()
    program(nc, **args, out=out)
    result = run_bass_kernel_spmd(nc, [arrays], core_ids=[0])
    return result.results[0]["out"].reshape(B, S, DM)
```

```python
from contextlib import ExitStack

import concourse.bass as bass
from concourse import mybir

F32 = mybir.dt.float32
F32R = mybir.dt.float32r
I32 = mybir.dt.int32
U32 = mybir.dt.uint32
U8 = mybir.dt.uint8
ALU = mybir.AluOpType
ACT = mybir.ActivationFunctionType
AX = mybir.AxisListType

P = 128
B, S, DM = 8, 512, 256
KT = DM // P
H, CK = 16, 64
HP = H // 2
PAIRS = CK // 2
NH, D = 16, 16
NT = S // P
TILES = B * NT
TOK = B * S
E, FF = 8, 1024
FT = FF // P
ETILES = (TOK - E) // P + E
SLOTS = ETILES * P
G = NH // 4
VC = 32
EPS = 1e-5
BIG = 3.0e38
MASKED = 1.0e30

COLS = {}
for _name, _n in (("temp", HP), ("ln1_g", KT), ("ln1_b", KT), ("bq", KT), ("bk", KT), ("bv", KT),
                  ("ln2_g", KT), ("ln2_b", KT)):
    COLS[_name] = sum(n for _, n in COLS.values()), _n
NCOLS = sum(n for _, n in COLS.values())

STEP = (1.3, 1.3, 1.3, 0.6)
START = (34.0, 57.0, 80.0, 103.0)
LEAD = 3


def at_proj(name, n):
    return {"q": 1.8 * n, "k": 3.6 + 1.8 * n, "v": 7.2 + 0.9 * n}[name]


def at_s(g, n):
    return 19.0 + 0.65 * n if g == 0 else START[g - 1] + STEP[g - 1] * (n - LEAD) - 0.1


def at_st(g, n):
    return START[g] + STEP[g] * n


def at_pv(g, t):
    return at_st(g, 4 * t + 3) + (1.5 * STEP[g] if t < NT - 1 else 0.9)


def at_ct(g):
    return 30.0 if g == 0 else at_st(g - 1, 15) + 0.3


def at_ot(g):
    return at_pv(g, NT - 1) + 2.0


def at_tail(t):
    return 117.5 + 2.6 * t


SPLIT = (99.5, 114.2, 1.8, 27.0)
PIECE = ((101.0, 1.0), (118.0, 0.9), (3.5, 1.3), (30.0, 2.6))
MASK = (113.0, 0.3, 20.5, 61.5)
DENOM = (116.5, 5.0, 25.0, 66.0)
SCORE = (94.0, 98.2, 119.0, 20.0)
PT = (121.5, 10.3, 31.0, 72.0)
YTURN = (9.3, 19.0, 42.0, 84.0)
RESID = (127.5, 16.3, 38.0, 79.0)
SHIFT = (101.2, 120.0, 9.0, 30.0)

XS = [("M", c) for c in range(4)] + [("VW", c) for c in range(4)]
XS += [("sc", t, h) for t in (0, 1, 2) for h in range(2)]
XS += [("pT", 0, h) for h in range(2)] + [("pT", 1, h) for h in range(2)] + [("sc", 3, h) for h in range(2)]
XS += [("pT", t, h) for t in (2, 3) for h in range(2)]
XT = [("xn", 0), ("xn", 1), ("xn", 2), ("av", 0), ("yn", 0), ("av", 1), ("yn", 1), ("xn", 3),
      ("av", 2), ("yn", 2), ("av", 3), ("yn", 3)]
FR_AT = {(name, n): at_proj(name, n) for name, count in (("q", 2), ("k", 2), ("v", NT)) for n in range(count)}
for _g in range(G):
    FR_AT |= {("s", _g, n): at_s(_g, n) for n in range(16)} | {("st", _g, n): at_st(_g, n) for n in range(16)}
    FR_AT |= {("ct", _g): at_ct(_g), ("ot", _g): at_ot(_g)}
for _t in range(NT):
    FR_AT |= {("oT", _t): at_tail(_t), ("wo", _t): at_tail(_t) + 1.2, ("zT", _t): at_tail(_t) + 5.3,
              ("gate", _t): at_tail(_t) + 6.6}
FR = sorted(FR_AT, key=FR_AT.get)
XS_N = {u: n for n, u in enumerate(XS)}
XT_N = {u: n for n, u in enumerate(XT)}
FR_N = {u: n for n, u in enumerate(FR)}
NFR = 4
assert len(XS) % 2 == 0 and len(FR) % NFR == 0
NSLOT = 3


def weave(*streams):
    due = [[next(s, None), s] for s in streams]
    while any(place is not None for place, _ in due):
        first = min((d for d in due if d[0] is not None), key=lambda d: d[0])
        first[0] = next(first[1], None)


NCONST = 12
VX_EARLY, VX, VF = 14, 37, 8
PX_EARLY, PX, PF = 3, 27, 8
W1COLS = KT * FF + FT

DCON = {}
for _name, _n in (("before", P), ("ones", P), ("order", E), ("steps", TILES), ("starts", ETILES + 1), ("tile", ETILES), ("row", P), ("part", 1),
                  ("token", TILES)):
    DCON[_name] = sum(n for _, n in DCON.values()), _n
NDCON = sum(n for _, n in DCON.values())

def reads(j, per, count):
    return j * per + count


def at(i, per, count):
    return i * per + (count + 1)


def program(nc, x, ctxT, maskb, wqT, wk, wv, wo, cols, fwq, fwk, fwv, fwo, bo, gate_w, gate_b,
            w1b, w2t, b2, ident_in, dcon_in, out):
    ctx = ExitStack()
    with ctx:
        started = []

        def sb(name, shape, dt=F32):
            return ctx.enter_context(nc.sbuf_tensor(name, shape, dt))

        def bank(name):
            return ctx.enter_context(nc.psum_tensor(name, [P, 512], F32))

        def sem(name):
            return ctx.enter_context(nc.semaphore(name))

        def lsem(name):
            started.append(sem(name))
            return started[-1]

        def dram(name, shape, dt=F32):
            return nc.dram_tensor(name, shape, dt, kind="Internal").ap()

        kT_d = dram("kT_d", (HP, P, B * CK))
        vT_d = dram("vT_d", (HP, P, B * CK))
        parts_d = dram("parts_d", (4, NH * D, S))
        xy_d = dram("xy_d", (TOK, 2 * DM))
        rows_d = dram("rows_d", (TOK + 1, 2 * DM))

        ident = sb("ident", [P, P])
        col = sb("col", [P, NCOLS])
        bias_m = sb("bias_m", [P, B * CK])
        mask_u = sb("mask_u", [P, B * CK], U8)
        bo_b = sb("bo_b", [P, DM])
        gb_b = sb("gb_b", [P, E])
        wqT_s = sb("wqT_s", [P, HP, DM])
        wo_s = sb("wo_s", [P, HP, DM])
        fw = {n: sb("f" + n, [P, KT, DM]) for n in ("q", "k", "v", "o")}
        gw = sb("gw", [P, KT, E])
        logits = sb("logits", [P, TILES * E])
        zrow = sb("zrow", [NT * 4, P])

        def cv(name, n):
            return col[:, COLS[name][0] + n:COLS[name][0] + n + 1]

        attn_space = ExitStack()

        def sa(name, shape, dt=F32):
            return attn_space.enter_context(nc.sbuf_tensor(name, shape, dt))

        kbd = sa("kbd", [P, HP, P])
        vbd = sa("vbd", [P, HP, P])
        M = sa("M", [P, KT, H * CK])
        VW = sa("VW", [P, HP, DM])
        xb = sa("xb", [P, NT, DM])
        xstat = sa("xstat", [P, NT, 6])
        xmv = sa("xmv", [P, NT, 2])
        xr = sa("xr", [P, NT, 2])
        xn = sa("xn", [P, NT, DM])
        xnT = sa("xnT", [P, KT, P])
        sraw = sa("sraw", [P, H * CK])
        s = sa("s", [P, 2, H, CK])
        e = sa("e", [P, H, CK])
        m = sa("m", [P, H, CK])
        hi = sa("hi", [P, H, PAIRS])
        lo = sa("lo", [P, 2, H, PAIRS])
        nhi = sa("nhi", [P, H, PAIRS])
        mx = sa("mx", [P, 2, H])
        lo17 = sa("lo17", [P, H, 17])
        nh17 = sa("nh17", [P, H, 17])
        merged = sa("merged", [P, H, 17])
        thr = sa("thr", [P, H])
        sums = sa("sums", [P, 2, H])
        den = sa("den", [P, H])
        rden = sa("rden", [P, 2, H])
        pT = sa("pT", [P, HP * P])
        xy = sa("xy", [P, 2, 2 * DM])
        ystat = sa("ystat", [P, 6])
        ymv = sa("ymv", [P, 2])
        yv = sa("yv", [P, 4])
        mhalf = sa("mhalf", [P, NT])
        yr = sa("yr", [P, 2, 4])
        yn = sa("yn", [P, DM])
        hnT = sa("hnT", [P, KT, S])

        parts = sa("parts", [P, 2, 2, S], F32R)
        qs = sa("qs", [P, 4 * NSLOT, S], F32R)
        ks = sa("ks", [P, 4 * NSLOT, S], F32R)
        v32 = sa("v32", [P, NT, NH, VC])
        nmax = sa("nmax", [P, 2, 4 * NT])
        cT = sa("cT", [NT * 4, P], F32R)
        pt = sa("pt", [P, 2, 4, S])
        osb = sa("osb", [P, S])
        rz = sa("rz", [P, NT, 4])
        on = sa("on", [P, NT, DM])
        oT = sa("oT", [P, KT, P])
        z = sa("z", [P, 2, DM])
        zstat = sa("zstat", [P, 6])
        zv = sa("zv", [P, 1])
        zmv = sa("zmv", [P, 2])
        zr = sa("zr", [P, 2, 2])
        xyf = sa("xyf", [P, 2, 2 * DM])
        row = sa("row", [P, 2, 2 * DM])
        znT = sa("znT", [P, KT, P])

        pre_ctx = sraw[:, :].rearrange("p (k n) -> p k n", k=KT)
        pre_w = [s[:, :, :, :].rearrange("p a h c -> p (a h c)").rearrange("p (k n) -> p k n", k=KT), M[:, :, :]]
        pre_out = [[VW[:, 4 * r + 2 * n:4 * r + 2 * n + 2, :].rearrange("p h d -> p (h d)") for n in range(2)]
                   for r in range(2)]

        xs = [bank(f"xs{n}") for n in range(2)]
        xt = bank("xt")
        fr = [bank(f"fr{n}") for n in range(NFR)]
        ob = bank("ob")
        ET, EH, EO = fr[0:2], [xs[0], xs[1], fr[2], fr[3]], [xt, ob]

        const_loaded, proj_loaded = sem("const_loaded"), sem("proj_loaded")
        zeroed, consts_ready = sem("zeroed"), sem("consts_ready")
        kv_full, p_set = sem("kv_full"), sem("p_set")
        kv_copied = [sem("k_copied"), sem("v_copied")]
        kv_stored = [[sem(f"k_stored{n}") for n in range(2)], [sem(f"v_stored{n}") for n in range(2)]]
        kbd_loaded, x_loaded = lsem("kbd_loaded"), lsem("x_loaded")
        vx_step, vf_step, v_gate = lsem("vx_step"), lsem("vf_step"), sem("v_gate")
        sp_gate = sem("sp_gate")
        px_step, pf_step, p_gate = lsem("px_step"), lsem("pf_step"), sem("p_gate")
        xs_full, xt_full, fr_full, o_full = lsem("xs_full"), lsem("xt_full"), lsem("fr_full"), lsem("o_full")
        xs_emptied = [lsem(f"xs_emptied{n}") for n in range(2)]
        xt_emptied, o_emptied = lsem("xt_emptied"), lsem("o_emptied")
        fr_emptied = [lsem(f"fr_emptied{n}") for n in range(NFR)]
        xr_ready, xn_ready = lsem("xr_ready"), lsem("xn_ready")
        s_ready, split_done, neg_done, mask_done = (lsem("s_ready"), lsem("split_done"), lsem("neg_done"),
                                                    lsem("mask_done"))
        d_ready, e_ready, em_ready, rden_ready, p_ready = (lsem("d_ready"), lsem("e_ready"), lsem("em_ready"),
                                                           lsem("rden_ready"), lsem("p_ready"))
        mx_ready, xmv_ready, ymv_ready, zmv_ready = lsem("mx_ready"), lsem("xmv_ready"), lsem("ymv_ready"), lsem("zmv_ready")
        yr_ready, y_ready, yn_ready, yb_ready = lsem("yr_ready"), lsem("y_ready"), lsem("yn_ready"), lsem("yb_ready")
        part_hi, parts_stored = lsem("part_hi"), [lsem(f"parts_stored{n}") for n in range(2)]
        stack_loaded = [lsem(f"stack_loaded{n}") for n in range(NSLOT)]
        xy_stored, xyf_loaded = [[lsem(f"{name}{n}") for n in range(2)] for name in ("xy_stored", "xyf_loaded")]
        c_loaded = lsem("c_loaded")
        zr_ready, zn_ready, res_ready = lsem("zr_ready"), lsem("zn_ready"), lsem("res_ready")
        rows_stored, scratch_set = [lsem(f"rows_stored{n}") for n in range(2)], sem("scratch_set")

        dcon_loaded = sem("dcon_loaded")
        d_step, oh_ready, count_full, counts_read = sem("d_step"), sem("oh_ready"), sem("count_full"), sem("counts_read")
        rows_ready, tokens_full, rec_ready = sem("rows_ready"), sem("tokens_full"), sem("rec_ready")

        def pair(name):
            return [sem(f"{name}{n}") for n in range(2)]

        gix_ready = pair("gix_ready")
        rows_in, w1_in, w2_in, b2_in = pair("rows_in"), pair("w1_in"), pair("w2_in"), pair("b2_in")
        turned, turned_out = pair("turned"), pair("turned_out")
        l1_full, l2_full = pair("l1_full"), pair("l2_full")
        mid_act, mid_dve = pair("mid_act"), pair("mid_dve")
        resb_ready, ot_ready, scattered = pair("resb_ready"), pair("ot_ready"), pair("scattered")

        def xs_written(eng, i, u):
            eng.wait_ge(xs_full, at(i, len(XS), XS_N[u] + 1))

        def xs_read(eng, i, u):
            n = XS_N[u]
            eng.wait_ge(xs_emptied[n % 2], at(i, len(XS) // 2, n // 2 + 1))

        def xt_written(eng, i, u):
            eng.wait_ge(xt_full, at(i, len(XT), XT_N[u] + 1))

        def xt_read(eng, i, u):
            eng.wait_ge(xt_emptied, at(i, len(XT), XT_N[u] + 1))

        def fr_written(eng, i, u):
            eng.wait_ge(fr_full, at(i, len(FR), FR_N[u] + 1))

        def fr_read(eng, i, u):
            n = FR_N[u]
            eng.wait_ge(fr_emptied[n % NFR], at(i, len(FR) // NFR, n // NFR + 1))

        def fr_bank(u):
            return fr[FR_N[u] % NFR]

        def fr_sem(u):
            return fr_emptied[FR_N[u] % NFR]

        with nc.Block() as start:
            def raise_to_one(eng, share):
                for q in started[share::5]:
                    eng.sem_inc(q, 1)

            @start.sync
            def _(sp):
                raise_to_one(sp, 0)

            @start.tensor
            def _(pe):
                raise_to_one(pe, 1)

            @start.scalar
            def _(act):
                raise_to_one(act, 2)

            @start.vector
            def _(dve):
                raise_to_one(dve, 3)

            @start.gpsimd
            def _(pool):
                raise_to_one(pool, 4)

        block_ctx = ExitStack()
        block = block_ctx.enter_context(nc.Block())

        def iterations(eng, F, x_early, x_late):
            def run(f=None, late=None, early=None):
                streams = []
                for part in (f and F(*f), late and x_late(*late), early and x_early(*early)):
                    streams += part if isinstance(part, (list, tuple)) else [part] if part else []
                weave(*streams)

            run(early=(0,))
            run(late=(0,), early=(1,))
            with eng.Fori(0, B - 2) as i:
                run(f=(i,), late=(i + 1, i), early=(i + 2,))
            run(f=(B - 2,), late=(B - 1, B - 2))
            run(f=(B - 1,))

        @block.sync
        def _(sp):
            def cload(dst, src):
                sp.dma_start(dst, src).then_inc(const_loaded, 16)

            sp.dma_start(pre_ctx, ctxT.rearrange("(k p) n -> p k n", p=P)).then_inc(proj_loaded, 16)
            sp.dma_start(pre_w[0], wk.rearrange("(k p) n -> p k n", p=P)).then_inc(proj_loaded, 16)
            sp.dma_start(pre_w[1], wv.rearrange("(k p) n -> p k n", p=P)).then_inc(proj_loaded, 16)
            cload(col[:, :], cols)
            cload(ident[:, :], ident_in)
            cload(mask_u[:, :], maskb.to_broadcast((P, B * CK)))
            cload(wqT_s[:, :, :], wqT.rearrange("(h p) n -> p h n", p=P))
            cload(wo_s[:, :, :], wo.rearrange("(h p) n -> p h n", p=P))
            for name, w in (("q", fwq), ("k", fwk), ("v", fwv), ("o", fwo)):
                cload(fw[name][:, :, :], w.rearrange("(k p) n -> p k n", p=P))
            cload(gw[:, :, :], gate_w.rearrange("(k p) n -> p k n", p=P))
            cload(bo_b[:, :], bo.to_broadcast((P, DM)))
            cload(gb_b[:, :], gate_b.to_broadcast((P, E)))
            for n in range(2 * HP):
                sp.wait_ge(kv_copied[n % 2], n // 2 + 1)
                sp.dma_start((kT_d, vT_d)[n % 2][n // 2], pre_out[(n // 2) % 2][n % 2])\
                  .then_inc(kv_stored[n % 2][(n // 2) % 2], 16)
            for q in kv_stored[0] + kv_stored[1]:
                sp.wait_ge(q, 16 * HP // 2)
            sp.wait_ge(zeroed, 2)
            sp.dma_start(rows_d[TOK:TOK + 1, :].rearrange("o (a c) -> (o a) c", c=P), zrow[0:4, :])\
              .then_inc(scratch_set, 16)

            def hold():
                sp.sem_inc(sp_gate, 1)

            def x_early(b):
                yield 70.0
                if not isinstance(b, int) or b > 0:
                    sp.wait_ge(xs_full, at(b, len(XS), XS_N["VW", 3] + 1 - len(XS)))
                    hold()
                for dst, src in ((kbd, kT_d), (vbd, vT_d)):
                    for hh in range(2):
                        r = slice(CK * hh, CK * hh + CK)
                        sp.dma_start(dst[r, :, r],
                                     src[:, r, bass.ds(b * CK, CK)].rearrange("h p s -> p h s"))\
                          .then_inc(kbd_loaded, 16)
                yield RESID[3] + 1.5
                if not isinstance(b, int) or b > 0:
                    sp.wait_ge(xt_emptied, at(b, len(XT), XT_N["av", 3] + 1 - len(XT)))
                    hold()
                sp.dma_start(xb[:, :, :], x[bass.ds(b, 1)].rearrange("a (t p) d -> p (a t) d", p=P))\
                  .then_inc(x_loaded, 16)

            def x_late(b, i=None):
                for t in range(NT):
                    yield (5.0, 22.0, 44.0, 86.0)[t]
                    sp.wait_ge(yb_ready, at(b, NT, t + 1))
                    hold()
                    sp.dma_start(xy_d[bass.ds(b * S + t * P, P), :], xy[:, t % 2, :]).then_inc(xy_stored[t % 2], 16)

            def store_parts(i):
                for n, u in enumerate((("q", 0), ("q", 1), ("k", 0), ("k", 1))):
                    yield FR_AT[u] + 2.8
                    base, mt = 2 * (n // 2), n % 2
                    fr_read(sp, i, u)
                    for j in range(2):
                        sp.dma_start(parts_d[base + j, mt * P:(mt + 1) * P, :],
                                     parts[:, n % 2, j, :].bitcast(F32)).then_inc(parts_stored[n % 2], 16)
                for q in parts_stored:
                    sp.wait_ge(q, at(i, 64, 64))
                    hold()

            def load_stack(i, g, place):
                slot = g % NSLOT
                sl = slice(4 * slot, 4 * slot + 4)
                yield place
                if g >= NSLOT:
                    fr_written(sp, i, ("st", g - NSLOT, 15))
                for dst, order in ((qs, (0, 0, 1, 1)), (ks, (2, 3, 2, 3))):
                    for r, part in enumerate(order):
                        src = parts_d[part, 64 * g:64 * g + 64, :].rearrange("(h d) s -> d h s", d=D)
                        sp.dma_start(dst[D * r:D * r + D, sl, :].bitcast(F32), src)\
                          .then_inc(stack_loaded[slot], 16)
                sp.dma_start(qs[4 * D:4 * D + 1, sl, :].bitcast(F32).rearrange("o h (t c) -> o (h t) c", c=P),
                             zrow[:, :]).then_inc(stack_loaded[slot], 16)

            def load_max(i):
                for g in range(G):
                    yield at_ct(g) + 0.6
                    sl = slice(4 * (g % NSLOT), 4 * (g % NSLOT) + 4)
                    fr_read(sp, i, ("ct", g))
                    sp.dma_start(qs[4 * D:4 * D + 1, sl, :].bitcast(F32).rearrange("o h (t c) -> o (h t) c", c=P),
                                 cT[:, :].bitcast(F32)).then_inc(c_loaded, 16)

            def load_xy(i):
                for t in range(NT):
                    yield at_tail(max(t - 1, 0)) - 6.0 if t < 2 else at_tail(t - 2) + 4.4
                    for q in xy_stored:
                        sp.wait_ge(q, at(i, 32, 32))
                        hold()
                    sp.wait_ge(res_ready, at(i, NT, max(t - 1, 0)))
                    hold()
                    sp.dma_start(xyf[:, t % 2, :], xy_d[bass.ds(i * S + t * P, P), :]).then_inc(xyf_loaded[t % 2], 16)

            def store_rows(i):
                for t in range(NT):
                    yield at_tail(t) + 5.4
                    sp.wait_ge(res_ready, at(i, NT, t + 1))
                    hold()
                    sp.wait_ge(zn_ready, at(i, NT, t + 1))
                    hold()
                    sp.dma_start(rows_d[bass.ds(i * S + t * P, P), :], row[:, t % 2, :]).then_inc(rows_stored[t % 2], 16)

            def F(i):
                return (store_parts(i), load_stack(i, 0, 9.5), load_stack(i, 1, 13.0), load_stack(i, 2, 17.0),
                        load_stack(i, 3, at_st(0, 15) + 1.0), load_max(i), load_xy(i), store_rows(i))

            iterations(sp, F, x_early, x_late)
            for q in rows_stored:
                sp.wait_ge(q, 16 * TILES // 2 + 1)
            sp.wait_ge(scratch_set, 16)

        @block.tensor
        def _(pe):
            def mm(o, l, r, first=True, last=True):
                return pe.matmul(o, l, r, start=first, stop=last)

            def tr(o, src):
                return pe.transpose(o, src, ident[:, :])

            pe.wait_ge(proj_loaded, 48)
            for n in range(2 * HP):
                if n >= NFR:
                    pe.wait_ge(kv_copied[n % 2], (n - NFR) // 2 + 1)
                hp = n // 2
                for k in range(KT):
                    ins = mm(fr[n % NFR][:, :], pre_w[n % 2][:, k, hp * P:(hp + 1) * P], pre_ctx[:, k, :],
                             k == 0, k == KT - 1)
                ins.then_inc(kv_full, 1)
            pe.wait_ge(const_loaded, 16 * NCONST)
            for q in kv_copied:
                pe.wait_ge(q, HP)
            pe.wait_ge(zeroed, 2)

            def xs_slot(i, u):
                n = XS_N[u]
                pe.wait_ge(xs_emptied[n % 2], at(i, len(XS) // 2, n // 2))
                return xs[n % 2]

            def xt_slot(i, u):
                pe.wait_ge(xt_emptied, at(i, len(XT), XT_N[u]))
                return xt

            def fr_slot(i, u):
                n = FR_N[u]
                pe.wait_ge(fr_emptied[n % NFR], at(i, len(FR) // NFR, n // NFR))
                return fr[n % NFR]

            def fold(i):
                for c in range(4):
                    yield 87.0 + 0.85 * c
                    if c == 0:
                        pe.wait_ge(kbd_loaded, at(i, 64, 64))
                    o = xs_slot(i, ("M", c))
                    mt, half = c // 2, c % 2
                    for j in range(4):
                        hp = 4 * half + j
                        ins = mm(o[:, j * P:(j + 1) * P], wqT_s[:, hp, mt * P:(mt + 1) * P], kbd[:, hp, :])
                    ins.then_inc(xs_full, 1)
                for c in range(4):
                    yield 90.5 + 0.85 * c
                    o = xs_slot(i, ("VW", c))
                    for j in range(2):
                        hp = 2 * c + j
                        ins = mm(o[:, j * DM:(j + 1) * DM], vbd[:, hp, :], wo_s[:, hp, :])
                    ins.then_inc(xs_full, 1)

            def x_scores(i, t):
                yield SCORE[t]
                pe.wait_ge(xn_ready, at(i, NT, t + 1))
                o = xt_slot(i, ("xn", t))
                for k in range(KT):
                    ins = tr(o[:, k * P:(k + 1) * P], xn[:, t, k * P:(k + 1) * P])
                ins.then_inc(xt_full, 1)
                for half in range(2):
                    yield SCORE[t] + 1.0 + 1.8 * half
                    if half == 0:
                        xt_read(pe, i, ("xn", t))
                    o = xs_slot(i, ("sc", t, half))
                    if t == 0 and half == 0:
                        xs_read(pe, i, ("M", 3))
                    for k in range(KT):
                        ins = mm(o[:, :], xnT[:, k, :], M[:, k, half * 512:(half + 1) * 512], k == 0, k == KT - 1)
                    ins.then_inc(xs_full, 1)

            def x_pT(i, t):
                for half in range(2):
                    yield PT[t] + 0.9 * half
                    if half == 0:
                        pe.wait_ge(p_ready, at(i, NT, t + 1))
                    o = xs_slot(i, ("pT", t, half))
                    for j in range(4):
                        h0 = 8 * half + 2 * j
                        ins = tr(o[:, j * P:(j + 1) * P], m[:, h0:h0 + 2, :].rearrange("p h c -> p (h c)"))
                    ins.then_inc(xs_full, 1)
                yield PT[t] + 2.2
                o = xt_slot(i, ("av", t))
                xs_read(pe, i, ("pT", t, 1))
                for hp in range(HP):
                    ins = mm(o[:, 0:DM], pT[:, hp * P:(hp + 1) * P], VW[:, hp, :], hp == 0, hp == HP - 1)
                ins.then_inc(xt_full, 1)

            def y_turn(i, t):
                yield YTURN[t]
                pe.wait_ge(yn_ready, at(i, NT, t + 1))
                o = xt_slot(i, ("yn", t))
                for k in range(KT):
                    ins = tr(o[:, k * P:(k + 1) * P], yn[:, k * P:(k + 1) * P])
                ins.then_inc(xt_full, 1)

            def x_early(b):
                yield from fold(b)
                yield from x_scores(b, 0)
                yield from x_scores(b, 1)
                yield from x_scores(b, 2)
                yield from x_pT(b, 0)

            def x_late(b, i=None):
                yield from y_turn(b, 0)
                yield from x_pT(b, 1)
                yield from y_turn(b, 1)
                yield from x_scores(b, 3)
                for t in (2, 3):
                    yield from x_pT(b, t)
                    yield from y_turn(b, t)

            def projections(i):
                for name in ("q", "k"):
                    for mt in range(2):
                        yield at_proj(name, mt)
                        if name == "q" and mt == 0:
                            xt_read(pe, i, ("yn", NT - 1))
                        o = fr_slot(i, (name, mt))
                        for k in range(KT):
                            ins = mm(o[:, :], fw[name][:, k, mt * P:(mt + 1) * P], hnT[:, k, :], k == 0, k == KT - 1)
                        ins.then_inc(fr_full, 1)
                for t in range(NT):
                    yield at_proj("v", t)
                    o = fr_slot(i, ("v", t))
                    for k in range(KT):
                        ins = mm(o[:, 0:DM], hnT[:, k, t * P:(t + 1) * P], fw["v"][:, k, :], k == 0, k == KT - 1)
                    ins.then_inc(fr_full, 1)

            def first_pass(i, g):
                for n in range(16):
                    t, h = n // 4, n % 4
                    yield at_s(g, n)
                    slot = g % NSLOT
                    if n == 0:
                        per = 144 * len(range(slot, G, NSLOT))
                        pe.wait_ge(stack_loaded[slot], at(i, per, 144 * (g // NSLOT + 1)))
                    o = fr_slot(i, ("s", g, n))
                    mm(o[:, :], qs[:, 4 * slot + h, t * P:(t + 1) * P], ks[:, 4 * slot + h, :]).then_inc(fr_full, 1)
                yield at_ct(g)
                fr_read(pe, i, ("s", g, 15))
                o = fr_slot(i, ("ct", g))
                tr(o[0:4 * NT, 0:P], nmax[:, g % 2, :]).then_inc(fr_full, 1)

            def second_pass(i, g):
                for n in range(16):
                    t, h = n // 4, n % 4
                    yield at_st(g, n)
                    sl = 4 * (g % NSLOT) + h
                    o = fr_slot(i, ("st", g, n))
                    if n == 0:
                        pe.wait_ge(c_loaded, at(i, 16 * G, 16 * (g + 1)))
                    mm(o[:, :], ks[:, sl, t * P:(t + 1) * P], qs[:, sl, :]).then_inc(fr_full, 1)

            def pv(i, g):
                for t in range(NT):
                    yield at_pv(g, t)
                    fr_read(pe, i, ("st", g, 4 * t + 3))
                    if t == 0:
                        pe.wait_ge(o_emptied, at(i, G, g))
                    for h in range(4):
                        ins = pe.matmul(ob[VC * h:VC * h + VC, :], v32[:, t, 4 * g + h, :], pt[:, t % 2, h, :],
                                        start=(t == 0), stop=(t == NT - 1))
                    ins.then_inc(o_full, 1)
                yield at_ot(g)
                pe.wait_ge(o_emptied, at(i, G, g + 1))
                o = fr_slot(i, ("ot", g))
                for t in range(NT):
                    ins = tr(o[:, t * P:(t + 1) * P], osb[:, t * P:(t + 1) * P])
                ins.then_inc(fr_full, 1)

            def out_proj(i, t):
                yield FR_AT["oT", t]
                if t == 0:
                    fr_read(pe, i, ("ot", G - 1))
                o = fr_slot(i, ("oT", t))
                for k in range(KT):
                    ins = tr(o[:, k * P:(k + 1) * P], on[:, t, k * P:(k + 1) * P])
                ins.then_inc(fr_full, 1)
                yield FR_AT["wo", t]
                o = fr_slot(i, ("wo", t))
                fr_read(pe, i, ("oT", t))
                for k in range(KT):
                    ins = mm(o[:, 0:DM], oT[:, k, :], fw["o"][:, k, :], k == 0, k == KT - 1)
                ins.then_inc(fr_full, 1)

            def gate(i, t):
                yield FR_AT["zT", t]
                pe.wait_ge(zn_ready, at(i, NT, t + 1))
                o = fr_slot(i, ("zT", t))
                for k in range(KT):
                    ins = tr(o[:, k * P:(k + 1) * P], row[:, t % 2, k * P:(k + 1) * P])
                ins.then_inc(fr_full, 1)
                yield FR_AT["gate", t]
                o = fr_slot(i, ("gate", t))
                fr_read(pe, i, ("zT", t))
                for k in range(KT):
                    ins = mm(o[:, 0:E], znT[:, k, :], gw[:, k, :], k == 0, k == KT - 1)
                ins.then_inc(fr_full, 1)

            def F(i):
                return ([projections(i)] + [part(i, g) for g in range(G) for part in (first_pass, second_pass, pv)]
                        + [part(i, t) for t in range(NT) for part in (out_proj, gate)])

            iterations(pe, F, x_early, x_late)

        @block.scalar
        def _(act):
            def copy(o, src, scale=1.0, bias=None):
                if bias is None:
                    return act.activation(o, src, ACT.Copy, scale=scale)
                return act.activation(o, src, ACT.Identity, scale=scale, bias=bias)

            act.wait_ge(consts_ready, 1)
            for n in range(HP):
                act.wait_ge(kv_full, 2 * n + 1)
                if n >= 2:
                    act.wait_ge(kv_stored[0][n % 2], 16 * (n // 2))
                act.activation(pre_out[n % 2][0], fr[(2 * n) % NFR][:, :], ACT.Copy, scale=cv("temp", n))\
                   .then_inc(kv_copied[0], 1)
            act.wait_ge(consts_ready, 2)

            def fold_out(i):
                for c in range(4):
                    u = ("M", c)
                    yield 87.6 + 0.85 * c
                    xs_written(act, i, u)
                    copy(M[:, c // 2, (c % 2) * 512:(c % 2 + 1) * 512], xs[XS_N[u] % 2][:, :])\
                        .then_inc(xs_emptied[XS_N[u] % 2], 1)
                for c in range(4):
                    u = ("VW", c)
                    yield 91.1 + 0.85 * c
                    xs_written(act, i, u)
                    copy(VW[:, 2 * c:2 * c + 2, :].rearrange("p h d -> p (h d)"), xs[XS_N[u] % 2][:, :])\
                        .then_inc(xs_emptied[XS_N[u] % 2], 1)

            def x_norm(i):
                for t in range(NT):
                    yield 92.0 + 0.01 * t if t < 2 else 97.0 + t
                    act.wait_ge(xr_ready, at(i, NT, t + 1))
                    copy(xn[:, t, :], xb[:, t, :], xr[:, t, 0:1], xr[:, t, 1:2]).then_inc(xn_ready, 1)

            def scores_out(i, t):
                yield SCORE[t] + 0.5
                xt_written(act, i, ("xn", t))
                copy(xnT[:, :, :].rearrange("p k c -> p (k c)"), xt[:, 0:DM]).then_inc(xt_emptied, 1)
                for half in range(2):
                    u = ("sc", t, half)
                    yield SCORE[t] + 1.9 + 1.8 * half
                    xs_written(act, i, u)
                    if t > 0 and half == 0:
                        act.wait_ge(s_ready, at(i, NT, t))
                    copy(sraw[:, half * 512:(half + 1) * 512], xs[XS_N[u] % 2][:, :])\
                        .then_inc(xs_emptied[XS_N[u] % 2], 1)

            def negate(i, t):
                yield SPLIT[t] + 0.8
                act.wait_ge(split_done, at(i, NT, t + 1))
                if t > 0:
                    act.wait_ge(mask_done, at(i, NT, t))
                act.activation(nhi[:, :, :].rearrange("p h c -> p (h c)"),
                               hi[:, :, :].rearrange("p h c -> p (h c)"), ACT.Copy, scale=-1.0)\
                   .then_inc(neg_done, 1)

            def exponent(i, t):
                yield SHIFT[t] + 2.3
                act.wait_ge(d_ready, at(i, NT, t + 1))
                ev = e[:, :, :].rearrange("p h c -> p (h c)")
                act.activation(ev, ev, ACT.Exp).then_inc(e_ready, 1)

            def pT_out(i, t):
                for half in range(2):
                    u = ("pT", t, half)
                    yield PT[t] + 0.5 + 0.9 * half
                    xs_written(act, i, u)
                    copy(pT[:, half * 512:(half + 1) * 512], xs[XS_N[u] % 2][:, :])\
                        .then_inc(xs_emptied[XS_N[u] % 2], 1)

            def y_norm(i, t):
                yield RESID[t] + 3.0 if t > 0 else 2.0
                act.wait_ge(yr_ready, at(i, NT, t + 1))
                r = yr[:, t % 2, :]
                x1 = xy[:, t % 2, 0:DM]
                copy(xy[:, t % 2, DM:2 * DM], x1, r[:, 0:1], r[:, 2:3]).then_inc(y_ready, 1)
                if t > 0:
                    xt_written(act, i, ("yn", t - 1))
                copy(yn[:, :], x1, r[:, 1:2], r[:, 3:4]).then_inc(yn_ready, 1)

            def y_out(b, t, i):
                yield YTURN[t] + 0.5
                if t == 0 and i is not None:
                    fr_written(act, i, ("v", NT - 1))
                xt_written(act, b, ("yn", t))
                for k in range(KT):
                    ins = copy(hnT[:, k, t * P:(t + 1) * P], xt[:, k * P:(k + 1) * P], cv("ln1_g", k), cv("ln1_b", k))
                ins.then_inc(xt_emptied, 1)

            def x_early(b):
                return [fold_out(b), x_norm(b), scores_out(b, 0), scores_out(b, 1), scores_out(b, 2), negate(b, 0),
                        exponent(b, 0), negate(b, 1), exponent(b, 1), pT_out(b, 0)]

            def x_late(b, i=None):
                return ([part(b, t) for t in (2, 3) for part in (negate, exponent)]
                        + [part(b, t) for t in (1, 2, 3) for part in (pT_out,)] + [scores_out(b, 3)]
                        + [y_norm(b, t) for t in range(NT)] + [y_out(b, t, i) for t in range(NT)])

            def heads_out(i):
                for n, u in enumerate((("q", 0), ("q", 1), ("k", 0), ("k", 1))):
                    yield FR_AT[u] + 1.7
                    fr_written(act, i, u)
                    if n >= 2:
                        act.wait_ge(parts_stored[n % 2], at(i, 64, 32))
                    copy(parts[:, n % 2, 0, :], fr_bank(u)[:, :], 1.0, cv("b" + u[0], n % 2))\
                        .then_inc(part_hi, 1)
                for t in range(NT):
                    u = ("v", t)
                    yield FR_AT[u] + 0.9
                    fr_written(act, i, u)
                    copy(v32[:, t, :, 0:D], fr_bank(u)[:, 0:DM].rearrange("p (h d) -> p h d", d=D))\
                        .then_inc(fr_sem(u), 1)

            def exps(i, g):
                for n in range(16):
                    t, h = n // 4, n % 4
                    u = ("st", g, n)
                    yield FR_AT[u] + 0.3
                    if h == 0:
                        act.wait_ge(o_full, at(i, G * NT, max(g * NT + t - 1, 0)))
                    fr_written(act, i, u)
                    act.activation(pt[:, t % 2, h, :], fr_bank(u)[:, :], ACT.Exp, scale=D ** -0.5)\
                       .then_inc(fr_sem(u), 1)

            def max_out(i, g):
                u = ("ct", g)
                yield at_ct(g) + 0.2
                fr_written(act, i, u)
                if g > 0:
                    act.wait_ge(c_loaded, at(i, 16 * G, 16 * g))
                copy(cT[:, :], fr_bank(u)[0:4 * NT, 0:P]).then_inc(fr_sem(u), 1)

            def o_out(i, g):
                yield at_pv(g, NT - 1) + 0.9
                act.wait_ge(o_full, at(i, G * NT, NT * (g + 1)))
                if g > 0:
                    fr_written(act, i, ("ot", g - 1))
                copy(osb[:, :], ob[:, :]).then_inc(o_emptied, 1)

            def tail_out(i, t):
                u = ("oT", t)
                yield FR_AT[u] + 0.4
                fr_written(act, i, u)
                for k in range(KT):
                    ins = copy(oT[:, k, :], fr_bank(u)[:, k * P:(k + 1) * P], 1.0, cv("bv", k))
                ins.then_inc(fr_sem(u), 1)

            def z_norm(i, t):
                yield at_tail(t) + 4.3
                act.wait_ge(zr_ready, at(i, NT, t + 1))
                act.wait_ge(rows_stored[t % 2], at(i, 8 * NT, 16 * (t // 2)))
                copy(row[:, t % 2, 0:DM], z[:, t % 2, :], zr[:, t % 2, 0:1], zr[:, t % 2, 1:2]).then_inc(zn_ready, 1)
                u = ("zT", t)
                yield FR_AT[u] + 0.4
                fr_written(act, i, u)
                for k in range(KT):
                    ins = copy(znT[:, k, :], fr_bank(u)[:, k * P:(k + 1) * P], cv("ln2_g", k), cv("ln2_b", k))
                ins.then_inc(fr_sem(u), 1)

            def F(i):
                return ([heads_out(i)] + [part(i, g) for g in range(G) for part in (exps, max_out, o_out)]
                        + [part(i, t) for t in range(NT) for part in (tail_out, z_norm)])

            iterations(act, F, x_early, x_late)

        @block.vector
        def _(dve):
            steps = {"xe": 0, "xl": VX_EARLY, "f": 0}

            def step(part, i, ins):
                signal, per = (vf_step, VF) if part == "f" else (vx_step, VX)
                steps[part] += 1
                ins.then_inc(signal, 1)
                dve.wait_ge(signal, at(i, per, steps[part]))

            nc.vector.memset(zrow[:, :], 0.0)
            nc.vector.memset(kbd[:, :, :], 0.0)
            nc.vector.memset(vbd[:, :, :], 0.0)
            nc.vector.memset(lo17[:, :, 0:1], BIG)
            nc.vector.memset(nh17[:, :, 16:17], -BIG).then_inc(zeroed, 1)
            dve.wait_ge(const_loaded, 16 * NCONST)
            t0 = COLS["temp"]
            nc.vector.tensor_scalar(col[:, t0[0]:t0[0] + t0[1]], col[:, t0[0]:t0[0] + t0[1]], CK ** -0.5, None,
                                    ALU.mult).then_inc(consts_ready, 1)
            nc.vector.tensor_scalar(bias_m[:, :], mask_u[:, :], 1.0, MASKED, ALU.subtract, ALU.mult)\
              .then_inc(consts_ready, 1)
            for n in range(HP):
                dve.wait_ge(kv_full, 2 * n + 2)
                if n >= 2:
                    dve.wait_ge(kv_stored[1][n % 2], 16 * (n // 2))
                nc.vector.tensor_copy(pre_out[n % 2][1], fr[(2 * n + 1) % NFR][:, :]).then_inc(kv_copied[1], 1)

            def x_stats(i):
                yield 88.0
                dve.wait_ge(x_loaded, at(i, 16, 16))
                for t in range(NT):
                    ins = nc.vector.bn_stats(xstat[:, t, :], xb[:, t, :])
                step("xe", i, ins)
                dve.wait_ge(xr_ready, at(i, NT, 0))
                dve.sem_inc(v_gate, 1)
                for t in range(NT):
                    ins = nc.vector.bn_aggr(xmv[:, t, :], xstat[:, t, :])
                ins.then_inc(xmv_ready, 1)

            def split(i, t, part):
                yield SPLIT[t]
                dve.wait_ge(s_ready, at(i, NT, t + 1))
                a, b = s[:, t % 2, :, 0:PAIRS], s[:, t % 2, :, PAIRS:CK]
                dve.wait_ge(neg_done, at(i, NT, t))
                nc.vector.tensor_tensor(hi[:, :, :], a, b, ALU.max).then_inc(split_done, 1)
                step(part, i, nc.vector.tensor_tensor(lo[:, t % 2, :, :], a, b, ALU.min))
                nc.vector.tensor_reduce(mx[:, t % 2, :], hi[:, :, :], AX.X, ALU.max).then_inc(mx_ready, 1)

            def threshold(i, t, part):
                lv, nv = lo[:, t % 2, :, :], nhi[:, :, :]
                first, apart = PIECE[t]
                for r in range(3):
                    for q in range(4):
                        yield first + apart * (4 * r + q)
                        if r == 0 and q == 0:
                            dve.wait_ge(neg_done, at(i, NT, t + 1))
                            dve.sem_inc(v_gate, 1)
                        for h in range(4 * q, 4 * q + 4):
                            if r == 0:
                                nc.vector.max(lo17[:, h, 1:9], lv[:, h, :])
                                ins = nc.vector.max(nh17[:, h, 0:8], nv[:, h, :])
                            elif r == 1:
                                nc.vector.match_replace(lv[:, h, :], lo17[:, h, 1:9], lv[:, h, :], -BIG)
                                ins = nc.vector.match_replace(nv[:, h, :], nh17[:, h, 0:8], nv[:, h, :], -BIG)
                            else:
                                nc.vector.max(lo17[:, h, 9:17], lv[:, h, :])
                                ins = nc.vector.max(nh17[:, h, 8:16], nv[:, h, :])
                    step(part, i, ins)
                    dve.sem_inc(v_gate, 1)

            def mask(i, t, part):
                yield MASK[t]
                step(part, i, nc.vector.scalar_tensor_tensor(merged[:, :, :], nh17[:, :, :], -1.0, lo17[:, :, :],
                                                                 ALU.mult, ALU.min))
                step(part, i, nc.vector.tensor_reduce(thr[:, :], merged[:, :, :], AX.X, ALU.max))
                if t > 0:
                    xs_written(dve, i, ("pT", t - 1, 1))
                else:
                    dve.wait_ge(xs_full, at(i, len(XS), 0))
                nc.vector.tensor_tensor(m[:, :, :], s[:, t % 2, :, :], thr[:, :].unsqueeze(2).to_broadcast((P, H, CK)),
                                        ALU.is_ge).then_inc(mask_done, 1)

            def denominators(i, t, part):
                yield DENOM[t]
                dve.wait_ge(e_ready, at(i, NT, t + 1))
                nc.vector.tensor_reduce(sums[:, 1, :], e[:, :, :], AX.X, ALU.add)
                dve.wait_ge(em_ready, at(i, NT, t + 1))
                step(part, i, nc.vector.tensor_reduce(sums[:, 0, :], m[:, :, :], AX.X, ALU.add))
                step(part, i, nc.vector.scalar_tensor_tensor(den[:, :], sums[:, 1, :], 1e-8, sums[:, 0, :],
                                                             ALU.mult, ALU.add))
                nc.vector.reciprocal(rden[:, t % 2, :], den[:, :]).then_inc(rden_ready, 1)

            def stats(part, i, src, st, mv):
                step(part, i, nc.vector.bn_stats(st, src))
                dve.sem_inc(v_gate, 1)
                return nc.vector.bn_aggr(mv, st)

            def residual(i, t, part):
                yield RESID[t]
                xt_written(dve, i, ("av", t))
                dve.wait_ge(xy_stored[t % 2], at(i, 32, 16 * (t // 2)))
                dve.wait_ge(yn_ready, at(i, NT, max(t - 1, 0)))
                nc.vector.tensor_tensor(xy[:, t % 2, 0:DM], xt[:, 0:DM], xb[:, t, :], ALU.add).then_inc(xt_emptied, 1)
                xt_read(dve, i, ("av", t))
                dve.wait_ge(yr_ready, at(i, NT, t))
                stats(part, i, xy[:, t % 2, 0:DM], ystat[:, :], ymv[:, :]).then_inc(ymv_ready, 1)

            def x_early(b):
                steps["xe"] = 0
                return [x_stats(b), split(b, 0, "xe"), threshold(b, 0, "xe"), mask(b, 0, "xe"),
                        denominators(b, 0, "xe"), split(b, 1, "xe"), threshold(b, 1, "xe"), residual(b, 0, "xe")]

            def x_late(b, i=None):
                steps["xl"] = VX_EARLY
                return ([mask(b, 1, "xl"), denominators(b, 1, "xl"), residual(b, 1, "xl")]
                        + [part(b, t, "xl") for t in (2, 3) for part in (split, threshold, mask, denominators, residual)])

            def low_parts(i):
                for n, u in enumerate((("q", 0), ("q", 1), ("k", 0), ("k", 1))):
                    yield FR_AT[u] + 2.2
                    dve.wait_ge(part_hi, at(i, 4, n + 1))
                    nc.vector.scalar_tensor_tensor(parts[:, n % 2, 1, :], fr_bank(u)[:, :], cv("b" + u[0], n % 2),
                                                   parts[:, n % 2, 0, :].bitcast(F32), ALU.add, ALU.subtract)\
                      .then_inc(fr_sem(u), 1)

            def maxima(i, g):
                for n in range(16):
                    t, h = n // 4, n % 4
                    u = ("s", g, n)
                    yield FR_AT[u] + 0.6
                    fr_written(dve, i, u)
                    nc.vector.tensor_reduce(nmax[:, g % 2, 4 * h + t:4 * h + t + 1], fr_bank(u)[:, :], AX.X, ALU.max,
                                            negate=True).then_inc(fr_sem(u), 1)

            def normalise(i, g):
                u = ("ot", g)
                yield FR_AT[u] + 0.6
                fr_written(dve, i, u)
                o = fr_bank(u)[:, :].rearrange("p (t h c) -> p t h c", t=NT, c=VC)
                step("f", i, nc.vector.reciprocal(rz[:, :, :], o[:, :, :, D]))
                nc.vector.tensor_tensor(on[:, :, 4 * D * g:4 * D * (g + 1)].rearrange("p t (h d) -> p t h d", d=D),
                                        o[:, :, :, 0:D], rz[:, :, :].unsqueeze(3).to_broadcast((P, NT, 4, D)),
                                        ALU.mult).then_inc(fr_sem(u), 1)

            def z_rows(i, t):
                u = ("wo", t)
                yield FR_AT[u] + 1.0
                fr_written(dve, i, u)
                dve.wait_ge(xyf_loaded[t % 2], at(i, 32, 16 * (t // 2) + 16))
                if t > 1:
                    dve.wait_ge(res_ready, at(i, NT, t - 1))
                nc.vector.tensor_tensor(z[:, t % 2, :], fr_bank(u)[:, 0:DM], xyf[:, t % 2, DM:2 * DM], ALU.add)\
                  .then_inc(fr_sem(u), 1)
                fr_read(dve, i, u)
                dve.wait_ge(zr_ready, at(i, NT, t))
                stats("f", i, z[:, t % 2, :], zstat[:, :], zmv[:, :]).then_inc(zmv_ready, 1)

            def gate(i, t):
                u = ("gate", t)
                yield FR_AT[u] + 0.6
                fr_written(dve, i, u)
                nc.vector.tensor_tensor(logits[:, bass.ds(i * (NT * E) + t * E, E)], fr_bank(u)[:, 0:E], gb_b[:, :],
                                        ALU.add).then_inc(fr_sem(u), 1)

            def F(i):
                steps["f"] = 0
                return ([low_parts(i)] + [part(i, g) for g in range(G) for part in (maxima, normalise)]
                        + [part(i, t) for t in range(NT) for part in (z_rows, gate)])

            iterations(dve, F, x_early, x_late)
            assert steps == {"xe": VX_EARLY, "xl": VX, "f": VF}, steps

        @block.gpsimd
        def _(pool):
            gp = nc.gpsimd
            gp.memset(qs[:, :, :].bitcast(F32), 0.0)
            gp.memset(ks[:, :, :].bitcast(F32), 0.0).then_inc(p_set, 1)
            gp.memset(mhalf[:, :], -0.5)
            gp.memset(v32[:, :, :, :], 0.0).then_inc(p_set, 1)
            pool.wait_ge(p_set, 2)
            gp.memset(ks[4 * D:4 * D + 1, :, :].bitcast(F32), 1.0).then_inc(p_set, 1)
            pool.wait_ge(p_set, 3)
            gp.memset(v32[:, :, :, D:D + 1], 1.0).then_inc(zeroed, 1)
            pool.wait_ge(consts_ready, 2)
            pool.wait_ge(zeroed, 2)

            steps = {"xe": 0, "xl": PX_EARLY, "f": 0}

            def hold():
                pool.sem_inc(p_gate, 1)

            def step(part, i, ins):
                signal, per = (pf_step, PF) if part == "f" else (px_step, PX)
                steps[part] += 1
                ins.then_inc(signal, 1)
                pool.wait_ge(signal, at(i, per, steps[part]))
                hold()

            def inv_std(part, i, o, var, tmp):
                step(part, i, gp.tensor_scalar(tmp, var, EPS, None, ALU.add))
                return gp.tensor_tensor(o, tmp, mhalf[:, 0:tmp.shape[1]], ALU.pow)

            def x_factors(i):
                yield 88.5
                pool.wait_ge(xmv_ready, at(i, 1, 1))
                hold()
                step("xe", i, inv_std("xe", i, xr[:, :, 0], xmv[:, :, 1], yv[:, 0:NT]))
                step("xe", i, gp.tensor_tensor(yv[:, 0:NT], xmv[:, :, 0], xr[:, :, 0], ALU.mult))
                gp.tensor_scalar(xr[:, :, 1], yv[:, 0:NT], -1.0, None, ALU.mult).then_inc(xr_ready, NT)

            def add_bias(i, t):
                yield SCORE[t] + 4.2
                xs_read(pool, i, ("sc", t, 1))
                if t > 1:
                    pool.wait_ge(mask_done, at(i, NT, t - 1))
                hold()
                gp.tensor_tensor(s[:, t % 2, :, :], sraw[:, :].rearrange("p (h c) -> p h c", c=CK),
                                 bias_m[:, bass.ds(i * CK, CK)].unsqueeze(1).to_broadcast((P, H, CK)), ALU.add)\
                  .then_inc(s_ready, 1)

            def shift(i, t):
                yield SHIFT[t]
                pool.wait_ge(mx_ready, at(i, NT, t + 1))
                pool.wait_ge(s_ready, at(i, NT, t + 1))
                pool.wait_ge(rden_ready, at(i, NT, t))
                gp.tensor_tensor(e[:, :, :], s[:, t % 2, :, :],
                                 mx[:, t % 2, :].unsqueeze(2).to_broadcast((P, H, CK)), ALU.subtract)\
                  .then_inc(d_ready, 1)

            def keep_top(i, t):
                yield MASK[t] + 0.9
                pool.wait_ge(mask_done, at(i, NT, t + 1))
                pool.wait_ge(e_ready, at(i, NT, t + 1))
                gp.tensor_tensor(m[:, :, :], m[:, :, :], e[:, :, :], ALU.mult).then_inc(em_ready, 1)

            def weights(i, t):
                yield DENOM[t] + 2.8
                pool.wait_ge(rden_ready, at(i, NT, t + 1))
                gp.tensor_tensor(m[:, :, :], m[:, :, :], rden[:, t % 2, :].unsqueeze(2).to_broadcast((P, H, CK)),
                                 ALU.mult).then_inc(p_ready, 1)

            def y_factors(i, t):
                yield RESID[t] + 1.0 if t > 0 else 0.1
                pool.wait_ge(ymv_ready, at(i, NT, t + 1))
                if t > 1:
                    pool.wait_ge(yn_ready, at(i, NT, t - 1))
                hold()
                r = yr[:, t % 2, :]
                step("xl", i, inv_std("xl", i, r[:, 0:1], ymv[:, 1:2], yv[:, 0:1]))
                step("xl", i, gp.tensor_scalar(yv[:, 1:2], ymv[:, 1:2], r[:, 0:1], r[:, 0:1], ALU.mult, ALU.mult))
                step("xl", i, inv_std("xl", i, yv[:, 2:3], yv[:, 1:2], yv[:, 3:4]))
                step("xl", i, gp.tensor_tensor(r[:, 1:2], r[:, 0:1], yv[:, 2:3], ALU.mult))
                gp.tensor_scalar(r[:, 2:4], r[:, 0:2], ymv[:, 0:1], -1.0, ALU.mult, ALU.mult).then_inc(yr_ready, 1)

            def y_bias(i, t):
                yield RESID[t] + 3.5 if t > 0 else 2.7
                pool.wait_ge(y_ready, at(i, NT, t + 1))
                yb = xy[:, t % 2, DM:2 * DM]
                gp.tensor_tensor(yb, yb, bo_b[:, :], ALU.add).then_inc(yb_ready, 1)

            def x_early(b):
                steps["xe"] = 0
                return [x_factors(b), add_bias(b, 0), add_bias(b, 1), add_bias(b, 2), shift(b, 0), shift(b, 1),
                        keep_top(b, 0), weights(b, 0)]

            def x_late(b, i=None):
                steps["xl"] = PX_EARLY
                return ([shift(b, 2), shift(b, 3), add_bias(b, 3)]
                        + [part(b, t) for t in (1, 2, 3) for part in (keep_top, weights)]
                        + [part(b, t) for t in range(NT) for part in (y_factors, y_bias)])

            def z_factors(i, t):
                yield FR_AT["wo", t] + 1.7
                pool.wait_ge(zmv_ready, at(i, NT, t + 1))
                if t > 1:
                    pool.wait_ge(zn_ready, at(i, NT, t - 1))
                hold()
                step("f", i, inv_std("f", i, zr[:, t % 2, 0:1], zmv[:, 1:2], zv[:, 0:1]))
                gp.tensor_scalar(zr[:, t % 2, 1:2], zmv[:, 0:1], zr[:, t % 2, 0:1], -1.0, ALU.mult, ALU.mult)\
                  .then_inc(zr_ready, 1)

            def residual_row(i, t):
                yield FR_AT["wo", t] + 2.8
                fr_read(pool, i, ("wo", t))
                pool.wait_ge(rows_stored[t % 2], at(i, 8 * NT, 16 * (t // 2)))
                pool.wait_ge(xyf_loaded[t % 2], at(i, 32, 16 * (t // 2) + 16))
                gp.tensor_tensor(row[:, t % 2, DM:2 * DM], xyf[:, t % 2, 0:DM], z[:, t % 2, :], ALU.add)\
                  .then_inc(res_ready, 1)

            def F(i):
                steps["f"] = 0
                return [part(i, t) for t in range(NT) for part in (z_factors, residual_row)]

            iterations(pool, F, x_early, x_late)
            assert steps == {"xe": PX_EARLY, "xl": PX, "f": PF}, steps

        attn_space.close()
        block_ctx.close()

        dcon = sb("dcon", [P, NDCON])
        oh = sb("oh", [P, TILES, E])
        ow = sb("ow", [P, TILES, E])
        best = sb("best", [P, TILES])
        tot = sb("tot", [P, TILES, E])
        pre = sb("pre", [P, 2, TILES, E])
        need = sb("need", [P, E, TILES])
        cnt = sb("cnt", [P, E])
        cum = sb("cum", [P, 3, E])
        base = sb("base", [P, E])
        slot = sb("slot", [P, TILES])
        passed = sb("passed", [P, TILES, ETILES + 1])
        at_tile = sb("at_tile", [P, TILES, ETILES])
        at_row = sb("at_row", [P, TILES, P])
        past = sb("past", [P, ETILES, E])
        keep = sb("keep", [P, ETILES])
        rec = sb("rec", [P, ETILES, 3])

        gix = sb("gix", [P, 2, 3], U32)
        sid = sb("sid", [P, 2, 1], U32)
        rows = sb("rows", [P, 2, 2 * DM])
        znT2 = sb("znT2", [P, 2, KT, P])
        w1s = sb("w1s", [P, 2, W1COLS])
        w2s = sb("w2s", [P, 2, FT, DM])
        b2s = sb("b2s", [P, 2, DM])
        mid = sb("mid", [P, 2, FT, P])
        resb = sb("resb", [P, 2, DM])
        ot = sb("ot", [P, 2, DM])

        def dc(name):
            a, n = DCON[name]
            return dcon[:, a:a + n]

        def freed(eng, signal, j, per):
            if not isinstance(j, int) or j > 0:
                eng.wait_ge(signal, reads(j, per, 0))

        def tiles(eng, step):
            full = (ETILES - 2) // 2
            for q in range(2):
                step(0, q, True)
            with eng.Fori(1, full) as j:
                step(j, 0, True)
                step(j, 1, True)
            for n in range(2 * full, ETILES):
                step(n // 2, n % 2, n + 2 < ETILES)

        block = ctx.enter_context(nc.Block())

        @block.sync
        def _(sp):
            sp.dma_start(dcon[:, :], dcon_in).then_inc(dcon_loaded, 16)

        @block.vector
        def _(dve):
            count = [0]

            def settle(ins):
                count[0] += 1
                ins.then_inc(d_step, 1)
                dve.wait_ge(d_step, count[0])

            lg = logits[:, :].rearrange("p (t e) -> p t e", e=E)
            v = nc.vector
            dve.wait_ge(dcon_loaded, 16)
            settle(v.tensor_reduce(best[:, :], lg, AX.X, ALU.max))
            settle(v.tensor_tensor(oh[:, :, :], lg, best[:, :].unsqueeze(2).to_broadcast((P, TILES, E)), ALU.is_ge))
            settle(v.tensor_tensor(ow[:, :, :], oh[:, :, :], dc("order").unsqueeze(1).to_broadcast((P, TILES, E)),
                                   ALU.mult))
            settle(v.tensor_reduce(best[:, :], ow[:, :, :], AX.X, ALU.max))
            v.tensor_tensor(oh[:, :, :], ow[:, :, :], best[:, :].unsqueeze(2).to_broadcast((P, TILES, E)),
                            ALU.is_equal).then_inc(oh_ready, 1)
            dve.wait_ge(count_full, 1)
            settle(v.tensor_copy(tot[:, :, :].rearrange("p t e -> p (t e)"), ob[:, 0:TILES * E]))
            settle(v.tensor_copy(pre[:, 0, :, :], tot[:, :, :]))
            a, step = 0, 1
            while step < TILES:
                v.tensor_copy(pre[:, 1 - a, 0:step, :], pre[:, a, 0:step, :])
                settle(v.tensor_tensor(pre[:, 1 - a, step:, :], pre[:, a, step:, :], pre[:, a, 0:TILES - step, :],
                                       ALU.add))
                a, step = 1 - a, 2 * step
            settle(v.tensor_copy(cnt[:, :], pre[:, a, TILES - 1, :]))
            settle(v.tensor_tensor(need[:, :, :], cnt[:, :].unsqueeze(2).to_broadcast((P, E, TILES)),
                                   dc("steps").unsqueeze(1).to_broadcast((P, E, TILES)), ALU.is_gt))
            settle(v.tensor_reduce(cum[:, 0, :], need[:, :, :], AX.X, ALU.add))
            settle(v.tensor_copy(cum[:, 1, :], cum[:, 0, :]))
            c, step = 1, 1
            while step < E:
                v.tensor_copy(cum[:, 3 - c, 0:step], cum[:, c, 0:step])
                settle(v.tensor_tensor(cum[:, 3 - c, step:], cum[:, c, step:], cum[:, c, 0:E - step], ALU.add))
                c, step = 3 - c, 2 * step
            settle(v.tensor_tensor(base[:, :], cum[:, c, :], cum[:, 0, :], ALU.subtract))
            settle(v.tensor_scalar(base[:, :], base[:, :], float(P), None, ALU.mult))
            settle(v.tensor_tensor(ow[:, :, :], pre[:, a, :, :], tot[:, :, :], ALU.subtract))
            settle(v.tensor_tensor(tot[:, :, :], ow[:, :, :], base[:, :].unsqueeze(1).to_broadcast((P, TILES, E)),
                                   ALU.add))
            settle(v.tensor_tensor(ow[:, :, :].rearrange("p t e -> p (t e)"), xt[:, 0:TILES * E],
                                   tot[:, :, :].rearrange("p t e -> p (t e)"), ALU.add))
            settle(v.tensor_tensor(tot[:, :, :], ow[:, :, :], oh[:, :, :], ALU.mult))
            settle(v.tensor_reduce(slot[:, :], tot[:, :, :], AX.X, ALU.add))
            settle(v.tensor_tensor(passed[:, :, :], slot[:, :].unsqueeze(2).to_broadcast((P, TILES, ETILES + 1)),
                                   dc("starts").unsqueeze(1).to_broadcast((P, TILES, ETILES + 1)), ALU.is_ge))
            settle(v.tensor_reduce(best[:, :], passed[:, :, :], AX.X, ALU.add))
            settle(v.scalar_tensor_tensor(best[:, :], best[:, :], -float(P), slot[:, :], ALU.mult, ALU.add))
            settle(v.tensor_scalar(best[:, :], best[:, :], float(P), None, ALU.add))
            settle(v.tensor_tensor(at_tile[:, :, :], passed[:, :, 0:ETILES], passed[:, :, 1:], ALU.subtract))
            settle(v.tensor_tensor(at_tile[:, :, :], at_tile[:, :, :],
                                   dc("token").unsqueeze(2).to_broadcast((P, TILES, ETILES)), ALU.mult))
            for t0 in range(0, TILES, 8):
                v.tensor_tensor(at_row[:, t0:t0 + 8, :], best[:, t0:t0 + 8].unsqueeze(2).to_broadcast((P, 8, P)),
                                dc("row").unsqueeze(1).to_broadcast((P, 8, P)), ALU.is_equal).then_inc(rows_ready, 1)
            ex, wix = rec[:, :, 2], rec[:, :, 1]
            settle(v.tensor_tensor(past[:, :, :], dc("tile").unsqueeze(2).to_broadcast((P, ETILES, E)),
                                   cum[:, c, :].unsqueeze(1).to_broadcast((P, ETILES, E)), ALU.is_ge))
            settle(v.tensor_reduce(ex, past[:, :, :], AX.X, ALU.add))
            v.memset(keep[:, 0:2], 0.0)
            settle(v.tensor_scalar(ex, ex, float(E - 1), None, ALU.min))
            settle(v.tensor_tensor(keep[:, 2:], rec[:, 2:, 2], rec[:, 0:ETILES - 2, 2], ALU.is_equal))
            settle(v.scalar_tensor_tensor(wix, keep[:, :], float(E), ex, ALU.mult, ALU.add))
            settle(v.tensor_scalar(wix, wix, float(P), dc("part"), ALU.mult, ALU.add))
            dve.wait_ge(tokens_full, 1)
            settle(v.tensor_scalar(rec[:, :, 0], EO[1][:, 0:ETILES], float(TOK), None, ALU.add))
            for q in range(2):
                v.tensor_scalar(gix[:, q, :], rec[:, q, :], 0.0, None, ALU.add).then_inc(gix_ready[q], 1)

            def tile(j, q, more):
                dve.wait_ge(rows_in[q], reads(j, 16, 16))
                dve.wait_ge(b2_in[q], reads(j, 16, 16))
                freed(dve, ot_ready[q], j, 2)
                v.tensor_tensor(resb[:, q, :], rows[:, q, DM:2 * DM], b2s[:, q, :], ALU.add)\
                 .then_inc(resb_ready[q], 1)
                dve.wait_ge(l1_full[q], reads(j, 2, 2))
                for f in range(FT // 2, FT):
                    o = EH[2 * q + 1]
                    c0 = (f - FT // 2) * P
                    ins = v.tensor_scalar(mid[:, q, f, :], o[:, c0:c0 + P], w1s[:, q, KT * FF + f:KT * FF + f + 1],
                                          0.0, ALU.add, ALU.max)
                ins.then_inc(mid_dve[q], 1)
                if more:
                    dve.wait_ge(w1_in[q], reads(j, 16, 16))
                    dve.wait_ge(w2_in[q], reads(j, 16, 16))
                    v.tensor_scalar(gix[:, q, :], rec[:, bass.ds(2 * j + q + 2, 1), :].rearrange("p a c -> p (a c)"),
                                    0.0, None, ALU.add).then_inc(gix_ready[q], 1)
                dve.wait_ge(l2_full[q], reads(j, 1, 1))
                dve.wait_ge(resb_ready[q], reads(j, 1, 1))
                freed(dve, scattered[q], j, 16)
                v.tensor_scalar(sid[:, q, :], rec[:, bass.ds(2 * j + q, 1), 0], 0.0, None, ALU.add)\
                 .then_inc(ot_ready[q], 1)
                v.tensor_tensor(ot[:, q, :], EO[q][:, 0:DM], resb[:, q, :], ALU.add).then_inc(ot_ready[q], 1)

            tiles(dve, tile)

        @block.tensor
        def _(pe):
            pe.wait_ge(oh_ready, 1)
            pe.matmul(xt[:, 0:TILES * E], dc("before"), oh[:, :, :].rearrange("p t e -> p (t e)"))
            pe.matmul(ob[:, 0:TILES * E], dc("ones"), oh[:, :, :].rearrange("p t e -> p (t e)"))\
              .then_inc(count_full, 1)

            def turn(j, q):
                pe.wait_ge(rows_in[q], reads(j, 16, 16))
                for k in range(KT):
                    ins = pe.transpose(ET[q][:, k * P:(k + 1) * P], rows[:, q, k * P:(k + 1) * P], ident[:, :])
                ins.then_inc(turned[q], 1)

            def tile(j, q, more, last=False):
                pe.wait_ge(turned_out[q], reads(j, 1, 1))
                pe.wait_ge(w1_in[q], reads(j, 16, 16))
                for half in range(2):
                    for f in range(FT // 2):
                        ff = half * (FT // 2) + f
                        for k in range(KT):
                            ins = pe.matmul(EH[2 * q + half][:, f * P:(f + 1) * P],
                                            w1s[:, q, k * FF + ff * P:k * FF + (ff + 1) * P], znT2[:, q, k, :],
                                            start=(k == 0), stop=(k == KT - 1))
                    ins.then_inc(l1_full[q], 1)
                if not last:
                    turn(j + q, 1 - q)
                pe.wait_ge(w2_in[q], reads(j, 16, 16))
                pe.wait_ge(mid_act[q], reads(j, 1, 1))
                freed(pe, ot_ready[q], j, 2)
                for f in range(FT):
                    if f == FT // 2:
                        pe.wait_ge(mid_dve[q], reads(j, 1, 1))
                    ins = pe.matmul(EO[q][:, 0:DM], mid[:, q, f, :], w2s[:, q, f, :], start=(f == 0), stop=(f == FT - 1))
                ins.then_inc(l2_full[q], 1)

            for t in range(TILES):
                if t % 8 == 0:
                    pe.wait_ge(rows_ready, t // 8 + 1)
                ins = pe.matmul(EO[1][:, 0:ETILES], at_row[:, t, :], at_tile[:, t, :], start=(t == 0),
                                stop=(t == TILES - 1))
            ins.then_inc(tokens_full, 1)
            turn(0, 0)
            tiles(pe, lambda j, q, more: tile(j, q, more, isinstance(j, int) and 2 * j + q == ETILES - 1))

        @block.scalar
        def _(act):
            def turned_to(j, q):
                act.wait_ge(turned[q], reads(j, 1, 1))
                for k in range(KT):
                    ins = act.activation(znT2[:, q, k, :], ET[q][:, k * P:(k + 1) * P], ACT.Identity,
                                         scale=cv("ln2_g", k), bias=cv("ln2_b", k))
                ins.then_inc(turned_out[q], 1)

            def tile(j, q, more):
                act.wait_ge(l1_full[q], reads(j, 2, 1))
                for f in range(FT // 2):
                    ins = act.activation(mid[:, q, f, :], EH[2 * q][:, f * P:(f + 1) * P], ACT.Relu,
                                         bias=w1s[:, q, KT * FF + f:KT * FF + f + 1])
                ins.then_inc(mid_act[q], 1)
                if more or not isinstance(j, int) or 2 * j + q + 1 < ETILES:
                    turned_to(j + q, 1 - q)

            turned_to(0, 0)
            tiles(act, tile)

        @block.gpsimd
        def _(pool):
            gp = nc.gpsimd

            def gather(dst, src, index, signal, bound=None):
                pool.sem_inc(p_gate, 1)
                gp.indirect_dma_start(dst, None, src, bass.IndirectOffsetOnAxis(index, 0), bounds_check=bound,
                                      oob_is_err=False).then_inc(signal, 16)

            def fetch_rows(j, q):
                pool.wait_ge(gix_ready[q], reads(j, 1, 1))
                gather(rows[:, q, :], rows_d, gix[:, q, 0:1], rows_in[q], TOK)
                gather(b2s[:, q, :], b2, gix[:, q, 2:3], b2_in[q], E - 1)

            def fetch_w1(j, q):
                gather(w1s[:, q, :], w1b, gix[:, q, 1:2], w1_in[q], E * P - 1)

            def fetch_w2(j, q):
                gather(w2s[:, q, :, :].rearrange("p f d -> p (f d)"), w2t, gix[:, q, 1:2], w2_in[q], E * P - 1)

            for q in range(2):
                fetch_rows(0, q)
                fetch_w1(0, q)
                fetch_w2(0, q)

            def tile(j, q, more):
                if more:
                    pool.wait_ge(turned[q], reads(j, 1, 1))
                    pool.wait_ge(resb_ready[q], reads(j, 1, 1))
                    fetch_rows(j + 1, q)
                    pool.wait_ge(l1_full[q], reads(j, 2, 2))
                    pool.wait_ge(mid_act[q], reads(j, 1, 1))
                    pool.wait_ge(mid_dve[q], reads(j, 1, 1))
                    fetch_w1(j + 1, q)
                    pool.wait_ge(l2_full[q], reads(j, 1, 1))
                    fetch_w2(j + 1, q)
                pool.wait_ge(ot_ready[q], reads(j, 2, 2))
                freed(pool, scattered[1 - q], j + q, 16)
                pool.sem_inc(p_gate, 1)
                gp.indirect_dma_start(out, bass.IndirectOffsetOnAxis(sid[:, q, 0:1], 0), ot[:, q, :], None,
                                      bounds_check=TOK - 1, oob_is_err=False).then_inc(scattered[q], 16)

            tiles(pool, tile)
            for q in range(2):
                pool.wait_ge(scattered[q], 16 * ((ETILES + 1 - q) // 2))
    return nc


def kernel(x, ctx_1024, mask_BxS2_bf1, L0_xattn_Wq, L0_xattn_Wk, L0_xattn_Wv, L0_xattn_Wo, L0_xattn_inv_temp,
           L0_ffn_ln1_g, L0_ffn_ln1_b, L0_ffn_ln2_g, L0_ffn_ln2_b, L0_ffn_wq, L0_ffn_bq, L0_ffn_wk, L0_ffn_bk,
           L0_ffn_wv, L0_ffn_bv, L0_ffn_wo, L0_ffn_bo, L0_ffn_gate_w, L0_ffn_gate_b, L0_ffn_w1, L0_ffn_b1,
           L0_ffn_w2, L0_ffn_b2):
    import numpy as np
    import concourse.bacc as bacc
    from concourse.bass_utils import run_bass_kernel_spmd

    def col(v):
        return v.reshape(-1, P).T

    temp = np.repeat(np.asarray(L0_xattn_inv_temp), CK)
    w1 = np.asarray(L0_ffn_w1).reshape(E, KT, P, FF).transpose(0, 2, 1, 3).reshape(E * P, KT * FF)
    b1 = np.asarray(L0_ffn_b1).reshape(E, FT, P).transpose(0, 2, 1).reshape(E * P, FT)
    w2 = np.asarray(L0_ffn_w2).reshape(E, FT, P, DM).transpose(0, 2, 1, 3).reshape(E * P, FT * DM)
    dcon = np.zeros((P, NDCON), np.float32)
    for name, value in (("before", np.triu(np.ones((P, P)), 1)), ("ones", 1.0), ("order", E - np.arange(E)),
                        ("steps", P * np.arange(TILES)), ("starts", P * np.arange(ETILES + 1)),
                        ("tile", np.arange(ETILES)), ("row", np.arange(P)),
                        ("part", np.arange(P)[:, None]),
                        ("token", P * np.arange(TILES)[None, :] + np.arange(P)[:, None] - TOK)):
        a, n = DCON[name]
        dcon[:, a:a + n] = value
    arrays = {
        "x": x,
        "ctxT": np.asarray(ctx_1024).reshape(B * CK, DM).T,
        "maskb": np.asarray(mask_BxS2_bf1).reshape(1, B * CK).view(np.uint8),
        "wqT": np.asarray(L0_xattn_Wq).T, "wk": L0_xattn_Wk, "wv": L0_xattn_Wv, "wo": L0_xattn_Wo,
        "cols": np.concatenate([col(np.asarray(v)) for v in (temp, L0_ffn_ln1_g, L0_ffn_ln1_b, L0_ffn_bq, L0_ffn_bk,
                                                             L0_ffn_bv, L0_ffn_ln2_g, L0_ffn_ln2_b)], axis=1),
        "fwq": L0_ffn_wq, "fwk": L0_ffn_wk, "fwv": L0_ffn_wv, "fwo": L0_ffn_wo,
        "bo": np.asarray(L0_ffn_bo).reshape(1, DM), "gate_w": L0_ffn_gate_w,
        "gate_b": np.asarray(L0_ffn_gate_b).reshape(1, E),
        "w1b": np.concatenate([w1, b1], axis=1), "w2t": w2, "b2": L0_ffn_b2,
        "ident_in": np.eye(P, dtype=np.float32), "dcon_in": dcon,
    }
    arrays = {name: np.ascontiguousarray(a) for name, a in arrays.items()}
    nc = bacc.Bacc("TRN2", target_bir_lowering=False, num_devices=1)
    args = {name: nc.dram_tensor(name, a.shape, mybir.dt.from_np(a.dtype), kind="ExternalInput").ap()
            for name, a in arrays.items()}
    out = nc.dram_tensor("out", (TOK, DM), F32, kind="ExternalOutput").ap()
    program(nc, **args, out=out)
    result = run_bass_kernel_spmd(nc, [arrays], core_ids=[0])
    return result.results[0]["out"].reshape(B, S, DM)
```

```python
from contextlib import ExitStack

import concourse.bass as bass
from concourse import mybir

F32 = mybir.dt.float32
F32R = mybir.dt.float32r
U32 = mybir.dt.uint32
U8 = mybir.dt.uint8
ALU = mybir.AluOpType
ACT = mybir.ActivationFunctionType
AX = mybir.AxisListType

P = 128
B, S, DM = 8, 512, 256
KT = DM // P
H, CK = 16, 64
HP = H // 2
PAIRS = CK // 2
NH, D = 16, 16
NT = S // P
TILES = B * NT
TOK = B * S
E, FF = 8, 1024
FT = FF // P
ETILES = (TOK - E) // P + E
SEGS = ETILES + ETILES % 2
G = NH // 4
VC = 32
EPS = 1e-5
BIG = 3.0e38
MASKED = 1.0e30

COLS = {}
for _name, _n in (("temp", HP), ("ln1_g", KT), ("ln1_b", KT), ("bq", KT), ("bk", KT), ("bv", KT),
                  ("ln2_g", KT), ("ln2_b", KT)):
    COLS[_name] = sum(n for _, n in COLS.values()), _n
NCOLS = sum(n for _, n in COLS.values())

HEAD = (79.78, 82.17, 83.12, 85.78)
FIRST = (90.69, 0.65)
CT0 = 1.0
VPROJ = 2.27
START = (5.87, 27.25, 50.25, 73.42)
STEP = (1.4, 1.4, 1.4, 0.6)
LEAD = 3
TAIL = (89.05, 2.09)
TAIL_IN = (1.2, 5.14, 6.6)
FOLD = 42.3
VFOLD = 68.8
STATS = (46.32, 97.29)
SCORE = (50.04, 78.05, 103.81, 21.55)
SPLIT = (57.03, 87.87, 3.03, 27.64)
PIECE = ((59.03, 2.2), (90.13, 2.2), (5.03, 1.6), (29.53, 2.1))
SHIFT = (60.82, 97.5, 14.01, 30.03)
MASK = (83.57, 0.69, 23.13, 56.1)
DENOM = (87.07, 4.13, 27.4, 58.53)
PT = (95.03, 9.56, 32.9, 64.03)
RESID = (100.67, 14.56, 37.9, 71.88)
YTURN = (9.63, 19.28, 42.9, 76.01)
YFAC = (-3.22, 15.56, 38.81, 70.34)
YNORM = (1.5, 18.6, 40.22, 72.03)
YBIAS = (2.62, 16.62, 42.44, 71.59)
Y_STORE = (12.63, 22.49, 45.65, 75.02)
X0_FOLD = -26.03
X0_VFOLD = -22.54
X0_STATS = (-25.65, -23.31)
X0_SCORE = (-19.01, -12.02, 6.03, 23.03)
X0_SPLIT = (-12.5, 5.5, 22.56, 39.5)
X0_PIECE = ((-10.0, 1.0), (7.37, 0.9), (24.72, 0.9), (42.0, 0.9))
X0_SHIFT = (-10.0, 10.06, 26.32, 43.6)
X0_MASK = (2.91, 20.51, 36.72, 54.0)
X0_DENOM = (7.31, 23.5, 40.18, 57.5)
X0_PT = (11.83, 29.5, 46.5, 62.62)
X0_RESID = (17.09, 34.5, 51.5, 69.01)
X0_YFAC = (19.86, 35.5, 52.5, 70.01)
X0_YNORM = (20.52, 36.94, 54.96, 72.01)
X0_YBIAS = (21.81, 38.0, 55.53, 73.5)
X0_YTURN = (22.5, 39.5, 56.5, 73.87)
X0_Y_STORE = (24.47, 41.0, 53.99, 71.2)


def x_tables(fold, v_fold, scores, weights, turns):
    xs = [{("M", c): fold + 0.85 * c for c in range(4)} | {("VW", c): v_fold + 0.85 * c for c in range(4)}, {}]
    xt = [{}, {}]
    for t in range(NT):
        for h in range(2):
            xs[t > 2]["sc", t, h] = scores[t] + 1.0 + 1.8 * h
            xs[t > 0]["pT", t, h] = weights[t] + 0.9 * h
        xt[t > 2]["xn", t] = scores[t]
        xt[t > 0]["av", t] = weights[t] + 2.2
        xt[1]["yn", t] = turns[t]
    return xs, xt


class Ring:

    def __init__(self, steady, first):
        def ranks(places):
            assert len(set(places.values())) == len(places)
            return {u: n for n, u in enumerate(sorted(places, key=places.get))}

        self.early = steady[0]
        self.first = ranks({(0, u): p for part in first for u, p in part.items()}
                           | {(1, u): p for u, p in steady[0].items()})
        self.steady, self.last = ranks(steady[0] | steady[1]), ranks(steady[1])
        self.count, self.before = len(self.steady), len(self.first)

    def number(self, b, u):
        if isinstance(b, int) and (b, u) in self.first:
            return self.first[b, u] - b * self.count
        if u in self.early:
            return self.before - 2 * self.count + self.steady[u]
        return self.before - self.count + (self.last if isinstance(b, int) and b == B - 1 else self.steady)[u]


X_AT, X0_AT = x_tables(FOLD, VFOLD, SCORE, PT, YTURN), x_tables(X0_FOLD, X0_VFOLD, X0_SCORE, X0_PT, X0_YTURN)
XS_AT, X0S_AT = X_AT[0][0], X0_AT[0][0]
XS, XT = Ring(X_AT[0], X0_AT[0]), Ring(X_AT[1], X0_AT[1])
assert XS.count % 2 == 0 and XS.before % 2 == 0


def first(b):
    return isinstance(b, int) and b == 0


def at_s(g, n):
    return FIRST[0] + FIRST[1] * n if g == 0 else START[g - 1] + STEP[g - 1] * (n - LEAD) - 0.1


def at_st(g, n):
    return START[g] + STEP[g] * n


def at_pv(g, t):
    return at_st(g, 4 * t + 3) + (1.5 * STEP[g] if t < NT - 1 else 0.9)


def at_ct(g):
    return CT0 if g == 0 else at_st(g - 1, 15) + 0.3


def at_ot(g):
    return at_pv(g, NT - 1) + 2.0


def at_tail(t):
    return TAIL[0] + TAIL[1] * t


FR_HEAD = {("q", 0): HEAD[0], ("k", 0): HEAD[1], ("q", 1): HEAD[2], ("k", 1): HEAD[3]}
FR_HEAD |= {("s", 0, n): at_s(0, n) for n in range(16)}
FR_BODY = {("v", t): VPROJ + 0.9 * t for t in range(NT)}
for _g in range(G):
    FR_BODY |= {("s", _g, n): at_s(_g, n) for n in range(16) if _g > 0} | {("st", _g, n): at_st(_g, n) for n in range(16)}
    FR_BODY |= {("ct", _g): at_ct(_g), ("ot", _g): at_ot(_g)}
for _t in range(NT):
    FR_BODY |= {("oT", _t): at_tail(_t), ("wo", _t): at_tail(_t) + TAIL_IN[0], ("zT", _t): at_tail(_t) + TAIL_IN[1],
                ("gate", _t): at_tail(_t) + TAIL_IN[2]}
FR_AT = {u: place + 1e-4 * n for n, (u, place) in enumerate((FR_HEAD | FR_BODY).items())}
FR_HEAD, FR_BODY = ({u: FR_AT[u] for u in units} for units in (FR_HEAD, FR_BODY))
NFR = 4
FR_N, FR_HEAD_N, FR_BODY_N = [{u: n for n, u in enumerate(sorted(places, key=places.get))}
                              for places in (FR_AT, FR_HEAD, FR_BODY)]
assert len(set(FR_AT.values())) == len(FR_AT)
assert len(FR_AT) % NFR == 0 and len(FR_HEAD) % NFR == 0
STACK = 16 * 9
NSLOT = 3
SLOT = (0, 1, 2, 0)


def weave(*streams):
    due = [[next(s, None), s] for s in streams]
    while any(place is not None for place, _ in due):
        first = min((d for d in due if d[0] is not None), key=lambda d: d[0])
        first[0] = next(first[1], None)


NCONST = 12
VX_EARLY, VX_LATE, VF = 15, 23, 8
PX_EARLY, PX_LATE, PF = 6, 24, 8
W1COLS = KT * FF + FT

DCON = {}
for _name, _n in (("before", P), ("ones", P), ("order", E), ("steps", TILES), ("starts", SEGS + 1),
                  ("tile", ETILES), ("row", P), ("part", 1), ("token", TILES)):
    DCON[_name] = sum(n for _, n in DCON.values()), _n
NDCON = sum(n for _, n in DCON.values())


def reads(j, per, count):
    return j * per + count


def at(i, per, count):
    return i * per + (count + 1)


def program(nc, x, ctxT, maskb, wqT, wk, wv, wo, cols, fwq, fwk, fwv, fwo, bo, gate_w, gate_b,
            w1b, w2t, b2, ident_in, dcon_in, out):
    ctx = ExitStack()
    with ctx:
        started = []

        def sb(name, shape, dt=F32):
            return ctx.enter_context(nc.sbuf_tensor(name, shape, dt))

        def bank(name):
            return ctx.enter_context(nc.psum_tensor(name, [P, 512], F32))

        def sem(name):
            return ctx.enter_context(nc.semaphore(name))

        def lsem(name):
            started.append(sem(name))
            return started[-1]

        def dram(name, shape, dt=F32):
            return nc.dram_tensor(name, shape, dt, kind="Internal").ap()

        kT_d = dram("kT_d", (HP, P, B * CK))
        vT_d = dram("vT_d", (HP, P, B * CK))
        parts_d = dram("parts_d", (4, NH * D, S))
        xy_d = dram("xy_d", (TOK, 2 * DM))
        rows_d = dram("rows_d", (TOK + 1, 2 * DM))

        ident = sb("ident", [P, P])
        col = sb("col", [P, NCOLS])
        bias_m = sb("bias_m", [P, B * CK])
        mask_u = sb("mask_u", [P, B * CK], U8)
        bo_b = sb("bo_b", [P, DM])
        gb_b = sb("gb_b", [P, E])
        wqT_s = sb("wqT_s", [P, HP, DM])
        wo_s = sb("wo_s", [P, HP, DM])
        fw = {n: sb("f" + n, [P, KT, DM]) for n in ("q", "k", "v", "o")}
        gw = sb("gw", [P, KT, E])
        logits = sb("logits", [P, TILES * E])
        zrow = sb("zrow", [NT * 4, P])

        def cv(name, n):
            return col[:, COLS[name][0] + n:COLS[name][0] + n + 1]

        attn_space = ExitStack()

        def sa(name, shape, dt=F32):
            return attn_space.enter_context(nc.sbuf_tensor(name, shape, dt))

        kbd = sa("kbd", [P, HP, P])
        vbd = sa("vbd", [P, HP, P])
        M = sa("M", [P, KT, H * CK])
        VW = sa("VW", [P, HP, DM])
        xb = sa("xb", [P, NT, DM])
        xstat = sa("xstat", [P, NT, 6])
        xmv = sa("xmv", [P, NT, 2])
        xr = sa("xr", [P, NT, 2])
        xn = sa("xn", [P, NT, DM])
        xnT = sa("xnT", [P, KT, P])
        sraw = sa("sraw", [P, H * CK])
        s = sa("s", [P, 2, H, CK])
        e = sa("e", [P, H, CK])
        m = sa("m", [P, H, CK])
        hi = sa("hi", [P, H, PAIRS])
        lo = sa("lo", [P, 2, H, PAIRS])
        nhi = sa("nhi", [P, H, PAIRS])
        mx = sa("mx", [P, 2, H])
        lo17 = sa("lo17", [P, H, 17])
        nh17 = sa("nh17", [P, H, 17])
        merged = sa("merged", [P, H, 17])
        thr = sa("thr", [P, H])
        sums = sa("sums", [P, 2, H])
        den = sa("den", [P, H])
        rden = sa("rden", [P, 2, H])
        pT = sa("pT", [P, HP * P])
        xy = sa("xy", [P, 2, 2 * DM])
        ystat = sa("ystat", [P, 6])
        ymv = sa("ymv", [P, 2])
        xv = sa("xv", [P, NT])
        yv = sa("yv", [P, 4])
        mhalf = sa("mhalf", [P, NT])
        yr = sa("yr", [P, 2, 4])
        yn = sa("yn", [P, DM])
        hnT = sa("hnT", [P, KT, S])

        parts = sa("parts", [P, 2, 2, S], F32R)
        qs = sa("qs", [P, 4 * NSLOT, S], F32R)
        ks = sa("ks", [P, 4 * NSLOT, S], F32R)
        v32 = sa("v32", [P, NT, NH, VC])
        nmax = sa("nmax", [P, 2, 4 * NT])
        cT = sa("cT", [NT * 4, P], F32R)
        pt = sa("pt", [P, 2, 4, S])
        osb = sa("osb", [P, S])
        rz = sa("rz", [P, NT, 4])
        on = sa("on", [P, NT, DM])
        oT = sa("oT", [P, KT, P])
        z = sa("z", [P, 2, DM])
        zstat = sa("zstat", [P, 6])
        zv = sa("zv", [P, 1])
        zmv = sa("zmv", [P, 2])
        zr = sa("zr", [P, 2, 2])
        xyf = sa("xyf", [P, 2, 2 * DM])
        row = sa("row", [P, 2, 2 * DM])
        znT = sa("znT", [P, KT, P])

        pre_ctx = sraw[:, :].rearrange("p (k n) -> p k n", k=KT)
        pre_w = [s[:, :, :, :].rearrange("p a h c -> p (a h c)").rearrange("p (k n) -> p k n", k=KT), M[:, :, :]]
        flat = [[VW[:, :, :].rearrange("p h d -> p (h d)"), e[:, :, :].rearrange("p h c -> p (h c)"),
                 m[:, :, :].rearrange("p h c -> p (h c)")],
                [pT[:, :], xy[:, :, :].rearrange("p t d -> p (t d)"), hnT[:, :, :].rearrange("p k s -> p (k s)"),
                 xyf[:, :, :].rearrange("p t d -> p (t d)")]]
        pre_out = [[part[:, n:n + B * CK] for part in parts_ for n in range(0, part.shape[1], B * CK)] for parts_ in flat]

        xs = [bank(f"xs{n}") for n in range(2)]
        xt = bank("xt")
        fr = [bank(f"fr{n}") for n in range(NFR)]
        ob = bank("ob")
        ET, EH, EO = fr[0:2], [xs[0], xs[1], fr[2], fr[3]], [xt, ob]

        const_loaded, proj_loaded = sem("const_loaded"), sem("proj_loaded")
        zeroed, consts_ready = sem("zeroed"), sem("consts_ready")
        kv_full, p_set = sem("kv_full"), sem("p_set")
        kv_copied = [sem("k_copied"), sem("v_copied")]
        kv_stored = [sem("k_stored"), sem("v_stored")]
        kbd_loaded, vbd_loaded, x_loaded = lsem("kbd_loaded"), lsem("vbd_loaded"), [lsem(f"x_loaded{n}") for n in range(2)]
        vxe_step, vxl_step, vf_step, v_gate = lsem("vxe_step"), lsem("vxl_step"), lsem("vf_step"), sem("v_gate")
        sp_gate, pe_gate = sem("sp_gate"), sem("pe_gate")
        pxe_step, pxl_step, pf_step, p_gate = lsem("pxe_step"), lsem("pxl_step"), lsem("pf_step"), sem("p_gate")
        xs_full, xt_full, fr_full, o_full = lsem("xs_full"), lsem("xt_full"), lsem("fr_full"), lsem("o_full")
        xs_emptied = [lsem(f"xs_emptied{n}") for n in range(2)]
        xt_emptied, o_emptied = lsem("xt_emptied"), lsem("o_emptied")
        fr_emptied = [lsem(f"fr_emptied{n}") for n in range(NFR)]
        xr_ready, xn_ready = lsem("xr_ready"), lsem("xn_ready")
        s_ready, split_done, neg_done, mask_done = (lsem("s_ready"), lsem("split_done"), lsem("neg_done"),
                                                    lsem("mask_done"))
        d_ready, e_ready, em_ready, rden_ready, p_ready = (lsem("d_ready"), lsem("e_ready"), lsem("em_ready"),
                                                           lsem("rden_ready"), lsem("p_ready"))
        mx_ready, xmv_ready, ymv_ready, zmv_ready = lsem("mx_ready"), lsem("xmv_ready"), lsem("ymv_ready"), lsem("zmv_ready")
        yr_ready, y_ready, yn_ready, yb_ready = lsem("yr_ready"), lsem("y_ready"), lsem("yn_ready"), lsem("yb_ready")
        part_hi, parts_stored = lsem("part_hi"), [lsem(f"parts_stored{n}") for n in range(2)]
        stack_loaded = [lsem(f"stack_loaded{n}") for n in range(NSLOT)]
        xy_stored, xyf_loaded = [[lsem(f"{name}{n}") for n in range(2)] for name in ("xy_stored", "xyf_loaded")]
        c_loaded = lsem("c_loaded")
        zr_ready, zn_ready, res_ready = lsem("zr_ready"), lsem("zn_ready"), lsem("res_ready")
        rows_stored, scratch_set = [lsem(f"rows_stored{n}") for n in range(2)], sem("scratch_set")

        dcon_loaded = sem("dcon_loaded")
        d_step, oh_ready, count_full, counts_read = sem("d_step"), sem("oh_ready"), sem("count_full"), sem("counts_read")
        rows_ready, tokens_full, rec_ready = sem("rows_ready"), sem("tokens_full"), sem("rec_ready")

        def pair(name):
            return [sem(f"{name}{n}") for n in range(2)]

        gix_ready = pair("gix_ready")
        rows_in, w1_in, w2_in, b2_in = pair("rows_in"), pair("w1_in"), pair("w2_in"), pair("b2_in")
        turned, turned_out = pair("turned"), pair("turned_out")
        l1_full, l2_full = pair("l1_full"), pair("l2_full")
        mid_act, mid_dve = pair("mid_act"), pair("mid_dve")
        resb_ready, ot_ready, scattered = pair("resb_ready"), pair("ot_ready"), pair("scattered")

        def xs_written(eng, i, u):
            eng.wait_ge(xs_full, at(i, XS.count, XS.number(i, u) + 1))

        def xs_read(eng, i, u):
            n = XS.number(i, u)
            eng.wait_ge(xs_emptied[n % 2], at(i, XS.count // 2, n // 2 + 1))

        def xt_written(eng, i, u):
            eng.wait_ge(xt_full, at(i, XT.count, XT.number(i, u) + 1))

        def xt_read(eng, i, u):
            eng.wait_ge(xt_emptied, at(i, XT.count, XT.number(i, u) + 1))

        def fr_place(i, u):
            if u in FR_HEAD:
                return FR_HEAD_N[u] if isinstance(i, int) and i == 0 else len(FR_HEAD) - len(FR_AT) + FR_N[u]
            return len(FR_HEAD) + (FR_BODY_N if isinstance(i, int) and i == B - 1 else FR_N)[u]

        def fr_written(eng, i, u):
            eng.wait_ge(fr_full, at(i, len(FR_AT), fr_place(i, u) + 1))

        def fr_read(eng, i, u):
            n = fr_place(i, u)
            eng.wait_ge(fr_emptied[n % NFR], at(i, len(FR_AT) // NFR, n // NFR + 1))

        def fr_bank(i, u):
            return fr[fr_place(i, u) % NFR]

        def fr_sem(i, u):
            return fr_emptied[fr_place(i, u) % NFR]

        with nc.Block() as start:
            def raise_to_one(eng, share):
                for q in started[share::5]:
                    eng.sem_inc(q, 1)

            @start.sync
            def _(sp):
                raise_to_one(sp, 0)

            @start.tensor
            def _(pe):
                raise_to_one(pe, 1)

            @start.scalar
            def _(act):
                raise_to_one(act, 2)

            @start.vector
            def _(dve):
                raise_to_one(dve, 3)

            @start.gpsimd
            def _(pool):
                raise_to_one(pool, 4)

        block_ctx = ExitStack()
        block = block_ctx.enter_context(nc.Block())

        def iterations(eng, body, head, x_early, x_late):
            def run(*parts):
                weave(*(stream for part in parts for stream in part))

            run(x_early(0), x_late(0), head(0), x_early(1))
            with eng.Fori(0, B - 2) as i:
                run(body(i), head(i + 1, i), x_late(i + 1, i), x_early(i + 2))
            run(body(B - 2), head(B - 1, B - 2), x_late(B - 1, B - 2))
            run(body(B - 1))

        @block.sync
        def _(sp):
            def cload(dst, src):
                sp.dma_start(dst, src).then_inc(const_loaded, 16)

            sp.dma_start(pre_ctx, ctxT.rearrange("(k p) n -> p k n", p=P)).then_inc(proj_loaded, 16)
            sp.dma_start(pre_w[0], wk.rearrange("(k p) n -> p k n", p=P)).then_inc(proj_loaded, 16)
            sp.dma_start(pre_w[1], wv.rearrange("(k p) n -> p k n", p=P)).then_inc(proj_loaded, 16)
            cload(col[:, :], cols)
            cload(ident[:, :], ident_in)
            cload(mask_u[:, :], maskb.to_broadcast((P, B * CK)))
            cload(wqT_s[:, :, :], wqT.rearrange("(h p) n -> p h n", p=P))
            cload(wo_s[:, :, :], wo.rearrange("(h p) n -> p h n", p=P))
            for name, w in (("q", fwq), ("k", fwk), ("v", fwv), ("o", fwo)):
                cload(fw[name][:, :, :], w.rearrange("(k p) n -> p k n", p=P))
            cload(gw[:, :, :], gate_w.rearrange("(k p) n -> p k n", p=P))
            for half in range(2):
                sp.dma_start(xb[:, 2 * half:2 * half + 2, :],
                             x[0, half * 2 * P:(half + 1) * 2 * P, :].rearrange("(t p) d -> p t d", p=P))\
                  .then_inc(x_loaded[half], 16)
            cload(bo_b[:, :], bo.to_broadcast((P, DM)))
            cload(gb_b[:, :], gate_b.to_broadcast((P, E)))
            for part in range(2):
                for n in range(HP):
                    sp.wait_ge(kv_copied[part], n + 1)
                    sp.dma_start((kT_d, vT_d)[part][n], pre_out[part][n]).then_inc(kv_stored[part], 16)
                if part == 0:
                    sp.wait_ge(zeroed, 2)
                sp.wait_ge(kv_stored[part], 16 * HP)
                for dst, src, signal in ((kbd, kT_d, kbd_loaded), (vbd, vT_d, vbd_loaded))[part:part + 1]:
                    for hh in range(2):
                        r = slice(CK * hh, CK * hh + CK)
                        sp.dma_start(dst[r, :, r], src[:, r, 0:CK].rearrange("h p s -> p h s")).then_inc(signal, 16)
            sp.dma_start(rows_d[TOK:TOK + 1, :].rearrange("o (a c) -> (o a) c", c=P), zrow[0:4, :])\
              .then_inc(scratch_set, 16)

            def hold():
                sp.sem_inc(sp_gate, 1)

            def x_loads(b):
                for half in range(2):
                    yield RESID[2 * half + 1] + 1.5
                    xt_read(sp, b - 1, ("av", 2 * half + 1))
                    hold()
                    sp.dma_start(xb[:, 2 * half:2 * half + 2, :],
                                 x[bass.ds(b, 1), half * 2 * P:(half + 1) * 2 * P, :].rearrange("a (t p) d -> p (a t) d", p=P))\
                      .then_inc(x_loaded[half], 16)

            def k_loads(b):
                yield FOLD - 10.0
                sp.wait_ge(s_ready, at(b - 1, NT, 2))
                hold()
                for dst, src, signal in ((kbd, kT_d, kbd_loaded), (vbd, vT_d, vbd_loaded)):
                    for hh in range(2):
                        r = slice(CK * hh, CK * hh + CK)
                        sp.dma_start(dst[r, :, r],
                                     src[:, r, bass.ds(b * CK, CK)].rearrange("h p s -> p h s"))\
                          .then_inc(signal, 16)

            def y_stores(b):
                for t in range(NT):
                    yield (X0_Y_STORE if first(b) else Y_STORE)[t]
                    sp.wait_ge(yb_ready, at(b, NT, t + 1))
                    hold()
                    sp.dma_start(xy_d[bass.ds(b * S + t * P, P), :], xy[:, t % 2, :]).then_inc(xy_stored[t % 2], 16)

            def store_parts(i):
                for n, u in enumerate((("q", 0), ("k", 0), ("q", 1), ("k", 1))):
                    yield FR_AT[u] + 2.8
                    base, mt = 2 * (u[0] == "k"), u[1]
                    if n == 0:
                        sp.wait_ge(stack_loaded[SLOT[3]], at(i, 2 * STACK, 0))
                        hold()
                    fr_read(sp, i, u)
                    hold()
                    sp.dma_start(parts_d[base:base + 2, mt * P:(mt + 1) * P, :].rearrange("j p s -> p j s"),
                                 parts[:, n % 2, :, :].bitcast(F32)).then_inc(parts_stored[n % 2], 16)

            def load_stack(i, g, place, after=None):
                slot = SLOT[g]
                sl = slice(4 * slot, 4 * slot + 4)
                yield place
                if after is not None:
                    fr_written(sp, *after)
                    hold()
                for q in parts_stored:
                    sp.wait_ge(q, at(i, 32, 16 + 16 * (g // 2)))
                    hold()

                def rows(part):
                    return parts_d[part, 64 * g:64 * g + 64, :].rearrange("(h d) s -> d h s", d=D)

                for r, part in enumerate((0, 0, 1, 1)):
                    sp.dma_start(qs[D * r:D * r + D, sl, :].bitcast(F32), rows(part)).then_inc(stack_loaded[slot], 16)
                for r, part in enumerate((2, 3, 2, 3)):
                    sp.dma_start(ks[D * r:D * r + D, sl, :].bitcast(F32), rows(part)).then_inc(stack_loaded[slot], 16)
                sp.dma_start(qs[4 * D:4 * D + 1, sl, :].bitcast(F32).rearrange("o h (t c) -> o (h t) c", c=P),
                             zrow[:, :]).then_inc(stack_loaded[slot], 16)

            def load_max(i):
                for g in range(G):
                    yield at_ct(g) + 0.6
                    sl = slice(4 * SLOT[g], 4 * SLOT[g] + 4)
                    fr_read(sp, i, ("ct", g))
                    sp.dma_start(qs[4 * D:4 * D + 1, sl, :].bitcast(F32).rearrange("o h (t c) -> o (h t) c", c=P),
                                 cT[:, :].bitcast(F32)).then_inc(c_loaded, 16)

            def load_xy(i):
                for t in range(NT):
                    yield at_tail(max(t - 1, 0)) - 6.0 if t < 2 else at_tail(t - 2) + 4.4
                    for q in xy_stored:
                        sp.wait_ge(q, at(i, 32, 32))
                        hold()
                    sp.wait_ge(res_ready, at(i, NT, max(t - 1, 0)))
                    hold()
                    sp.dma_start(xyf[:, t % 2, :], xy_d[bass.ds(i * S + t * P, P), :]).then_inc(xyf_loaded[t % 2], 16)

            def store_rows(i):
                for t in range(NT):
                    yield at_tail(t) + 5.4
                    sp.wait_ge(res_ready, at(i, NT, t + 1))
                    hold()
                    sp.wait_ge(zn_ready, at(i, NT, t + 1))
                    hold()
                    sp.dma_start(rows_d[bass.ds(i * S + t * P, P), :], row[:, t % 2, :]).then_inc(rows_stored[t % 2], 16)

            def head(i, last=None):
                def after(g):
                    return (last, ("st", g, 15)) if last is not None else None

                return (store_parts(i), load_stack(i, 0, HEAD[1] + 5.0, after(3)), load_stack(i, 1, HEAD[3] + 4.0, after(1)),
                        load_stack(i, 2, HEAD[3] + 8.0, after(2)))

            def body(i):
                return load_stack(i, 3, at_st(0, 15) + 1.0, (i, ("st", 0, 15))), load_max(i), load_xy(i), store_rows(i)

            def x_early(b):
                return () if first(b) else (x_loads(b), k_loads(b))

            def x_late(b, last=None):
                return [y_stores(b)]

            iterations(sp, body, head, x_early, x_late)
            for q in rows_stored:
                sp.wait_ge(q, 16 * TILES // 2 + 1)
            sp.wait_ge(scratch_set, 16)

        @block.tensor
        def _(pe):
            def mm(o, l, r, first=True, last=True):
                return pe.matmul(o, l, r, start=first, stop=last)

            def tr(o, src):
                return pe.transpose(o, src, ident[:, :])

            pe.wait_ge(proj_loaded, 48)
            for n in range(2 * HP):
                part, hp = n // HP, n % HP
                if n >= NFR:
                    pe.wait_ge(kv_copied[(n - NFR) // HP], (n - NFR) % HP + 1)
                for k in range(KT):
                    ins = mm(fr[n % NFR][:, :], pre_w[part][:, k, hp * P:(hp + 1) * P], pre_ctx[:, k, :],
                             k == 0, k == KT - 1)
                ins.then_inc(kv_full, 1)
            pe.wait_ge(const_loaded, 16 * NCONST)
            for q in kv_copied:
                pe.wait_ge(q, HP)
            pe.wait_ge(zeroed, 2)

            def xs_slot(i, u):
                n = XS.number(i, u)
                pe.wait_ge(xs_emptied[n % 2], at(i, XS.count // 2, n // 2))
                return xs[n % 2]

            def xt_slot(i, u):
                pe.wait_ge(xt_emptied, at(i, XT.count, XT.number(i, u)))
                return xt

            def fr_slot(i, u):
                n = fr_place(i, u)
                pe.wait_ge(fr_emptied[n % NFR], at(i, len(FR_AT) // NFR, n // NFR))
                return fr[n % NFR]

            def fold(i):
                for c in range(4):
                    yield (X0S_AT if first(i) else XS_AT)["M", c]
                    if c == 0:
                        pe.wait_ge(kbd_loaded, at(i, 32, 32))
                    o = xs_slot(i, ("M", c))
                    mt, half = c // 2, c % 2
                    for j in range(4):
                        hp = 4 * half + j
                        ins = mm(o[:, j * P:(j + 1) * P], wqT_s[:, hp, mt * P:(mt + 1) * P], kbd[:, hp, :])
                    ins.then_inc(xs_full, 1)
                for c in range(4):
                    yield (X0S_AT if first(i) else XS_AT)["VW", c]
                    if c == 0:
                        pe.wait_ge(vbd_loaded, at(i, 32, 32))
                    o = xs_slot(i, ("VW", c))
                    for j in range(2):
                        hp = 2 * c + j
                        ins = mm(o[:, j * DM:(j + 1) * DM], vbd[:, hp, :], wo_s[:, hp, :])
                    ins.then_inc(xs_full, 1)

            def x_scores(i, t):
                yield (X0_SCORE if first(i) else SCORE)[t]
                pe.wait_ge(xn_ready, at(i, NT, t + 1))
                o = xt_slot(i, ("xn", t))
                for k in range(KT):
                    ins = tr(o[:, k * P:(k + 1) * P], xn[:, t, k * P:(k + 1) * P])
                ins.then_inc(xt_full, 1)
                for half in range(2):
                    yield (X0_SCORE if first(i) else SCORE)[t] + 1.0 + 1.8 * half
                    if half == 0:
                        xt_read(pe, i, ("xn", t))
                    o = xs_slot(i, ("sc", t, half))
                    if t == 0 and half == 0:
                        xs_read(pe, i, ("M", 3))
                    for k in range(KT):
                        ins = mm(o[:, :], xnT[:, k, :], M[:, k, half * 512:(half + 1) * 512], k == 0, k == KT - 1)
                    ins.then_inc(xs_full, 1)

            def x_pT(i, t):
                for half in range(2):
                    yield (X0_PT if first(i) else PT)[t] + 0.9 * half
                    if half == 0:
                        pe.wait_ge(p_ready, at(i, NT, t + 1))
                    o = xs_slot(i, ("pT", t, half))
                    for j in range(4):
                        h0 = 8 * half + 2 * j
                        ins = tr(o[:, j * P:(j + 1) * P], m[:, h0:h0 + 2, :].rearrange("p h c -> p (h c)"))
                    ins.then_inc(xs_full, 1)
                yield (X0_PT if first(i) else PT)[t] + 2.2
                o = xt_slot(i, ("av", t))
                xs_read(pe, i, ("pT", t, 1))
                for hp in range(HP):
                    ins = mm(o[:, 0:DM], pT[:, hp * P:(hp + 1) * P], VW[:, hp, :], hp == 0, hp == HP - 1)
                ins.then_inc(xt_full, 1)

            def y_turn(i, t):
                yield (X0_YTURN if first(i) else YTURN)[t]
                pe.wait_ge(yn_ready, at(i, NT, t + 1))
                o = xt_slot(i, ("yn", t))
                for k in range(KT):
                    ins = tr(o[:, k * P:(k + 1) * P], yn[:, k * P:(k + 1) * P])
                ins.then_inc(xt_full, 1)

            def x_early(b):
                return [fold(b), x_pT(b, 0)] + [x_scores(b, t) for t in range(3)]

            def x_late(b, last=None):
                return [x_scores(b, 3)] + [x_pT(b, t) for t in (1, 2, 3)] + [y_turn(b, t) for t in range(NT)]

            def projections(i):
                for n, (name, mt) in enumerate((("q", 0), ("k", 0), ("q", 1), ("k", 1))):
                    yield FR_AT[name, mt]
                    if n == 0:
                        xt_read(pe, i, ("yn", NT - 1))
                    o = fr_slot(i, (name, mt))
                    for k in range(KT):
                        ins = mm(o[:, :], fw[name][:, k, mt * P:(mt + 1) * P], hnT[:, k, :], k == 0, k == KT - 1)
                    ins.then_inc(fr_full, 1)

            def values(i):
                for t in range(NT):
                    yield FR_AT["v", t]
                    o = fr_slot(i, ("v", t))
                    for k in range(KT):
                        ins = mm(o[:, 0:DM], hnT[:, k, t * P:(t + 1) * P], fw["v"][:, k, :], k == 0, k == KT - 1)
                    ins.then_inc(fr_full, 1)

            def first_pass(i, g):
                for n in range(16):
                    t, h = n // 4, n % 4
                    yield FR_AT["s", g, n]
                    slot = SLOT[g]
                    if n == 0:
                        pe.wait_ge(stack_loaded[slot], at(i, STACK * SLOT.count(slot), STACK * (1 + SLOT[:g].count(slot))))
                    o = fr_slot(i, ("s", g, n))
                    mm(o[:, :], qs[:, 4 * slot + h, t * P:(t + 1) * P], ks[:, 4 * slot + h, :]).then_inc(fr_full, 1)

            def maxima_taken(i):
                yield 1000.0
                fr_read(pe, i, ("s", 0, 15))
                pe.sem_inc(pe_gate, 1)

            def turn_max(i, g):
                yield FR_AT["ct", g]
                if g > 0:
                    fr_read(pe, i, ("s", g, 15))
                o = fr_slot(i, ("ct", g))
                tr(o[0:4 * NT, 0:P], nmax[:, g % 2, :]).then_inc(fr_full, 1)

            def second_pass(i, g):
                for n in range(16):
                    t, h = n // 4, n % 4
                    yield FR_AT["st", g, n]
                    sl = 4 * SLOT[g] + h
                    o = fr_slot(i, ("st", g, n))
                    if n == 0:
                        pe.wait_ge(c_loaded, at(i, 16 * G, 16 * (g + 1)))
                    mm(o[:, :], ks[:, sl, t * P:(t + 1) * P], qs[:, sl, :]).then_inc(fr_full, 1)

            def pv(i, g):
                for t in range(NT):
                    yield at_pv(g, t)
                    fr_read(pe, i, ("st", g, 4 * t + 3))
                    if t == 0:
                        pe.wait_ge(o_emptied, at(i, G, g))
                    for h in range(4):
                        ins = pe.matmul(ob[VC * h:VC * h + VC, :], v32[:, t, 4 * g + h, :], pt[:, t % 2, h, :],
                                        start=(t == 0), stop=(t == NT - 1))
                    ins.then_inc(o_full, 1)
                yield FR_AT["ot", g]
                pe.wait_ge(o_emptied, at(i, G, g + 1))
                o = fr_slot(i, ("ot", g))
                for t in range(NT):
                    ins = tr(o[:, t * P:(t + 1) * P], osb[:, t * P:(t + 1) * P])
                ins.then_inc(fr_full, 1)

            def out_proj(i, t):
                yield FR_AT["oT", t]
                if t == 0:
                    fr_read(pe, i, ("ot", G - 1))
                o = fr_slot(i, ("oT", t))
                for k in range(KT):
                    ins = tr(o[:, k * P:(k + 1) * P], on[:, t, k * P:(k + 1) * P])
                ins.then_inc(fr_full, 1)
                yield FR_AT["wo", t]
                o = fr_slot(i, ("wo", t))
                fr_read(pe, i, ("oT", t))
                for k in range(KT):
                    ins = mm(o[:, 0:DM], oT[:, k, :], fw["o"][:, k, :], k == 0, k == KT - 1)
                ins.then_inc(fr_full, 1)

            def gate(i, t):
                yield FR_AT["zT", t]
                pe.wait_ge(zn_ready, at(i, NT, t + 1))
                o = fr_slot(i, ("zT", t))
                for k in range(KT):
                    ins = tr(o[:, k * P:(k + 1) * P], row[:, t % 2, k * P:(k + 1) * P])
                ins.then_inc(fr_full, 1)
                yield FR_AT["gate", t]
                o = fr_slot(i, ("gate", t))
                fr_read(pe, i, ("zT", t))
                for k in range(KT):
                    ins = mm(o[:, 0:E], znT[:, k, :], gw[:, k, :], k == 0, k == KT - 1)
                ins.then_inc(fr_full, 1)

            def head(i, last=None):
                return projections(i), first_pass(i, 0), maxima_taken(i)

            def body(i):
                return ([values(i)] + [first_pass(i, g) for g in range(1, G)]
                        + [part(i, g) for g in range(G) for part in (turn_max, second_pass, pv)]
                        + [part(i, t) for t in range(NT) for part in (out_proj, gate)])

            iterations(pe, body, head, x_early, x_late)

        @block.scalar
        def _(act):
            def copy(o, src, scale=1.0, bias=None):
                if bias is None:
                    return act.activation(o, src, ACT.Copy, scale=scale)
                return act.activation(o, src, ACT.Identity, scale=scale, bias=bias)

            act.wait_ge(consts_ready, 1)
            for n in range(2 * HP):
                act.wait_ge(kv_full, n + 1)
                part, hp = n // HP, n % HP
                act.activation(pre_out[part][hp], fr[n % NFR][:, :], ACT.Copy, scale=cv("temp", hp) if part == 0 else 1.0)\
                   .then_inc(kv_copied[part], 1)
            act.wait_ge(consts_ready, 2)

            def fold_out(i):
                for c in range(4):
                    u = ("M", c)
                    yield (X0S_AT if first(i) else XS_AT)["M", c] + 0.6
                    xs_written(act, i, u)
                    copy(M[:, c // 2, (c % 2) * 512:(c % 2 + 1) * 512], xs[XS.number(i, u) % 2][:, :])\
                        .then_inc(xs_emptied[XS.number(i, u) % 2], 1)
                for c in range(4):
                    u = ("VW", c)
                    yield (X0S_AT if first(i) else XS_AT)["VW", c] + 0.6
                    xs_written(act, i, u)
                    copy(VW[:, 2 * c:2 * c + 2, :].rearrange("p h d -> p (h d)"), xs[XS.number(i, u) % 2][:, :])\
                        .then_inc(xs_emptied[XS.number(i, u) % 2], 1)

            def x_norm(i):
                for t in range(NT):
                    yield (X0_STATS if first(i) else STATS)[t // 2] + 2.5 + 0.6 * (t % 2)
                    act.wait_ge(xr_ready, at(i, NT, 2 * (t // 2) + 2))
                    copy(xn[:, t, :], xb[:, t, :], xr[:, t, 0:1], xr[:, t, 1:2]).then_inc(xn_ready, 1)

            def scores_out(i, t):
                yield (X0_SCORE if first(i) else SCORE)[t] + 0.5
                xt_written(act, i, ("xn", t))
                copy(xnT[:, :, :].rearrange("p k c -> p (k c)"), xt[:, 0:DM]).then_inc(xt_emptied, 1)
                for half in range(2):
                    u = ("sc", t, half)
                    yield (X0_SCORE if first(i) else SCORE)[t] + 1.9 + 1.8 * half
                    xs_written(act, i, u)
                    if half == 0:
                        act.wait_ge(s_ready, at(i, NT, t))
                    copy(sraw[:, half * 512:(half + 1) * 512], xs[XS.number(i, u) % 2][:, :])\
                        .then_inc(xs_emptied[XS.number(i, u) % 2], 1)

            def negate(i, t):
                yield (X0_SPLIT if first(i) else SPLIT)[t] + 0.8
                act.wait_ge(split_done, at(i, NT, t + 1))
                if not first(i) or t > 0:
                    act.wait_ge(mask_done, at(i, NT, t))
                act.activation(nhi[:, :, :].rearrange("p h c -> p (h c)"),
                               hi[:, :, :].rearrange("p h c -> p (h c)"), ACT.Copy, scale=-1.0)\
                   .then_inc(neg_done, 1)

            def exponent(i, t):
                yield (X0_SHIFT if first(i) else SHIFT)[t] + 2.3
                act.wait_ge(d_ready, at(i, NT, t + 1))
                ev = e[:, :, :].rearrange("p h c -> p (h c)")
                act.activation(ev, ev, ACT.Exp).then_inc(e_ready, 1)

            def pT_out(i, t):
                for half in range(2):
                    u = ("pT", t, half)
                    yield (X0_PT if first(i) else PT)[t] + 0.5 + 0.9 * half
                    xs_written(act, i, u)
                    copy(pT[:, half * 512:(half + 1) * 512], xs[XS.number(i, u) % 2][:, :])\
                        .then_inc(xs_emptied[XS.number(i, u) % 2], 1)

            def y_norm(i, t):
                yield (X0_YNORM if first(i) else YNORM)[t]
                act.wait_ge(yr_ready, at(i, NT, t + 1))
                r = yr[:, t % 2, :]
                x1 = xy[:, t % 2, 0:DM]
                copy(xy[:, t % 2, DM:2 * DM], x1, r[:, 0:1], r[:, 2:3]).then_inc(y_ready, 1)
                if not first(i) or t > 0:
                    xt_written(act, *((i, ("yn", t - 1)) if t > 0 else (i - 1, ("yn", NT - 1))))
                copy(yn[:, :], x1, r[:, 1:2], r[:, 3:4]).then_inc(yn_ready, 1)

            def y_out(b, t, i):
                yield (X0_YTURN if first(b) else YTURN)[t] + 0.5
                if t == 0 and i is not None:
                    fr_written(act, i, ("v", NT - 1))
                xt_written(act, b, ("yn", t))
                for k in range(KT):
                    ins = copy(hnT[:, k, t * P:(t + 1) * P], xt[:, k * P:(k + 1) * P], cv("ln1_g", k), cv("ln1_b", k))
                ins.then_inc(xt_emptied, 1)

            def x_early(b):
                return [fold_out(b), x_norm(b), scores_out(b, 0), scores_out(b, 1), scores_out(b, 2), negate(b, 0),
                        exponent(b, 0), negate(b, 1), exponent(b, 1), pT_out(b, 0)]

            def x_late(b, last=None):
                return ([part(b, t) for t in (2, 3) for part in (negate, exponent)]
                        + [pT_out(b, t) for t in (1, 2, 3)] + [scores_out(b, 3)]
                        + [y_norm(b, t) for t in range(NT)] + [y_out(b, t, last) for t in range(NT)])

            def heads_out(i):
                for n, u in enumerate((("q", 0), ("k", 0), ("q", 1), ("k", 1))):
                    yield FR_AT[u] + 1.7
                    fr_written(act, i, u)
                    act.wait_ge(parts_stored[n % 2], at(i, 32, 16 * (n // 2)))
                    copy(parts[:, n % 2, 0, :], fr_bank(i, u)[:, :], 1.0, cv("b" + u[0], u[1]))\
                        .then_inc(part_hi, 1)

            def values_out(i):
                for t in range(NT):
                    u = ("v", t)
                    yield FR_AT[u] + 0.9
                    if t == 0:
                        act.wait_ge(o_full, at(i, G * NT, 0))
                    fr_written(act, i, u)
                    copy(v32[:, t, :, 0:D], fr_bank(i, u)[:, 0:DM].rearrange("p (h d) -> p h d", d=D))\
                        .then_inc(fr_sem(i, u), 1)

            def exps(i, g):
                for n in range(16):
                    t, h = n // 4, n % 4
                    u = ("st", g, n)
                    yield FR_AT[u] + 0.3
                    if h == 0:
                        act.wait_ge(o_full, at(i, G * NT, max(g * NT + t - 1, 0)))
                    fr_written(act, i, u)
                    act.activation(pt[:, t % 2, h, :], fr_bank(i, u)[:, :], ACT.Exp, scale=D ** -0.5)\
                       .then_inc(fr_sem(i, u), 1)

            def max_out(i, g):
                u = ("ct", g)
                yield at_ct(g) + 0.2
                fr_written(act, i, u)
                act.wait_ge(c_loaded, at(i, 16 * G, 16 * g))
                copy(cT[:, :], fr_bank(i, u)[0:4 * NT, 0:P]).then_inc(fr_sem(i, u), 1)

            def o_out(i, g):
                yield at_pv(g, NT - 1) + 0.9
                act.wait_ge(o_full, at(i, G * NT, NT * (g + 1)))
                if g > 0:
                    fr_written(act, i, ("ot", g - 1))
                copy(osb[:, :], ob[:, :]).then_inc(o_emptied, 1)

            def tail_out(i, t):
                u = ("oT", t)
                yield FR_AT[u] + 0.4
                fr_written(act, i, u)
                for k in range(KT):
                    ins = copy(oT[:, k, :], fr_bank(i, u)[:, k * P:(k + 1) * P], 1.0, cv("bv", k))
                ins.then_inc(fr_sem(i, u), 1)

            def z_norm(i, t):
                yield at_tail(t) + 4.3
                act.wait_ge(zr_ready, at(i, NT, t + 1))
                act.wait_ge(rows_stored[t % 2], at(i, 8 * NT, 16 * (t // 2)))
                copy(row[:, t % 2, 0:DM], z[:, t % 2, :], zr[:, t % 2, 0:1], zr[:, t % 2, 1:2]).then_inc(zn_ready, 1)
                u = ("zT", t)
                yield FR_AT[u] + 0.4
                fr_written(act, i, u)
                for k in range(KT):
                    ins = copy(znT[:, k, :], fr_bank(i, u)[:, k * P:(k + 1) * P], cv("ln2_g", k), cv("ln2_b", k))
                ins.then_inc(fr_sem(i, u), 1)

            def body(i):
                return ([values_out(i)] + [part(i, g) for g in range(G) for part in (exps, max_out, o_out)]
                        + [part(i, t) for t in range(NT) for part in (tail_out, z_norm)])

            def head(i, last=None):
                return [heads_out(i)]

            iterations(act, body, head, x_early, x_late)

        @block.vector
        def _(dve):
            steps = {(part, zero): 0 for part in ("xe", "xl", "f") for zero in (False, True)}

            def step(part, i, ins):
                signal, per = {"f": (vf_step, VF), "xe": (vxe_step, VX_EARLY), "xl": (vxl_step, VX_LATE)}[part]
                key = (part, first(i))
                steps[key] += 1
                ins.then_inc(signal, 1)
                dve.wait_ge(signal, at(i, per, steps[key]))

            nc.vector.memset(zrow[:, :], 0.0)
            nc.vector.memset(kbd[:, :, :], 0.0)
            nc.vector.memset(vbd[:, :, :], 0.0)
            nc.vector.memset(lo17[:, :, 0:1], BIG)
            nc.vector.memset(nh17[:, :, 16:17], -BIG).then_inc(zeroed, 1)
            dve.wait_ge(const_loaded, 16 * NCONST)
            t0 = COLS["temp"]
            nc.vector.tensor_scalar(col[:, t0[0]:t0[0] + t0[1]], col[:, t0[0]:t0[0] + t0[1]], CK ** -0.5, None,
                                    ALU.mult).then_inc(consts_ready, 1)
            nc.vector.tensor_scalar(bias_m[:, :], mask_u[:, :], 1.0, MASKED, ALU.subtract, ALU.mult)\
              .then_inc(consts_ready, 1)
            def x_stats(i, half):
                yield (X0_STATS if first(i) else STATS)[half]
                dve.wait_ge(x_loaded[half], at(i, 16, 16))
                for t in range(2 * half, 2 * half + 2):
                    ins = nc.vector.bn_stats(xstat[:, t, :], xb[:, t, :])
                step("xe", i, ins)
                dve.wait_ge(xr_ready, at(i, NT, 0))
                dve.sem_inc(v_gate, 1)
                for t in range(2 * half, 2 * half + 2):
                    ins = nc.vector.bn_aggr(xmv[:, t, :], xstat[:, t, :])
                ins.then_inc(xmv_ready, 1)

            def split(i, t, part):
                yield (X0_SPLIT if first(i) else SPLIT)[t]
                dve.wait_ge(s_ready, at(i, NT, t + 1))
                a, b = s[:, t % 2, :, 0:PAIRS], s[:, t % 2, :, PAIRS:CK]
                dve.wait_ge(neg_done, at(i, NT, t))
                nc.vector.tensor_tensor(hi[:, :, :], a, b, ALU.max).then_inc(split_done, 1)
                step(part, i, nc.vector.tensor_tensor(lo[:, t % 2, :, :], a, b, ALU.min))
                nc.vector.tensor_reduce(mx[:, t % 2, :], hi[:, :, :], AX.X, ALU.max).then_inc(mx_ready, 1)

            def threshold(i, t, part):
                lv, nv = lo[:, t % 2, :, :], nhi[:, :, :]
                start, apart = (X0_PIECE if first(i) else PIECE)[t]
                for r in range(3):
                    for q in range(4):
                        yield start + apart * (4 * r + q)
                        if r == 0 and q == 0:
                            dve.wait_ge(neg_done, at(i, NT, t + 1))
                            dve.sem_inc(v_gate, 1)
                        for h in range(4 * q, 4 * q + 4):
                            if r == 0:
                                nc.vector.max(lo17[:, h, 1:9], lv[:, h, :])
                                ins = nc.vector.max(nh17[:, h, 0:8], nv[:, h, :])
                            elif r == 1:
                                nc.vector.match_replace(lv[:, h, :], lo17[:, h, 1:9], lv[:, h, :], -BIG)
                                ins = nc.vector.match_replace(nv[:, h, :], nh17[:, h, 0:8], nv[:, h, :], -BIG)
                            else:
                                nc.vector.max(lo17[:, h, 9:17], lv[:, h, :])
                                ins = nc.vector.max(nh17[:, h, 8:16], nv[:, h, :])
                    step(part, i, ins)
                    dve.sem_inc(v_gate, 1)

            def mask(i, t, part):
                yield (X0_MASK if first(i) else MASK)[t]
                step(part, i, nc.vector.scalar_tensor_tensor(merged[:, :, :], nh17[:, :, :], -1.0, lo17[:, :, :],
                                                                 ALU.mult, ALU.min))
                step(part, i, nc.vector.tensor_reduce(thr[:, :], merged[:, :, :], AX.X, ALU.max))
                nc.vector.tensor_tensor(m[:, :, :], s[:, t % 2, :, :], thr[:, :].unsqueeze(2).to_broadcast((P, H, CK)),
                                        ALU.is_ge).then_inc(mask_done, 1)

            def denominators(i, t, part):
                yield (X0_DENOM if first(i) else DENOM)[t]
                dve.wait_ge(e_ready, at(i, NT, t + 1))
                nc.vector.tensor_reduce(sums[:, 1, :], e[:, :, :], AX.X, ALU.add)
                dve.wait_ge(em_ready, at(i, NT, t + 1))
                step(part, i, nc.vector.tensor_reduce(sums[:, 0, :], m[:, :, :], AX.X, ALU.add))
                step(part, i, nc.vector.scalar_tensor_tensor(den[:, :], sums[:, 1, :], 1e-8, sums[:, 0, :],
                                                             ALU.mult, ALU.add))
                nc.vector.reciprocal(rden[:, t % 2, :], den[:, :]).then_inc(rden_ready, 1)

            def stats(part, i, src, st, mv):
                step(part, i, nc.vector.bn_stats(st, src))
                dve.sem_inc(v_gate, 1)
                return nc.vector.bn_aggr(mv, st)

            def residual(i, t, part):
                yield (X0_RESID if first(i) else RESID)[t]
                xt_written(dve, i, ("av", t))
                dve.wait_ge(xy_stored[t % 2], at(i, 32, 16 * (t // 2)))
                if not first(i) or t > 0:
                    dve.wait_ge(yn_ready, at(i, NT, t - 1))
                nc.vector.tensor_tensor(xy[:, t % 2, 0:DM], xt[:, 0:DM], xb[:, t, :], ALU.add).then_inc(xt_emptied, 1)
                xt_read(dve, i, ("av", t))
                dve.wait_ge(yr_ready, at(i, NT, t))
                stats(part, i, xy[:, t % 2, 0:DM], ystat[:, :], ymv[:, :]).then_inc(ymv_ready, 1)

            def x_early(b):
                steps["xe", False] = 0
                return [x_stats(b, 0), x_stats(b, 1), split(b, 0, "xe"), threshold(b, 0, "xe"), mask(b, 0, "xe"),
                        denominators(b, 0, "xe"), split(b, 1, "xe"), threshold(b, 1, "xe"), residual(b, 0, "xe")]

            def x_late(b, last=None):
                steps["xl", False] = 0
                return ([mask(b, 1, "xl"), denominators(b, 1, "xl"), residual(b, 1, "xl")]
                        + [part(b, t, "xl") for t in (2, 3) for part in (split, threshold, mask, denominators, residual)])

            def low_parts(i):
                for n, u in enumerate((("q", 0), ("k", 0), ("q", 1), ("k", 1))):
                    yield FR_AT[u] + 2.2
                    dve.wait_ge(part_hi, at(i, 4, n + 1))
                    nc.vector.scalar_tensor_tensor(parts[:, n % 2, 1, :], fr_bank(i, u)[:, :], cv("b" + u[0], u[1]),
                                                   parts[:, n % 2, 0, :].bitcast(F32), ALU.add, ALU.subtract)\
                      .then_inc(fr_sem(i, u), 1)

            def maxima(i, g):
                for n in range(16):
                    t, h = n // 4, n % 4
                    u = ("s", g, n)
                    yield FR_AT[u] + 0.6
                    fr_written(dve, i, u)
                    nc.vector.tensor_reduce(nmax[:, g % 2, 4 * h + t:4 * h + t + 1], fr_bank(i, u)[:, :], AX.X, ALU.max,
                                            negate=True).then_inc(fr_sem(i, u), 1)

            def normalise(i, g):
                u = ("ot", g)
                yield FR_AT[u] + 0.6
                fr_written(dve, i, u)
                o = fr_bank(i, u)[:, :].rearrange("p (t h c) -> p t h c", t=NT, c=VC)
                step("f", i, nc.vector.reciprocal(rz[:, :, :], o[:, :, :, D]))
                nc.vector.tensor_tensor(on[:, :, 4 * D * g:4 * D * (g + 1)].rearrange("p t (h d) -> p t h d", d=D),
                                        o[:, :, :, 0:D], rz[:, :, :].unsqueeze(3).to_broadcast((P, NT, 4, D)),
                                        ALU.mult).then_inc(fr_sem(i, u), 1)

            def z_rows(i, t):
                u = ("wo", t)
                yield FR_AT[u] + 1.0
                fr_written(dve, i, u)
                dve.wait_ge(xyf_loaded[t % 2], at(i, 32, 16 * (t // 2) + 16))
                if t > 1:
                    dve.wait_ge(res_ready, at(i, NT, t - 1))
                nc.vector.tensor_tensor(z[:, t % 2, :], fr_bank(i, u)[:, 0:DM], xyf[:, t % 2, DM:2 * DM], ALU.add)\
                  .then_inc(fr_sem(i, u), 1)
                fr_read(dve, i, u)
                dve.wait_ge(zr_ready, at(i, NT, t))
                stats("f", i, z[:, t % 2, :], zstat[:, :], zmv[:, :]).then_inc(zmv_ready, 1)

            def gate(i, t):
                u = ("gate", t)
                yield FR_AT[u] + 0.6
                fr_written(dve, i, u)
                nc.vector.tensor_tensor(logits[:, bass.ds(i * (NT * E) + t * E, E)], fr_bank(i, u)[:, 0:E], gb_b[:, :],
                                        ALU.add).then_inc(fr_sem(i, u), 1)

            def body(i):
                steps["f", False] = 0
                steps["f", True] = 0
                return ([maxima(i, g) for g in range(1, G)] + [normalise(i, g) for g in range(G)]
                        + [part(i, t) for t in range(NT) for part in (z_rows, gate)])

            def head(i, last=None):
                return low_parts(i), maxima(i, 0)

            iterations(dve, body, head, x_early, x_late)
            assert [steps[part, False] for part in ("xe", "xl", "f")] == [VX_EARLY, VX_LATE, VF], steps

        @block.gpsimd
        def _(pool):
            gp = nc.gpsimd
            gp.memset(qs[:, :, :].bitcast(F32), 0.0)
            gp.memset(ks[:, :, :].bitcast(F32), 0.0).then_inc(p_set, 1)
            gp.memset(mhalf[:, :], -0.5)
            gp.memset(v32[:, :, :, :], 0.0).then_inc(p_set, 1)
            pool.wait_ge(p_set, 2)
            gp.memset(ks[4 * D:4 * D + 1, :, :].bitcast(F32), 1.0).then_inc(p_set, 1)
            pool.wait_ge(p_set, 3)
            gp.memset(v32[:, :, :, D:D + 1], 1.0).then_inc(zeroed, 1)
            pool.wait_ge(consts_ready, 2)
            pool.wait_ge(zeroed, 2)

            steps = {(part, zero): 0 for part in ("xe", "xl", "f") for zero in (False, True)}

            def hold():
                pool.sem_inc(p_gate, 1)

            def step(part, i, ins):
                signal, per = {"f": (pf_step, PF), "xe": (pxe_step, PX_EARLY), "xl": (pxl_step, PX_LATE)}[part]
                key = (part, first(i))
                steps[key] += 1
                ins.then_inc(signal, 1)
                pool.wait_ge(signal, at(i, per, steps[key]))
                hold()

            def inv_std(part, i, o, var, tmp):
                step(part, i, gp.tensor_scalar(tmp, var, EPS, None, ALU.add))
                return gp.tensor_tensor(o, tmp, mhalf[:, 0:tmp.shape[1]], ALU.pow)

            def x_factors(i, half):
                yield (X0_STATS if first(i) else STATS)[half] + 0.8
                r = slice(2 * half, 2 * half + 2)
                pool.wait_ge(xmv_ready, at(i, 2, half + 1))
                hold()
                step("xe", i, inv_std("xe", i, xr[:, r, 0], xmv[:, r, 1], xv[:, r]))
                step("xe", i, gp.tensor_tensor(xv[:, r], xmv[:, r, 0], xr[:, r, 0], ALU.mult))
                gp.tensor_scalar(xr[:, r, 1], xv[:, r], -1.0, None, ALU.mult).then_inc(xr_ready, 2)

            def add_bias(i, t):
                yield (X0_SCORE if first(i) else SCORE)[t] + 4.2
                xs_read(pool, i, ("sc", t, 1))
                if not first(i) or t > 1:
                    pool.wait_ge(mask_done, at(i, NT, t - 1))
                hold()
                gp.tensor_tensor(s[:, t % 2, :, :], sraw[:, :].rearrange("p (h c) -> p h c", c=CK),
                                 bias_m[:, bass.ds(i * CK, CK)].unsqueeze(1).to_broadcast((P, H, CK)), ALU.add)\
                  .then_inc(s_ready, 1)

            def shift(i, t):
                yield (X0_SHIFT if first(i) else SHIFT)[t]
                pool.wait_ge(mx_ready, at(i, NT, t + 1))
                pool.wait_ge(s_ready, at(i, NT, t + 1))
                pool.wait_ge(rden_ready, at(i, NT, t))
                gp.tensor_tensor(e[:, :, :], s[:, t % 2, :, :],
                                 mx[:, t % 2, :].unsqueeze(2).to_broadcast((P, H, CK)), ALU.subtract)\
                  .then_inc(d_ready, 1)

            def keep_top(i, t):
                yield (X0_MASK if first(i) else MASK)[t] + 0.9
                pool.wait_ge(mask_done, at(i, NT, t + 1))
                pool.wait_ge(e_ready, at(i, NT, t + 1))
                gp.tensor_tensor(m[:, :, :], m[:, :, :], e[:, :, :], ALU.mult).then_inc(em_ready, 1)

            def weights(i, t):
                yield (X0_DENOM if first(i) else DENOM)[t] + 2.8
                pool.wait_ge(rden_ready, at(i, NT, t + 1))
                gp.tensor_tensor(m[:, :, :], m[:, :, :], rden[:, t % 2, :].unsqueeze(2).to_broadcast((P, H, CK)),
                                 ALU.mult).then_inc(p_ready, 1)

            def y_factors(i, t):
                yield (X0_YFAC if first(i) else YFAC)[t]
                pool.wait_ge(ymv_ready, at(i, NT, t + 1))
                if not first(i) or t > 1:
                    pool.wait_ge(yn_ready, at(i, NT, t - 1))
                hold()
                r = yr[:, t % 2, :]
                step("xl", i, inv_std("xl", i, r[:, 0:1], ymv[:, 1:2], yv[:, 0:1]))
                step("xl", i, gp.tensor_scalar(yv[:, 1:2], ymv[:, 1:2], r[:, 0:1], r[:, 0:1], ALU.mult, ALU.mult))
                step("xl", i, inv_std("xl", i, yv[:, 2:3], yv[:, 1:2], yv[:, 3:4]))
                step("xl", i, gp.tensor_tensor(r[:, 1:2], r[:, 0:1], yv[:, 2:3], ALU.mult))
                gp.tensor_scalar(r[:, 2:4], r[:, 0:2], ymv[:, 0:1], -1.0, ALU.mult, ALU.mult).then_inc(yr_ready, 1)

            def y_bias(i, t):
                yield (X0_YBIAS if first(i) else YBIAS)[t]
                pool.wait_ge(y_ready, at(i, NT, t + 1))
                yb = xy[:, t % 2, DM:2 * DM]
                gp.tensor_tensor(yb, yb, bo_b[:, :], ALU.add).then_inc(yb_ready, 1)

            def x_early(b):
                steps["xe", False] = 0
                return [x_factors(b, 0), x_factors(b, 1), add_bias(b, 0), add_bias(b, 1), add_bias(b, 2), shift(b, 0), shift(b, 1),
                        keep_top(b, 0), weights(b, 0)]

            def x_late(b, last=None):
                steps["xl", False] = 0
                return ([shift(b, 2), shift(b, 3), add_bias(b, 3)]
                        + [part(b, t) for t in (1, 2, 3) for part in (keep_top, weights)]
                        + [part(b, t) for t in range(NT) for part in (y_factors, y_bias)])

            def z_factors(i, t):
                yield FR_AT["wo", t] + 1.7
                pool.wait_ge(zmv_ready, at(i, NT, t + 1))
                if t > 1:
                    pool.wait_ge(zn_ready, at(i, NT, t - 1))
                hold()
                step("f", i, inv_std("f", i, zr[:, t % 2, 0:1], zmv[:, 1:2], zv[:, 0:1]))
                gp.tensor_scalar(zr[:, t % 2, 1:2], zmv[:, 0:1], zr[:, t % 2, 0:1], -1.0, ALU.mult, ALU.mult)\
                  .then_inc(zr_ready, 1)

            def residual_row(i, t):
                yield FR_AT["wo", t] + 2.8
                fr_read(pool, i, ("wo", t))
                pool.wait_ge(rows_stored[t % 2], at(i, 8 * NT, 16 * (t // 2)))
                pool.wait_ge(xyf_loaded[t % 2], at(i, 32, 16 * (t // 2) + 16))
                gp.tensor_tensor(row[:, t % 2, DM:2 * DM], xyf[:, t % 2, 0:DM], z[:, t % 2, :], ALU.add)\
                  .then_inc(res_ready, 1)

            def body(i):
                steps["f", False] = 0
                steps["f", True] = 0
                return [part(i, t) for t in range(NT) for part in (z_factors, residual_row)]

            def head(i, last=None):
                return []

            iterations(pool, body, head, x_early, x_late)
            assert [steps[part, False] for part in ("xe", "xl", "f")] == [PX_EARLY, PX_LATE, PF], steps

        attn_space.close()
        block_ctx.close()

        dcon = sb("dcon", [P, NDCON])
        oh = sb("oh", [P, TILES, E])
        ow = sb("ow", [P, TILES, E])
        best = sb("best", [P, TILES])
        tot = sb("tot", [P, TILES, E])
        pre = sb("pre", [P, 2, TILES, E])
        need = sb("need", [P, E, TILES])
        cnt = sb("cnt", [P, E])
        cum = sb("cum", [P, 3, E])
        base = sb("base", [P, E])
        slot = sb("slot", [P, TILES])
        passed = sb("passed", [P, TILES, SEGS + 1])
        at_tile = sb("at_tile", [P, TILES, SEGS], F32R)
        at_row = sb("at_row", [P, TILES, P], F32R)
        past = sb("past", [P, ETILES, E])
        keep = sb("keep", [P, ETILES])
        rec = sb("rec", [P, ETILES, 3])

        gix = sb("gix", [P, 2, 3], U32)
        sid = sb("sid", [P, 2, 1], U32)
        rows = sb("rows", [P, 2, 2 * DM])
        znT2 = sb("znT2", [P, 2, KT, P])
        w1s = sb("w1s", [P, 2, W1COLS])
        w2s = sb("w2s", [P, 2, FT, DM])
        b2s = sb("b2s", [P, 2, DM])
        mid = sb("mid", [P, 2, FT, P])
        resb = sb("resb", [P, 2, DM])
        ot = sb("ot", [P, 2, DM])

        def dc(name):
            a, n = DCON[name]
            return dcon[:, a:a + n]

        def freed(eng, signal, j, per):
            if not isinstance(j, int) or j > 0:
                eng.wait_ge(signal, reads(j, per, 0))

        def tiles(eng, step):
            full = (ETILES - 2) // 2
            for q in range(2):
                step(0, q, True)
            with eng.Fori(1, full) as j:
                step(j, 0, True)
                step(j, 1, True)
            for n in range(2 * full, ETILES):
                step(n // 2, n % 2, n + 2 < ETILES)

        block = ctx.enter_context(nc.Block())

        @block.sync
        def _(sp):
            sp.dma_start(dcon[:, :], dcon_in).then_inc(dcon_loaded, 16)

        @block.vector
        def _(dve):
            count = [0]

            def settle(ins):
                count[0] += 1
                ins.then_inc(d_step, 1)
                dve.wait_ge(d_step, count[0])

            lg = logits[:, :].rearrange("p (t e) -> p t e", e=E)
            v = nc.vector
            dve.wait_ge(dcon_loaded, 16)
            settle(v.tensor_reduce(best[:, :], lg, AX.X, ALU.max))
            settle(v.tensor_tensor(oh[:, :, :], lg, best[:, :].unsqueeze(2).to_broadcast((P, TILES, E)), ALU.is_ge))
            settle(v.tensor_tensor(ow[:, :, :], oh[:, :, :], dc("order").unsqueeze(1).to_broadcast((P, TILES, E)),
                                   ALU.mult))
            settle(v.tensor_reduce(best[:, :], ow[:, :, :], AX.X, ALU.max))
            v.tensor_tensor(oh[:, :, :], ow[:, :, :], best[:, :].unsqueeze(2).to_broadcast((P, TILES, E)),
                            ALU.is_equal).then_inc(oh_ready, 1)
            dve.wait_ge(count_full, 1)
            settle(v.tensor_copy(tot[:, :, :].rearrange("p t e -> p (t e)"), ob[:, 0:TILES * E]))
            settle(v.tensor_copy(pre[:, 0, :, :], tot[:, :, :]))
            a, step = 0, 1
            while step < TILES:
                v.tensor_copy(pre[:, 1 - a, 0:step, :], pre[:, a, 0:step, :])
                settle(v.tensor_tensor(pre[:, 1 - a, step:, :], pre[:, a, step:, :], pre[:, a, 0:TILES - step, :],
                                       ALU.add))
                a, step = 1 - a, 2 * step
            settle(v.tensor_copy(cnt[:, :], pre[:, a, TILES - 1, :]))
            settle(v.tensor_tensor(need[:, :, :], cnt[:, :].unsqueeze(2).to_broadcast((P, E, TILES)),
                                   dc("steps").unsqueeze(1).to_broadcast((P, E, TILES)), ALU.is_gt))
            settle(v.tensor_reduce(cum[:, 0, :], need[:, :, :], AX.X, ALU.add))
            settle(v.tensor_copy(cum[:, 1, :], cum[:, 0, :]))
            c, step = 1, 1
            while step < E:
                v.tensor_copy(cum[:, 3 - c, 0:step], cum[:, c, 0:step])
                settle(v.tensor_tensor(cum[:, 3 - c, step:], cum[:, c, step:], cum[:, c, 0:E - step], ALU.add))
                c, step = 3 - c, 2 * step
            ex, wix = rec[:, :, 2], rec[:, :, 1]
            settle(v.tensor_tensor(past[:, :, :], dc("tile").unsqueeze(2).to_broadcast((P, ETILES, E)),
                                   cum[:, c, :].unsqueeze(1).to_broadcast((P, ETILES, E)), ALU.is_ge))
            settle(v.tensor_reduce(ex, past[:, :, :], AX.X, ALU.add))
            v.memset(keep[:, 0:2], 0.0)
            settle(v.tensor_scalar(ex, ex, float(E - 1), None, ALU.min))
            settle(v.tensor_tensor(keep[:, 2:], rec[:, 2:, 2], rec[:, 0:ETILES - 2, 2], ALU.is_equal))
            settle(v.scalar_tensor_tensor(wix, keep[:, :], float(E), ex, ALU.mult, ALU.add))
            settle(v.tensor_scalar(wix, wix, float(P), dc("part"), ALU.mult, ALU.add))
            for q in range(2):
                v.tensor_scalar(gix[:, q, 1:3], rec[:, q, 1:3], 0.0, None, ALU.add).then_inc(gix_ready[q], 1)

            settle(v.tensor_tensor(base[:, :], cum[:, c, :], cum[:, 0, :], ALU.subtract))
            settle(v.tensor_scalar(base[:, :], base[:, :], float(P), None, ALU.mult))
            settle(v.tensor_tensor(ow[:, :, :], pre[:, a, :, :], tot[:, :, :], ALU.subtract))
            settle(v.tensor_tensor(tot[:, :, :], ow[:, :, :], base[:, :].unsqueeze(1).to_broadcast((P, TILES, E)),
                                   ALU.add))
            settle(v.tensor_tensor(ow[:, :, :].rearrange("p t e -> p (t e)"), xt[:, 0:TILES * E],
                                   tot[:, :, :].rearrange("p t e -> p (t e)"), ALU.add))
            settle(v.tensor_tensor(tot[:, :, :], ow[:, :, :], oh[:, :, :], ALU.mult))
            settle(v.tensor_reduce(slot[:, :], tot[:, :, :], AX.X, ALU.add))
            settle(v.tensor_tensor(passed[:, :, :], slot[:, :].unsqueeze(2).to_broadcast((P, TILES, SEGS + 1)),
                                   dc("starts").unsqueeze(1).to_broadcast((P, TILES, SEGS + 1)), ALU.is_ge))
            settle(v.tensor_reduce(best[:, :], passed[:, :, :], AX.X, ALU.add))
            settle(v.scalar_tensor_tensor(best[:, :], best[:, :], -float(P), slot[:, :], ALU.mult, ALU.add))
            settle(v.tensor_scalar(best[:, :], best[:, :], float(P), None, ALU.add))
            settle(v.tensor_tensor(at_tile[:, :, :], passed[:, :, 0:SEGS], passed[:, :, 1:], ALU.subtract))
            settle(v.tensor_tensor(at_tile[:, :, :], at_tile[:, :, :],
                                   dc("token").unsqueeze(2).to_broadcast((P, TILES, SEGS)), ALU.mult))
            for t0 in range(0, TILES, 8):
                v.tensor_tensor(at_row[:, t0:t0 + 8, :], best[:, t0:t0 + 8].unsqueeze(2).to_broadcast((P, 8, P)),
                                dc("row").unsqueeze(1).to_broadcast((P, 8, P)), ALU.is_equal).then_inc(rows_ready, 1)
            dve.wait_ge(tokens_full, 1)
            settle(v.tensor_scalar(rec[:, :, 0], EO[1][:, 0:ETILES], float(TOK), None, ALU.add))
            for q in range(2):
                v.tensor_scalar(gix[:, q, 0:1], rec[:, q, 0:1], 0.0, None, ALU.add).then_inc(gix_ready[q], 1)

            def tile(j, q, more):
                dve.wait_ge(rows_in[q], reads(j, 16, 16))
                dve.wait_ge(b2_in[q], reads(j, 16, 16))
                freed(dve, ot_ready[q], j, 2)
                v.tensor_tensor(resb[:, q, :], rows[:, q, DM:2 * DM], b2s[:, q, :], ALU.add)\
                 .then_inc(resb_ready[q], 1)
                dve.wait_ge(l1_full[q], reads(j, 2, 2))
                for f in range(FT // 2, FT):
                    o = EH[2 * q + 1]
                    c0 = (f - FT // 2) * P
                    ins = v.tensor_scalar(mid[:, q, f, :], o[:, c0:c0 + P], w1s[:, q, KT * FF + f:KT * FF + f + 1],
                                          0.0, ALU.add, ALU.max)
                ins.then_inc(mid_dve[q], 1)
                if more:
                    dve.wait_ge(w1_in[q], reads(j, 16, 16))
                    dve.wait_ge(w2_in[q], reads(j, 16, 16))
                    v.tensor_scalar(gix[:, q, :], rec[:, bass.ds(2 * j + q + 2, 1), :].rearrange("p a c -> p (a c)"),
                                    0.0, None, ALU.add).then_inc(gix_ready[q], 2)
                dve.wait_ge(l2_full[q], reads(j, 1, 1))
                dve.wait_ge(resb_ready[q], reads(j, 1, 1))
                freed(dve, scattered[q], j, 16)
                v.tensor_scalar(sid[:, q, :], rec[:, bass.ds(2 * j + q, 1), 0], 0.0, None, ALU.add)\
                 .then_inc(ot_ready[q], 1)
                v.tensor_tensor(ot[:, q, :], EO[q][:, 0:DM], resb[:, q, :], ALU.add).then_inc(ot_ready[q], 1)

            tiles(dve, tile)

        @block.tensor
        def _(pe):
            pe.wait_ge(oh_ready, 1)
            pe.matmul(xt[:, 0:TILES * E], dc("before"), oh[:, :, :].rearrange("p t e -> p (t e)"))
            pe.matmul(ob[:, 0:TILES * E], dc("ones"), oh[:, :, :].rearrange("p t e -> p (t e)"))\
              .then_inc(count_full, 1)

            def turn(j, q):
                pe.wait_ge(rows_in[q], reads(j, 16, 16))
                for k in range(KT):
                    ins = pe.transpose(ET[q][:, k * P:(k + 1) * P], rows[:, q, k * P:(k + 1) * P], ident[:, :])
                ins.then_inc(turned[q], 1)

            def tile(j, q, more, last=False):
                pe.wait_ge(turned_out[q], reads(j, 1, 1))
                pe.wait_ge(w1_in[q], reads(j, 16, 16))
                for half in range(2):
                    for f in range(FT // 2):
                        ff = half * (FT // 2) + f
                        for k in range(KT):
                            ins = pe.matmul(EH[2 * q + half][:, f * P:(f + 1) * P],
                                            w1s[:, q, k * FF + ff * P:k * FF + (ff + 1) * P], znT2[:, q, k, :],
                                            start=(k == 0), stop=(k == KT - 1))
                    ins.then_inc(l1_full[q], 1)
                if not last:
                    turn(j + q, 1 - q)
                pe.wait_ge(w2_in[q], reads(j, 16, 16))
                pe.wait_ge(mid_act[q], reads(j, 1, 1))
                freed(pe, ot_ready[q], j, 2)
                for f in range(FT):
                    if f == FT // 2:
                        pe.wait_ge(mid_dve[q], reads(j, 1, 1))
                    ins = pe.matmul(EO[q][:, 0:DM], mid[:, q, f, :], w2s[:, q, f, :], start=(f == 0), stop=(f == FT - 1))
                ins.then_inc(l2_full[q], 1)

            for t in range(TILES):
                if t % 8 == 0:
                    pe.wait_ge(rows_ready, t // 8 + 1)
                ins = pe.matmul(EO[1][:, 0:SEGS], at_row[:, t, :], at_tile[:, t, :], start=(t == 0),
                                stop=(t == TILES - 1))
            ins.then_inc(tokens_full, 1)
            turn(0, 0)
            tiles(pe, lambda j, q, more: tile(j, q, more, isinstance(j, int) and 2 * j + q == ETILES - 1))

        @block.scalar
        def _(act):
            def turned_to(j, q):
                act.wait_ge(turned[q], reads(j, 1, 1))
                for k in range(KT):
                    ins = act.activation(znT2[:, q, k, :], ET[q][:, k * P:(k + 1) * P], ACT.Identity,
                                         scale=cv("ln2_g", k), bias=cv("ln2_b", k))
                ins.then_inc(turned_out[q], 1)

            def tile(j, q, more):
                act.wait_ge(l1_full[q], reads(j, 2, 1))
                for f in range(FT // 2):
                    ins = act.activation(mid[:, q, f, :], EH[2 * q][:, f * P:(f + 1) * P], ACT.Relu,
                                         bias=w1s[:, q, KT * FF + f:KT * FF + f + 1])
                ins.then_inc(mid_act[q], 1)
                if more or not isinstance(j, int) or 2 * j + q + 1 < ETILES:
                    turned_to(j + q, 1 - q)

            turned_to(0, 0)
            tiles(act, tile)

        @block.gpsimd
        def _(pool):
            gp = nc.gpsimd

            def gather(dst, src, index, signal, bound=None):
                pool.sem_inc(p_gate, 1)
                gp.indirect_dma_start(dst, None, src, bass.IndirectOffsetOnAxis(index, 0), bounds_check=bound,
                                      oob_is_err=False).then_inc(signal, 16)

            def fetch_rows(j, q):
                pool.wait_ge(gix_ready[q], reads(j, 2, 2))
                gather(rows[:, q, :], rows_d, gix[:, q, 0:1], rows_in[q], TOK)

            def fetch_w1(j, q):
                gather(w1s[:, q, :], w1b, gix[:, q, 1:2], w1_in[q], E * P - 1)

            def fetch_w2(j, q):
                gather(w2s[:, q, :, :].rearrange("p f d -> p (f d)"), w2t, gix[:, q, 1:2], w2_in[q], E * P - 1)
                gather(b2s[:, q, :], b2, gix[:, q, 2:3], b2_in[q], E - 1)

            for q in range(2):
                pool.wait_ge(gix_ready[q], 1)
                fetch_w1(0, q)
                fetch_w2(0, q)
            for q in range(2):
                fetch_rows(0, q)

            def tile(j, q, more):
                if more:
                    pool.wait_ge(turned[q], reads(j, 1, 1))
                    pool.wait_ge(resb_ready[q], reads(j, 1, 1))
                    fetch_rows(j + 1, q)
                    pool.wait_ge(l1_full[q], reads(j, 2, 2))
                    pool.wait_ge(mid_act[q], reads(j, 1, 1))
                    pool.wait_ge(mid_dve[q], reads(j, 1, 1))
                    fetch_w1(j + 1, q)
                    pool.wait_ge(l2_full[q], reads(j, 1, 1))
                    fetch_w2(j + 1, q)
                pool.wait_ge(ot_ready[q], reads(j, 2, 2))
                freed(pool, scattered[1 - q], j + q, 16)
                pool.sem_inc(p_gate, 1)
                gp.indirect_dma_start(out, bass.IndirectOffsetOnAxis(sid[:, q, 0:1], 0), ot[:, q, :], None,
                                      bounds_check=TOK - 1, oob_is_err=False).then_inc(scattered[q], 16)

            tiles(pool, tile)
            for q in range(2):
                pool.wait_ge(scattered[q], 16 * ((ETILES + 1 - q) // 2))
    return nc


def kernel(x, ctx_1024, mask_BxS2_bf1, L0_xattn_Wq, L0_xattn_Wk, L0_xattn_Wv, L0_xattn_Wo, L0_xattn_inv_temp,
           L0_ffn_ln1_g, L0_ffn_ln1_b, L0_ffn_ln2_g, L0_ffn_ln2_b, L0_ffn_wq, L0_ffn_bq, L0_ffn_wk, L0_ffn_bk,
           L0_ffn_wv, L0_ffn_bv, L0_ffn_wo, L0_ffn_bo, L0_ffn_gate_w, L0_ffn_gate_b, L0_ffn_w1, L0_ffn_b1,
           L0_ffn_w2, L0_ffn_b2):
    import numpy as np
    import concourse.bacc as bacc
    from concourse.bass_utils import run_bass_kernel_spmd

    def col(v):
        return v.reshape(-1, P).T

    temp = np.repeat(np.asarray(L0_xattn_inv_temp), CK)
    w1 = np.asarray(L0_ffn_w1).reshape(E, KT, P, FF).transpose(0, 2, 1, 3).reshape(E * P, KT * FF)
    b1 = np.asarray(L0_ffn_b1).reshape(E, FT, P).transpose(0, 2, 1).reshape(E * P, FT)
    w2 = np.asarray(L0_ffn_w2).reshape(E, FT, P, DM).transpose(0, 2, 1, 3).reshape(E * P, FT * DM)
    dcon = np.zeros((P, NDCON), np.float32)
    for name, value in (("before", np.triu(np.ones((P, P)), 1)), ("ones", 1.0), ("order", E - np.arange(E)),
                        ("steps", P * np.arange(TILES)), ("starts", P * np.arange(SEGS + 1)),
                        ("tile", np.arange(ETILES)), ("row", np.arange(P)),
                        ("part", np.arange(P)[:, None]),
                        ("token", P * np.arange(TILES)[None, :] + np.arange(P)[:, None] - TOK)):
        a, n = DCON[name]
        dcon[:, a:a + n] = value
    arrays = {
        "x": x,
        "ctxT": np.asarray(ctx_1024).reshape(B * CK, DM).T,
        "maskb": np.asarray(mask_BxS2_bf1).reshape(1, B * CK).view(np.uint8),
        "wqT": np.asarray(L0_xattn_Wq).T, "wk": L0_xattn_Wk, "wv": L0_xattn_Wv, "wo": L0_xattn_Wo,
        "cols": np.concatenate([col(np.asarray(v)) for v in (temp, L0_ffn_ln1_g, L0_ffn_ln1_b, L0_ffn_bq, L0_ffn_bk,
                                                             L0_ffn_bv, L0_ffn_ln2_g, L0_ffn_ln2_b)], axis=1),
        "fwq": L0_ffn_wq, "fwk": L0_ffn_wk, "fwv": L0_ffn_wv, "fwo": L0_ffn_wo,
        "bo": np.asarray(L0_ffn_bo).reshape(1, DM), "gate_w": L0_ffn_gate_w,
        "gate_b": np.asarray(L0_ffn_gate_b).reshape(1, E),
        "w1b": np.concatenate([w1, b1], axis=1), "w2t": w2, "b2": L0_ffn_b2,
        "ident_in": np.eye(P, dtype=np.float32), "dcon_in": dcon,
    }
    arrays = {name: np.ascontiguousarray(a) for name, a in arrays.items()}
    nc = bacc.Bacc("TRN2", target_bir_lowering=False, num_devices=1)
    args = {name: nc.dram_tensor(name, a.shape, mybir.dt.from_np(a.dtype), kind="ExternalInput").ap()
            for name, a in arrays.items()}
    out = nc.dram_tensor("out", (TOK, DM), F32, kind="ExternalOutput").ap()
    program(nc, **args, out=out)
    result = run_bass_kernel_spmd(nc, [arrays], core_ids=[0])
    return result.results[0]["out"].reshape(B, S, DM)
```
